# Optimizing a Trainium2 kernel written in Bass

```python
import numpy as np
import jax
import jax.numpy as jnp

def _softmax(x, axis=-1):
    return jax.nn.softmax(x, axis=axis)

def _gelu(x):
    return jax.nn.gelu(x, approximate=True)

def _silu(x):
    return jax.nn.silu(x)

def _sigmoid(x):
    return jax.nn.sigmoid(x)

def _layernorm(x, axis=-1, eps=1e-05):
    m = jnp.mean(x, axis=axis, keepdims=True)
    v = jnp.var(x, axis=axis, keepdims=True)
    return (x - m) / jnp.sqrt(v + eps)

def _scatter_add(tgt, idx, src, axis=0):
    return tgt.at[idx].add(src)

def _segment_sum(src, seg, n):
    return jax.ops.segment_sum(src, seg, n)
kernel_name = 'mk_gnn_preln_d2_gnn_r32_6b7f76'

def setup_inputs(seed: int=0):
    np.random.seed(seed)
    _w = jnp.asarray

    def _rec_inputs():
        import jax
        import jax.numpy as jnp
        _gk = jax.random.key(seed)
        x = -0.000202 + 1 * jax.random.normal(jax.random.fold_in(_gk, 1), (50000, 128), jnp.float32)
        src = jax.random.randint(jax.random.fold_in(_gk, 2), (50000,), 0, 50000, jnp.int32)
        dst = jax.random.randint(jax.random.fold_in(_gk, 3), (50000,), 0, 50000, jnp.int32)
        _o = jnp.argsort(dst, stable=True)
        src = src[_o]
        dst = dst[_o]
        edge_weight = jax.random.uniform(jax.random.fold_in(_gk, 13), (50000,), jnp.float32, 0.0, 5)
        return (x, src, dst, edge_weight)
    x, src, dst, edge_weight = _rec_inputs()

    def _L0_gnn_setup():
        import jax, jax.numpy as jnp
        import numpy as np
        N_NODES = 50000
        N_EDGES = 50000
        CHANNELS = 128
        EXPANSION = 50
        CUTOFF = 5.0
        LOG2 = 0.6931471805599453

        def shifted_softplus(x):
            return jax.nn.softplus(x) - LOG2

        def gaussian_smearing(r, cutoff=CUTOFF, n=EXPANSION):
            centers = jnp.linspace(0.0, cutoff, n, dtype=r.dtype)
            delta = centers[1] - centers[0]
            coef = 1.0 / (2.0 * delta * delta)
            d = r[:, None] - centers[None, :]
            return jnp.exp(-coef * d * d)
        key = jax.random.key(seed)
        ks = jax.random.split(key, 12)
        C, F = (CHANNELS, EXPANSION)

        def lin(k, fan_in, shape):
            bound = 1.0 / np.sqrt(fan_in)
            return jax.random.uniform(k, shape, jnp.float32, -bound, bound)
        return {'features': jax.random.normal(ks[0], (N_NODES, C), jnp.float32), 'edge_distances': jax.random.uniform(ks[1], (N_EDGES,), jnp.float32) * CUTOFF, 'W_lin': lin(ks[2], C, (C, C)), 'Wf1': lin(ks[3], F, (F, C)), 'bf1': lin(ks[4], F, (C,)), 'Wf2': lin(ks[5], C, (C, C)), 'bf2': lin(ks[6], C, (C,)), 'Wm1': lin(ks[7], C, (C, C)), 'bm1': lin(ks[8], C, (C,)), 'Wm2': lin(ks[9], C, (C, C)), 'bm2': lin(ks[10], C, (C,)), 'senders': jax.random.randint(ks[11], (N_EDGES,), 0, N_NODES, jnp.int32), 'receivers': jax.random.randint(jax.random.fold_in(key, 99), (N_EDGES,), 0, N_NODES, jnp.int32)}
    _L0_gnn_all = _L0_gnn_setup()
    _L0_gnn_in = {k: v for k, v in _L0_gnn_all.items() if k in ('W_lin', 'Wf1', 'bf1', 'Wf2', 'bf2', 'Wm1', 'bm1', 'Wm2', 'bm2')}
    del _L0_gnn_all

    def _L1_gnn_setup():
        import jax, jax.numpy as jnp
        import numpy as np
        N = 10000
        E = 20000
        D_IN = 128
        D_OUT = 128
        key = jax.random.key(seed)
        k1, k2, k3, k4, k5, k6 = jax.random.split(key, 6)
        x = jax.random.normal(k1, (N, D_IN), dtype=jnp.float32)
        edge_index = jax.random.randint(k2, (2, E), 0, N, dtype=jnp.int64)
        s = 1.0 / np.sqrt(D_IN)
        W_self = jax.random.uniform(k3, (D_OUT, D_IN), jnp.float32, -s, s)
        b_self = jax.random.uniform(k4, (D_OUT,), jnp.float32, -s, s)
        W_neigh = jax.random.uniform(k5, (D_OUT, D_IN), jnp.float32, -s, s)
        b_neigh = jax.random.uniform(k6, (D_OUT,), jnp.float32, -s, s)
        return {'x': x, 'edge_index': edge_index, 'W_self': W_self, 'b_self': b_self, 'W_neigh': W_neigh, 'b_neigh': b_neigh}
    _L1_gnn_all = _L1_gnn_setup()
    _L1_gnn_in = {k: v for k, v in _L1_gnn_all.items() if k in ('W_self', 'b_self', 'W_neigh', 'b_neigh')}
    del _L1_gnn_all
    return {'x': x, 'src': src, 'dst': dst, 'edge_weight': edge_weight, 'L0_gnn_W_lin': _L0_gnn_in['W_lin'], 'L0_gnn_Wf1': _L0_gnn_in['Wf1'], 'L0_gnn_bf1': _L0_gnn_in['bf1'], 'L0_gnn_Wf2': _L0_gnn_in['Wf2'], 'L0_gnn_bf2': _L0_gnn_in['bf2'], 'L0_gnn_Wm1': _L0_gnn_in['Wm1'], 'L0_gnn_bm1': _L0_gnn_in['bm1'], 'L0_gnn_Wm2': _L0_gnn_in['Wm2'], 'L0_gnn_bm2': _L0_gnn_in['bm2'], 'L1_gnn_W_self': _L1_gnn_in['W_self'], 'L1_gnn_b_self': _L1_gnn_in['b_self'], 'L1_gnn_W_neigh': _L1_gnn_in['W_neigh'], 'L1_gnn_b_neigh': _L1_gnn_in['b_neigh']}

def reference(x, src, dst, edge_weight, L0_gnn_W_lin, L0_gnn_Wf1, L0_gnn_bf1, L0_gnn_Wf2, L0_gnn_bf2, L0_gnn_Wm1, L0_gnn_bm1, L0_gnn_Wm2, L0_gnn_bm2, L1_gnn_W_self, L1_gnn_b_self, L1_gnn_W_neigh, L1_gnn_b_neigh):
    import jax
    import jax.numpy as jnp

    def _L0_gnn_ref(features, edge_distances, W_lin, Wf1, bf1, Wf2, bf2, Wm1, bm1, Wm2, bm2, senders, receivers):
        import jax, jax.numpy as jnp
        import numpy as np
        N_NODES = 50000
        N_EDGES = 50000
        CHANNELS = 128
        EXPANSION = 50
        CUTOFF = 5.0
        LOG2 = 0.6931471805599453

        def shifted_softplus(x):
            return jax.nn.softplus(x) - LOG2

        def gaussian_smearing(r, cutoff=CUTOFF, n=EXPANSION):
            centers = jnp.linspace(0.0, cutoff, n, dtype=r.dtype)
            delta = centers[1] - centers[0]
            coef = 1.0 / (2.0 * delta * delta)
            d = r[:, None] - centers[None, :]
            return jnp.exp(-coef * d * d)
        h = features @ W_lin.T
        basis = gaussian_smearing(edge_distances)
        ef = shifted_softplus(basis @ Wf1 + bf1) @ Wf2 + bf2
        messages = h[senders] * ef
        agg = jax.ops.segment_sum(messages, receivers, num_segments=N_NODES)
        return shifted_softplus(agg @ Wm1 + bm1) @ Wm2 + bm2

    def _L1_gnn_ref(x, edge_index, W_self, b_self, W_neigh, b_neigh):
        import jax, jax.numpy as jnp
        import numpy as np
        N = 10000
        E = 20000
        D_IN = 128
        D_OUT = 128
        row, col = (edge_index[0], edge_index[1])
        n = x.shape[0]
        out = x @ W_self.T + b_self
        neigh = x[col] @ W_neigh.T + b_neigh
        agg = jax.ops.segment_sum(neigh, row, num_segments=n)
        count = jax.ops.segment_sum(jnp.ones((row.shape[0],), dtype=x.dtype), row, num_segments=n)
        count = jnp.clip(count, 1.0, None)[:, None]
        return out + agg / count
    edge_index = jnp.stack([src, dst])
    h = jnp.maximum(_layernorm(x, axis=-1), 0.0)
    x = x + _L0_gnn_ref(h, edge_weight, L0_gnn_W_lin, L0_gnn_Wf1, L0_gnn_bf1, L0_gnn_Wf2, L0_gnn_bf2, L0_gnn_Wm1, L0_gnn_bm1, L0_gnn_Wm2, L0_gnn_bm2, src, dst)
    h = jnp.maximum(_layernorm(x, axis=-1), 0.0)
    x = x + _L1_gnn_ref(h, edge_index, L1_gnn_W_self, L1_gnn_b_self, L1_gnn_W_neigh, L1_gnn_b_neigh)
    return x

_drawn_inputs = setup_inputs


def setup_inputs(seed=0):
    import zlib

    import numpy as np

    out = dict(_drawn_inputs(seed))
    spreads = {}
    factors = {'edge_weight': 8.0,
     'L0_gnn_W_lin': 8.0,
     'L0_gnn_Wf1': 8.0,
     'L0_gnn_bf1': 8.0,
     'L0_gnn_Wf2': 8.0,
     'L0_gnn_bf2': 8.0,
     'L0_gnn_Wm1': 8.0,
     'L0_gnn_bm1': 26.36,
     'L0_gnn_Wm2': 3.598,
     'L0_gnn_bm2': 29.482,
     'L1_gnn_W_self': 5.229,
     'L1_gnn_b_self': 41.759,
     'L1_gnn_W_neigh': 6.449,
     'L1_gnn_b_neigh': 45.873}
    for name, (base, spread) in spreads.items():
        noise = np.random.default_rng([zlib.crc32(name.encode()), seed]).standard_normal(out[name].shape)
        drawn = base * np.exp(spread * noise) if base else spread * noise
        out[name] = jnp.asarray(drawn.astype(out[name].dtype))
    for name, factor in factors.items():
        out[name] = (out[name] * factor).astype(out[name].dtype)
    return out
```

```python
from contextlib import ExitStack

import numpy as np

import concourse.bass as bass
from concourse import mybir

N_ROWS = 50000
C = 128
P = 128
QT = 4
QROWS = QT * P
QUADS = -(-N_ROWS // QROWS)
ROWS = QUADS * QROWS
TABLE_ROWS = ROWS + P
CHAINS = 2
W2 = 132
BASIS = 50
BASIS_AT = (0, 64)
LN_EPS = 1e-5


def over_quads(eng, step):
    step(0, 0)
    step(1, 1)
    with eng.Fori(1, QUADS // 2 - 1) as i:
        step(2 * i, 0)
        step(2 * i + 1, 1)
    step(QUADS - 2, 0)
    step(QUADS - 1, 1)


def wait_used(eng, used, q, back):
    if isinstance(q, int) and q < back:
        return
    eng.wait_ge(used, q - back + 1)


def hold(eng, passed):
    eng.sem_inc(passed, 1)


def exists(q):
    return not isinstance(q, int) or q < QUADS


def gnn_kernel(nc, ins, out_dram):
    f32, i32 = mybir.dt.float32, mybir.dt.int32
    ALU = mybir.AluOpType
    ACT = mybir.ActivationFunctionType
    AX = mybir.AxisListType

    with ExitStack() as ctx:
        def sb(name, shape, dt=f32):
            return ctx.enter_context(nc.sbuf_tensor(name, shape, dt))

        def sem(name):
            return ctx.enter_context(nc.semaphore(name))

        def dram(name, shape):
            return nc.dram_tensor(name, shape, f32, kind="Internal").ap()

        agg1 = [dram(f"agg1_{k}", [TABLE_ROWS, C]) for k in range(CHAINS)]
        agg2 = [dram(f"agg2_{k}", [TABLE_ROWS, W2]) for k in range(CHAINS)]
        h1_dram = dram("h1_table", [ROWS, C])
        y_dram = dram("y_table", [ROWS, C])

        def quad_rows(table, q, width):
            return table[0:ROWS, :].rearrange("(q p t) c -> q p (t c)", p=P, t=QT)[q, :, :]

        ident = sb("ident", [P, P])
        lower = sb("lower", [P, P])
        cols = sb("cols", [P, 8])
        negc, dump, bf1, bm1 = (cols[:, k:k + 1] for k in range(4))
        wlin = sb("wlin", [P, C])
        wf1 = sb("wf1", [P, C])
        wf2 = sb("wf2", [P, C])
        wm1 = sb("wm1", [P, C])
        wm2 = sb("wm2", [P, C])
        wself = sb("wself", [P, C])
        wneigh = sb("wneigh", [P, C])
        bf2 = sb("bf2", [P, C])
        bm2 = sb("bm2", [P, C])
        bself = sb("bself", [P, C])
        bneigh = sb("bneigh", [P, C])
        weights = [(ident, "ident"), (lower, "lower"), (cols, "cols"), (wlin, "wlin"), (wf1, "wf1"), (wf2, "wf2"),
                   (wm1, "wm1"), (wm2, "wm2"), (wself, "wself"), (wneigh, "wneigh")]
        rows = [(bf2, "bf2"), (bm2, "bm2"), (bself, "bself"), (bneigh, "bneigh")]
        weights_loaded = sem("weights_loaded")
        ALL_WEIGHTS = 16 * (len(weights) + len(rows))

        zeros = sb("zeros", [P, 4096])
        zeros_set = sem("zeros_set")
        tables_zeroed = sem("tables_zeroed")
        pool_passed, dve_passed, sp_passed = sem("pool_passed"), sem("dve_passed"), sem("sp_passed")

        ew = sb("ew", [P, 2, QROWS])
        basis = sb("basis", [P, 2, QROWS])
        idx = sb("idx", [P, 2, 2, QT], i32)
        idxf = sb("idxf", [P, 2, QT])
        key_rows = sb("key_rows", [P, 2, QROWS], i32)
        same = sb("same", [P, 2, QT, P])
        junk = sb("junk", [P, QT, P])
        before = sb("before", [P, 2, QT])
        spare = sb("spare", [P, 2, QT])
        target = sb("target", [P, 2, QT], i32)
        counts = sb("counts", [P, 2, QT])
        xg = sb("xg", [P, 2, QT, C])
        stats = sb("stats", [P, QT, 6])
        mv = sb("mv", [P, QT, 2])
        ve = sb("ve", [P, QT])
        lnv = sb("lnv", [P, QT])
        r0 = sb("r0", [P, QT])
        r1 = sb("r1", [P, QT])
        r2 = sb("r2", [P, QT])
        r3 = sb("r3", [P, QT])
        rstd = sb("rstd", [P, QT])
        xn = sb("xn", [P, QT, C])
        hT = sb("hT", [P, QROWS])
        aT = sb("aT", [P, QROWS])
        absu = sb("absu", [P, QROWS])
        posu = sb("posu", [P, QROWS])
        eu = sb("eu", [P, QROWS])
        lu = sb("lu", [P, QROWS])
        su = sb("su", [P, QROWS])
        efb = sb("efb", [P, QROWS])
        msg = sb("msg", [P, QROWS])
        comb = sb("comb", [P, 2, QT, W2])
        comb1 = sb("comb1", [P, 2, QT, C])
        nagg = [sb(f"nagg{k}", [P, 2, QT, W2]) for k in range(CHAINS)]
        nx = sb("nx", [P, 2, QT, C])
        x1 = sb("x1", [P, 2, QT, C])
        h1s = sb("h1s", [P, 2, QT, C])
        ys = sb("ys", [P, 2, QT, C])
        rc = sb("rc", [P, 2, QT])
        cm = sb("cm", [P, 2, QT])

        bank = [ctx.enter_context(nc.psum_tensor(f"bank{k}", [P, 512], f32)) for k in range(8)]

        phase = [sem(f"phase{k}_done") for k in range(5)]

        def zero_parts(table, width):
            flat = table.rearrange("r c -> (r c)")
            total = TABLE_ROWS * width
            per = total // P
            view = flat.rearrange("(p n) -> p n", p=P)
            at = 0
            while at < per:
                n = min(4096, per - at)
                yield view[:, at:at + n], n
                at += n

        with nc.Block() as block:
            @block.vector
            def _(dve):
                nc.vector.memset(zeros[:], 0.0).then_inc(zeros_set, 1)

            @block.sync
            def _(sp):
                for t, name in weights:
                    sp.dma_start(t[:], ins[name]).then_inc(weights_loaded, 16)
                for t, name in rows:
                    sp.dma_start(t[:], ins[name].partition_broadcast(P)).then_inc(weights_loaded, 16)
                sp.wait_ge(weights_loaded, ALL_WEIGHTS)
                sp.wait_ge(zeros_set, 1)
                n = 0
                for table, width in [(t, C) for t in agg1] + [(t, W2) for t in agg2]:
                    for part, m in zero_parts(table, width):
                        sp.dma_start(part, zeros[:, 0:m]).then_inc(tables_zeroed, 16)
                        n += 16
                sp.wait_ge(tables_zeroed, n)

        with ExitStack() as sems:
            def s1(name):
                return sems.enter_context(nc.semaphore("e1_" + name))
            idx_loaded = [s1(f"idx_loaded{p}") for p in range(2)]
            keys_loaded = [s1(f"keys_loaded{p}") for p in range(2)]
            ew_loaded = s1("ew_loaded")
            gathered = [s1(f"gathered{p}") for p in range(2)]
            added = [s1(f"added{k}") for k in range(CHAINS)]
            squared, basis_ready = s1("squared"), s1("basis_ready")
            stats_ready, aggr_ready, var_ready = s1("stats_ready"), s1("aggr_ready"), s1("var_ready")
            ln_ready, r0_ready = s1("ln_ready"), s1("r0_ready")
            r1_ready, r2_ready, r3_ready, rstd_ready = s1("r1_ready"), s1("r2_ready"), s1("r3_ready"), s1("rstd_ready")
            xn_ready, xnT_ready, hT_ready, hs_ready = s1("xn_ready"), s1("xnT_ready"), s1("hT_ready"), s1("hs_ready")
            u_ready, absu_ready, posu_ready = s1("u_ready"), s1("absu_ready"), s1("posu_ready")
            eu_ready, lu_ready, su_ready, ef_ready = s1("eu_ready"), s1("lu_ready"), s1("su_ready"), s1("ef_ready")
            efb_ready, msg_ready, sum_ready, comb_ready = s1("efb_ready"), s1("msg_ready"), s1("sum_ready"), s1("comb_ready")
            idxf_ready, same_ready = s1("idxf_ready"), s1("same_ready")
            before_ready, spare_ready, target_ready = s1("before_ready"), s1("spare_ready"), s1("target_ready")
            u_ps, xT_ps, hs_ps, ef_ps, sum_ps = bank[0], bank[1], bank[2], bank[3], bank[4]

            block = sems.enter_context(nc.Block())

            @block.sync
            def _(sp):
                def load(q, par):
                    if not (isinstance(q, int) and q < 2):
                        sp.wait_ge(gathered[par], 64 * ((q - par) // 2) if isinstance(q, int) else 32 * q - 32 * par)
                    hold(sp, sp_passed)
                    wait_used(sp, idxf_ready, q, 2)
                    hold(sp, sp_passed)
                    sp.dma_start(idx[:, par, :, :].rearrange("p a t -> p (a t)"), ins["edge_cols"][q, :, :]).then_inc(idx_loaded[par], 16)
                    wait_used(sp, same_ready, q, 2)
                    hold(sp, sp_passed)
                    sp.dma_start(key_rows[:, par, :], ins["dst_rows"][q, :].partition_broadcast(P)).then_inc(keys_loaded[par], 16)

                def pair(j, n):
                    if not isinstance(j, int) or j >= 2:
                        sp.wait_ge(squared, j - 1)
                    hold(sp, sp_passed)
                    for half in range(2):
                        sp.dma_start(ew[64 * half:64 * half + 64, n, :],
                                     ins["ew_rows"][2 * j + half, :].partition_broadcast(64)).then_inc(ew_loaded, 16)
                pair(0, 0)
                load(0, 0)
                load(1, 1)
                with sp.Fori(0, QUADS // 2 - 1) as i:
                    sp.wait_ge(squared, i + 1)
                    hold(sp, sp_passed)
                    for half in range(2):
                        sp.dma_start(ew[64 * half:64 * half + 64, 0, :],
                                     ins["ew_rows"][2 * i + (2 + half), :].partition_broadcast(64)).then_inc(ew_loaded, 16)
                    for par in range(2):
                        q = 2 * i + (2 + par)
                        sp.wait_ge(gathered[par], 64 * i + 64)
                        hold(sp, sp_passed)
                        sp.wait_ge(idxf_ready, 2 * i + (par + 1))
                        hold(sp, sp_passed)
                        sp.dma_start(idx[:, par, :, :].rearrange("p a t -> p (a t)"), ins["edge_cols"][q, :, :]).then_inc(idx_loaded[par], 16)
                        sp.wait_ge(same_ready, 2 * i + (par + 1))
                        hold(sp, sp_passed)
                        sp.dma_start(key_rows[:, par, :], ins["dst_rows"][q, :].partition_broadcast(P)).then_inc(keys_loaded[par], 16)

            def half_count(q, par, unit):
                return unit * ((q - par) // 2 + 1) if isinstance(q, int) else (unit // 2) * q + (unit - (unit // 2) * par)

            @block.gpsimd
            def _(pool):
                def gather(q, par, t):
                    if t == 0:
                        pool.wait_ge(idx_loaded[par], half_count(q, par, 16))
                        wait_used(pool, xn_ready, q, 2)
                    hold(pool, pool_passed)
                    nc.gpsimd.indirect_dma_start(
                        out=xg[:, par, t, :], out_offset=None, in_=ins["x"],
                        in_offset=bass.IndirectOffsetOnAxis(ap=idx[:, par, 0, t:t + 1], axis=0)).then_inc(gathered[par], 16)

                def add(q, par, t):
                    if t == 0:
                        pool.wait_ge(comb_ready, q + 1)
                        pool.wait_ge(target_ready, q + 1)
                    k = t % CHAINS
                    n = 32 * q + 16 * (t // CHAINS)
                    if not (isinstance(n, int) and n == 0):
                        pool.wait_ge(added[k], n)
                    hold(pool, pool_passed)
                    nc.gpsimd.indirect_dma_start(
                        out=agg1[k], out_offset=bass.IndirectOffsetOnAxis(ap=target[:, par, t:t + 1], axis=0),
                        in_=comb1[:, par, t, :], in_offset=None, compute_op=ALU.add).then_inc(added[k], 16)

                for t in range(QT):
                    gather(0, 0, t)
                for t in range(QT):
                    gather(1, 1, t)

                def step(q, par):
                    for t in range(QT):
                        add(q, par, t)
                        if exists(q + 2):
                            gather(q + 2, par, t)
                over_quads(pool, step)
                for k in range(CHAINS):
                    pool.wait_ge(added[k], 32 * QUADS)

            @block.vector
            def _(dve):
                def norm_stats(q, par):
                    dve.wait_ge(gathered[par], half_count(q, par, 64))
                    for t in range(QT):
                        last = nc.vector.bn_stats(out=stats[:, t, :], in_=xg[:, par, t, :])
                    last.then_inc(stats_ready, 1)
                    dve.wait_ge(stats_ready, q + 1)
                    hold(dve, dve_passed)
                    for t in range(QT):
                        last = nc.vector.bn_aggr(out=mv[:, t, :], in_=stats[:, t, :])
                    last.then_inc(aggr_ready, 1)
                    dve.wait_ge(aggr_ready, q + 1)
                    wait_used(dve, ln_ready, q, 1)
                    nc.vector.tensor_scalar(ve[:], mv[:, :, 1], LN_EPS, None, ALU.add).then_inc(var_ready, 1)

                def normalise(q, par):
                    dve.wait_ge(r0_ready, q + 1)
                    nc.vector.tensor_tensor(r1[:], r0[:], r0[:], ALU.mult).then_inc(r1_ready, 1)
                    dve.wait_ge(r1_ready, q + 1)
                    nc.vector.tensor_tensor(r2[:], r1[:], ve[:], ALU.mult).then_inc(r2_ready, 1)
                    dve.wait_ge(r2_ready, q + 1)
                    nc.vector.tensor_scalar(r3[:], r2[:], -0.5, 1.5, ALU.mult, ALU.add).then_inc(r3_ready, 1)
                    dve.wait_ge(r3_ready, q + 1)
                    nc.vector.tensor_tensor(rstd[:], r3[:], r0[:], ALU.mult).then_inc(rstd_ready, 1)
                    dve.wait_ge(rstd_ready, q + 1)
                    wait_used(dve, xnT_ready, q, 1)
                    for t in range(QT):
                        last = nc.vector.tensor_scalar(xn[:, t, :], xg[:, par, t, :], mv[:, t, 0:1], rstd[:, t:t + 1],
                                                       ALU.subtract, ALU.mult)
                    last.then_inc(xn_ready, 1)

                def keys(q, par):
                    dve.wait_ge(idx_loaded[par], half_count(q, par, 16))
                    nc.vector.tensor_copy(idxf[:, par, :], idx[:, par, 1, :]).then_inc(idxf_ready, 1)
                    dve.wait_ge(idxf_ready, q + 1)
                    dve.wait_ge(keys_loaded[par], half_count(q, par, 16))
                    wait_used(dve, sum_ready, q, 2)
                    for t in range(QT):
                        last = nc.vector.tensor_scalar(same[:, par, t, :], key_rows[:, par, t * P:(t + 1) * P],
                                                       idxf[:, par, t:t + 1], None, ALU.is_equal)
                    last.then_inc(same_ready, 1)
                    dve.wait_ge(same_ready, q + 1)
                    for t in range(QT):
                        last = nc.vector.tensor_tensor_reduce(out=junk[:, t, :], in0=same[:, par, t, :], in1=lower[:], scale=1.0,
                                                              scalar=0.0, op0=ALU.mult, op1=ALU.add, accum_out=before[:, par, t:t + 1])
                    last.then_inc(before_ready, 1)
                    dve.wait_ge(before_ready, q + 1)
                    nc.vector.tensor_scalar(spare[:, par, :], before[:, par, :], 1.0, dump, ALU.min, ALU.mult).then_inc(spare_ready, 1)
                    dve.wait_ge(spare_ready, q + 1)
                    if not (isinstance(q, int) and q < 2):
                        for k in range(CHAINS):
                            dve.wait_ge(added[k], 32 * (q - 1))
                    nc.vector.tensor_tensor(target[:, par, :], spare[:, par, :], idxf[:, par, :], ALU.max).then_inc(target_ready, 1)

                def filter_in(q, par):
                    dve.wait_ge(u_ready, q + 1)
                    wait_used(dve, su_ready, q, 1)
                    nc.vector.tensor_scalar(posu[:], u_ps[:], bf1, 0.0, ALU.add, ALU.max).then_inc(posu_ready, 1)

                def filter_out(q, par):
                    dve.wait_ge(posu_ready, q + 1)
                    dve.wait_ge(lu_ready, q + 1)
                    wait_used(dve, ef_ready, q, 1)
                    nc.vector.tensor_tensor(su[:], posu[:], lu[:], ALU.add).then_inc(su_ready, 1)

                def message(q, par):
                    dve.wait_ge(ef_ready, q + 1)
                    wait_used(dve, msg_ready, q, 1)
                    nc.vector.tensor_tensor(efb[:].rearrange("p (t c) -> p t c", t=QT), ef_ps[:].rearrange("p (t c) -> p t c", t=QT),
                                            bf2[:].unsqueeze(1).broadcast_to([P, QT, C]), ALU.add).then_inc(efb_ready, 1)
                    dve.wait_ge(efb_ready, q + 1)
                    dve.wait_ge(hs_ready, q + 1)
                    wait_used(dve, sum_ready, q, 1)
                    nc.vector.tensor_tensor(msg[:], hs_ps[:], efb[:], ALU.mult).then_inc(msg_ready, 1)

                def stage_a(q, par):
                    norm_stats(q, par)
                    filter_in(q, par)
                    normalise(q, par)
                    filter_out(q, par)
                    keys(q, par)
                stage_a(0, 0)

                def step(q, par):
                    if exists(q + 1):
                        norm_stats(q + 1, 1 - par)
                    message(q, par)
                    if exists(q + 1):
                        normalise(q + 1, 1 - par)
                        filter_in(q + 1, 1 - par)
                        keys(q + 1, 1 - par)
                        filter_out(q + 1, 1 - par)
                over_quads(dve, step)

            @block.scalar
            def _(act):
                coef = 1.0 / (2.0 * float(CENTERS[1] - CENTERS[0]) ** 2)

                def make_basis(j):
                    act.wait_ge(ew_loaded, 32 * j + 32)
                    if not (isinstance(j, int) and j < 1):
                        act.wait_ge(u_ready, 2 * j)
                    nc.scalar.activation(basis[:, 1, :], ew[:, 0, :], ACT.Square, bias=negc).then_inc(squared, 1)
                    act.wait_ge(squared, j + 1)
                    nc.scalar.activation(basis[:, 0, :], basis[:, 1, :], ACT.Exp, scale=-coef).then_inc(basis_ready, 1)

                def rstd_start(q):
                    act.wait_ge(var_ready, q + 1)
                    nc.scalar.activation(lnv[:], ve[:], ACT.Ln).then_inc(ln_ready, 1)
                    act.wait_ge(ln_ready, q + 1)
                    wait_used(act, rstd_ready, q, 1)
                    nc.scalar.activation(r0[:], lnv[:], ACT.Exp, scale=-0.5).then_inc(r0_ready, 1)

                def softplus(q):
                    act.wait_ge(posu_ready, q + 1)
                    wait_used(act, eu_ready, q, 1)
                    nc.scalar.activation(absu[:], u_ps[:], ACT.Abs, bias=bf1).then_inc(absu_ready, 1)
                    act.wait_ge(absu_ready, q + 1)
                    nc.scalar.activation(eu[:], absu[:], ACT.Exp, scale=-1.0).then_inc(eu_ready, 1)
                    act.wait_ge(eu_ready, q + 1)
                    wait_used(act, su_ready, q, 1)
                    nc.scalar.activation(lu[:], eu[:], ACT.Ln, scale=0.5, bias=half).then_inc(lu_ready, 1)

                def relu(q):
                    act.wait_ge(xnT_ready, q + 1)
                    wait_used(act, hs_ready, q, 1)
                    nc.scalar.activation(hT[:], xT_ps[:], ACT.Relu).then_inc(hT_ready, 1)

                def sum_out(q, par):
                    act.wait_ge(sum_ready, q + 1)
                    if not (isinstance(q, int) and q < 2):
                        for k in range(CHAINS):
                            act.wait_ge(added[k], 32 * (q - 1))
                    nc.scalar.activation(comb1[:, par, :, :].rearrange("p t c -> p (t c)"), sum_ps[:], ACT.Copy).then_inc(comb_ready, 1)

                half = cols[:, 4:5]
                make_basis(0)
                rstd_start(0)
                softplus(0)
                relu(0)

                def step(q, par):
                    if exists(q + 1):
                        rstd_start(q + 1)
                        if par == 1:
                            make_basis((q + 1) // 2 if isinstance(q, int) else pair_of[0])
                        relu(q + 1)
                    sum_out(q, par)
                    if exists(q + 1):
                        softplus(q + 1)
                pair_of = [None]
                step(0, 0)
                step(1, 1)
                with act.Fori(1, QUADS // 2 - 1) as i:
                    pair_of[0] = i + 1
                    step(2 * i, 0)
                    step(2 * i + 1, 1)
                step(QUADS - 2, 0)
                step(QUADS - 1, 1)

            @block.tensor
            def _(pe):
                def filter_up(q, par):
                    pe.wait_ge(basis_ready, half_count(q, par, 2) // 2 if isinstance(q, int) else pair_of[0])
                    wait_used(pe, posu_ready, q, 1)
                    wait_used(pe, absu_ready, q, 1)
                    at = BASIS_AT[par]
                    nc.tensor.matmul(u_ps[:], wf1[at:at + BASIS, :], basis[at:at + BASIS, 0, :],
                                     start=True, stop=True).then_inc(u_ready, 1)

                def filter_down(q):
                    pe.wait_ge(su_ready, q + 1)
                    wait_used(pe, efb_ready, q, 1)
                    for t in range(QT):
                        last = nc.tensor.matmul(ef_ps[:, t * P:(t + 1) * P], su[:, t * P:(t + 1) * P], wf2[:], start=True, stop=True)
                    last.then_inc(ef_ready, 1)

                def turn(q):
                    pe.wait_ge(xn_ready, q + 1)
                    wait_used(pe, hT_ready, q, 1)
                    for t in range(QT):
                        last = nc.tensor.transpose(xT_ps[:, t * P:(t + 1) * P], xn[:, t, :], ident[:])
                    last.then_inc(xnT_ready, 1)

                def project(q):
                    pe.wait_ge(hT_ready, q + 1)
                    wait_used(pe, msg_ready, q, 1)
                    for t in range(QT):
                        last = nc.tensor.matmul(hs_ps[:, t * P:(t + 1) * P], hT[:, t * P:(t + 1) * P], wlin[:], start=True, stop=True)
                    last.then_inc(hs_ready, 1)

                def tile_sums(q, par):
                    pe.wait_ge(msg_ready, q + 1)
                    pe.wait_ge(same_ready, q + 1)
                    wait_used(pe, comb_ready, q, 1)
                    for t in range(QT):
                        last = nc.tensor.matmul(sum_ps[:, t * P:(t + 1) * P], same[:, par, t, :], msg[:, t * P:(t + 1) * P], start=True, stop=True)
                    last.then_inc(sum_ready, 1)

                pair_of = [None]
                filter_up(0, 0)
                turn(0)
                project(0)
                filter_down(0)

                def step(q, par):
                    tile_sums(q, par)
                    if exists(q + 1):
                        turn(q + 1)
                        filter_up(q + 1, 1 - par)
                        project(q + 1)
                        filter_down(q + 1)
                step(0, 0)
                step(1, 1)
                with pe.Fori(1, QUADS // 2 - 1) as i:
                    pair_of[0] = i + 1
                    step(2 * i, 0)
                    pair_of[0] = i + 2
                    step(2 * i + 1, 1)
                step(QUADS - 2, 0)
                step(QUADS - 1, 1)

        with ExitStack() as sems:
            def s2(name):
                return sems.enter_context(nc.semaphore("n1_" + name))
            loaded = [s2(f"loaded{p}") for p in range(2)]
            stored = [s2(f"stored{p}") for p in range(2)]
            agg_ready, xb_ready, aggT_ready, aT_ready = s2("agg_ready"), s2("xb_ready"), s2("aggT_ready"), s2("aT_ready")
            stats_ready, aggr_ready, var_ready = s2("stats_ready"), s2("aggr_ready"), s2("var_ready")
            ln_ready, r0_ready = s2("ln_ready"), s2("r0_ready")
            r1_ready, r2_ready, r3_ready, rstd_ready = s2("r1_ready"), s2("r2_ready"), s2("r3_ready"), s2("rstd_ready")
            xn_ready, xnT_ready, hT_ready, self_ready = s2("xn_ready"), s2("xnT_ready"), s2("hT_ready"), s2("self_ready")
            u_ready, absu_ready, posu_ready = s2("u_ready"), s2("absu_ready"), s2("posu_ready")
            eu_ready, lu_ready, su_ready, mlp_ready = s2("eu_ready"), s2("lu_ready"), s2("su_ready"), s2("mlp_ready")
            x1_ready, x1b_ready, h1_ready, y_ready = s2("x1_ready"), s2("x1b_ready"), s2("h1_ready"), s2("y_ready")
            aggT_ps, u_ps, mlp_ps, xT_ps, self_ps = bank[0], bank[1], bank[2], bank[3], bank[4]
            block = sems.enter_context(nc.Block())

            def half_count(q, par, unit):
                return unit * ((q - par) // 2 + 1) if isinstance(q, int) else (unit // 2) * q + (unit - (unit // 2) * par)

            def flat(t, par, width=C):
                return t[:, par, :, :].rearrange("p t c -> p (t c)")

            def agg_in(k, par):
                return nagg[k][:, par, :, :].rearrange("p t c -> p (t c)")[:, 0:QT * C]

            @block.sync
            def _(sp):
                def load(q, par):
                    wait_used(sp, agg_ready, q, 2)
                    hold(sp, sp_passed)
                    wait_used(sp, xb_ready, q, 2)
                    hold(sp, sp_passed)
                    for k in range(CHAINS):
                        sp.dma_start(agg_in(k, par), quad_rows(agg1[k], q, C)).then_inc(loaded[par], 16)
                    sp.dma_start(flat(nx, par), quad_rows(ins["x"], q, C)).then_inc(loaded[par], 16)
                over_quads(sp, load)

            @block.gpsimd
            def _(pool):
                def enter(q, par):
                    pool.wait_ge(loaded[par], half_count(q, par, 48))
                    wait_used(pool, aggT_ready, q, 1)
                    nc.gpsimd.tensor_tensor(msg[:], agg_in(0, par), agg_in(1, par), ALU.add).then_inc(agg_ready, 1)
                    wait_used(pool, x1_ready, q, 2)
                    nc.gpsimd.tensor_tensor(xg[:, par, :, :], nx[:, par, :, :], bm2[:].unsqueeze(1).broadcast_to([P, QT, C]),
                                            ALU.add).then_inc(xb_ready, 1)
                enter(0, 0)

                def step(q, par):
                    if exists(q + 1):
                        enter(q + 1, 1 - par)
                    pool.wait_ge(x1_ready, q + 1)
                    wait_used(pool, y_ready, q, 1)
                    nc.gpsimd.tensor_tensor(efb[:].rearrange("p (t c) -> p t c", t=QT), x1[:, par, :, :],
                                            bself[:].unsqueeze(1).broadcast_to([P, QT, C]), ALU.add).then_inc(x1b_ready, 1)
                    pool.wait_ge(xn_ready, q + 1)
                    if not (isinstance(q, int) and q < 2):
                        pool.wait_ge(stored[par], half_count(q, par, 32) - 32)
                    hold(pool, pool_passed)
                    nc.gpsimd.tensor_scalar(h1s[:, par, :, :].rearrange("p t c -> p (t c)"), xn[:].rearrange("p t c -> p (t c)"), 0.0, None, ALU.max).then_inc(h1_ready, 1)
                over_quads(pool, step)

            @block.vector
            def _(dve):
                def mlp_in(q):
                    dve.wait_ge(u_ready, q + 1)
                    wait_used(dve, su_ready, q, 1)
                    nc.vector.tensor_scalar(posu[:], u_ps[:], bm1, 0.0, ALU.add, ALU.max).then_inc(posu_ready, 1)

                def mlp_out(q):
                    dve.wait_ge(posu_ready, q + 1)
                    dve.wait_ge(lu_ready, q + 1)
                    wait_used(dve, mlp_ready, q, 1)
                    nc.vector.tensor_tensor(su[:], posu[:], lu[:], ALU.add).then_inc(su_ready, 1)

                def residual(q, par):
                    dve.wait_ge(mlp_ready, q + 1)
                    dve.wait_ge(xb_ready, q + 1)
                    wait_used(dve, xn_ready, q, 2)
                    wait_used(dve, x1b_ready, q, 2)
                    nc.vector.tensor_tensor(flat(x1, par), mlp_ps[:], flat(xg, par), ALU.add).then_inc(x1_ready, 1)
                    dve.wait_ge(x1_ready, q + 1)
                    for t in range(QT):
                        last = nc.vector.bn_stats(out=stats[:, t, :], in_=x1[:, par, t, :])
                    last.then_inc(stats_ready, 1)
                    dve.wait_ge(stats_ready, q + 1)
                    hold(dve, dve_passed)
                    for t in range(QT):
                        last = nc.vector.bn_aggr(out=mv[:, t, :], in_=stats[:, t, :])
                    last.then_inc(aggr_ready, 1)
                    dve.wait_ge(aggr_ready, q + 1)
                    wait_used(dve, ln_ready, q, 1)
                    nc.vector.tensor_scalar(ve[:], mv[:, :, 1], LN_EPS, None, ALU.add).then_inc(var_ready, 1)

                def normalise(q, par):
                    dve.wait_ge(r0_ready, q + 1)
                    nc.vector.tensor_tensor(r1[:], r0[:], r0[:], ALU.mult).then_inc(r1_ready, 1)
                    dve.wait_ge(r1_ready, q + 1)
                    nc.vector.tensor_tensor(r2[:], r1[:], ve[:], ALU.mult).then_inc(r2_ready, 1)
                    dve.wait_ge(r2_ready, q + 1)
                    nc.vector.tensor_scalar(r3[:], r2[:], -0.5, 1.5, ALU.mult, ALU.add).then_inc(r3_ready, 1)
                    dve.wait_ge(r3_ready, q + 1)
                    nc.vector.tensor_tensor(rstd[:], r3[:], r0[:], ALU.mult).then_inc(rstd_ready, 1)
                    dve.wait_ge(rstd_ready, q + 1)
                    wait_used(dve, xnT_ready, q, 1)
                    wait_used(dve, h1_ready, q, 1)
                    for t in range(QT):
                        last = nc.vector.tensor_scalar(xn[:, t, :], x1[:, par, t, :], mv[:, t, 0:1], rstd[:, t:t + 1],
                                                       ALU.subtract, ALU.mult)
                    last.then_inc(xn_ready, 1)

                def leave(q, par):
                    dve.wait_ge(self_ready, q + 1)
                    dve.wait_ge(x1b_ready, q + 1)
                    if not (isinstance(q, int) and q < 2):
                        dve.wait_ge(stored[par], half_count(q, par, 32) - 32)
                    nc.vector.tensor_tensor(flat(ys, par), self_ps[:], efb[:], ALU.add).then_inc(y_ready, 1)

                mlp_in(0)
                mlp_out(0)

                def step(q, par):
                    residual(q, par)
                    if exists(q + 1):
                        mlp_in(q + 1)
                    normalise(q, par)
                    if exists(q + 1):
                        mlp_out(q + 1)
                    leave(q, par)
                over_quads(dve, step)

            @block.scalar
            def _(act):
                half = cols[:, 4:5]

                def agg_turned(q):
                    act.wait_ge(aggT_ready, q + 1)
                    wait_used(act, u_ready, q, 1)
                    nc.scalar.activation(aT[:], aggT_ps[:], ACT.Copy).then_inc(aT_ready, 1)

                def softplus(q):
                    act.wait_ge(posu_ready, q + 1)
                    wait_used(act, eu_ready, q, 1)
                    nc.scalar.activation(absu[:], u_ps[:], ACT.Abs, bias=bm1).then_inc(absu_ready, 1)
                    act.wait_ge(absu_ready, q + 1)
                    nc.scalar.activation(eu[:], absu[:], ACT.Exp, scale=-1.0).then_inc(eu_ready, 1)
                    act.wait_ge(eu_ready, q + 1)
                    wait_used(act, su_ready, q, 1)
                    nc.scalar.activation(lu[:], eu[:], ACT.Ln, scale=0.5, bias=half).then_inc(lu_ready, 1)

                agg_turned(0)
                softplus(0)

                def step(q, par):
                    if exists(q + 1):
                        agg_turned(q + 1)
                    act.wait_ge(var_ready, q + 1)
                    nc.scalar.activation(lnv[:], ve[:], ACT.Ln).then_inc(ln_ready, 1)
                    act.wait_ge(ln_ready, q + 1)
                    wait_used(act, rstd_ready, q, 1)
                    nc.scalar.activation(r0[:], lnv[:], ACT.Exp, scale=-0.5).then_inc(r0_ready, 1)
                    if exists(q + 1):
                        softplus(q + 1)
                    act.wait_ge(xnT_ready, q + 1)
                    wait_used(act, self_ready, q, 1)
                    nc.scalar.activation(hT[:], xT_ps[:], ACT.Relu).then_inc(hT_ready, 1)
                    act.wait_ge(h1_ready, q + 1)
                    act.dma_start(quad_rows(h1_dram, q, C), flat(h1s, par)).then_inc(stored[par], 16)
                    act.wait_ge(y_ready, q + 1)
                    act.dma_start(quad_rows(y_dram, q, C), flat(ys, par)).then_inc(stored[par], 16)
                over_quads(act, step)
                for par in range(2):
                    act.wait_ge(stored[par], 32 * (QUADS // 2))

            @block.tensor
            def _(pe):
                def agg_up(q):
                    pe.wait_ge(agg_ready, q + 1)
                    wait_used(pe, aT_ready, q, 1)
                    for t in range(QT):
                        last = nc.tensor.transpose(aggT_ps[:, t * P:(t + 1) * P], msg[:, t * P:(t + 1) * P], ident[:])
                    last.then_inc(aggT_ready, 1)
                    pe.wait_ge(aT_ready, q + 1)
                    wait_used(pe, posu_ready, q, 1)
                    wait_used(pe, absu_ready, q, 1)
                    nc.tensor.matmul(u_ps[:], wm1[:], aT[:], start=True, stop=True).then_inc(u_ready, 1)

                def mlp_down(q):
                    pe.wait_ge(su_ready, q + 1)
                    wait_used(pe, x1_ready, q, 1)
                    for t in range(QT):
                        last = nc.tensor.matmul(mlp_ps[:, t * P:(t + 1) * P], su[:, t * P:(t + 1) * P], wm2[:], start=True, stop=True)
                    last.then_inc(mlp_ready, 1)
                agg_up(0)
                mlp_down(0)

                def step(q, par):
                    if exists(q + 1):
                        agg_up(q + 1)
                    pe.wait_ge(xn_ready, q + 1)
                    wait_used(pe, hT_ready, q, 1)
                    for t in range(QT):
                        last = nc.tensor.transpose(xT_ps[:, t * P:(t + 1) * P], xn[:, t, :], ident[:])
                    last.then_inc(xnT_ready, 1)
                    if exists(q + 1):
                        mlp_down(q + 1)
                    pe.wait_ge(hT_ready, q + 1)
                    wait_used(pe, y_ready, q, 1)
                    for t in range(QT):
                        last = nc.tensor.matmul(self_ps[:, t * P:(t + 1) * P], hT[:, t * P:(t + 1) * P], wself[:], start=True, stop=True)
                    last.then_inc(self_ready, 1)
                over_quads(pe, step)

        with ExitStack() as sems:
            def s3(name):
                return sems.enter_context(nc.semaphore("e2_" + name))
            idx_loaded = [s3(f"idx_loaded{p}") for p in range(2)]
            keys_loaded = [s3(f"keys_loaded{p}") for p in range(2)]
            gathered = [s3(f"gathered{p}") for p in range(2)]
            added = [s3(f"added{k}") for k in range(CHAINS)]
            idxf_ready, same_ready, counted = s3("idxf_ready"), s3("same_ready"), s3("counted")
            before_ready, spare_ready, target_ready = s3("before_ready"), s3("spare_ready"), s3("target_ready")
            sumT_ready, sT_ready, neigh_ready, comb_ready = s3("sumT_ready"), s3("sT_ready"), s3("neigh_ready"), s3("comb_ready")
            sumT_ps, neigh_ps = bank[0], bank[1]
            block = sems.enter_context(nc.Block())

            @block.sync
            def _(sp):
                def load(q, par):
                    if not (isinstance(q, int) and q < 2):
                        sp.wait_ge(gathered[par], half_count(q, par, 64) - 64)
                    hold(sp, sp_passed)
                    wait_used(sp, idxf_ready, q, 2)
                    hold(sp, sp_passed)
                    sp.dma_start(idx[:, par, :, :].rearrange("p a t -> p (a t)"), ins["edge_cols"][q, :, :]).then_inc(idx_loaded[par], 16)
                    wait_used(sp, same_ready, q, 2)
                    hold(sp, sp_passed)
                    sp.dma_start(key_rows[:, par, :], ins["src_rows"][q, :].partition_broadcast(P)).then_inc(keys_loaded[par], 16)
                over_quads(sp, load)

            @block.gpsimd
            def _(pool):
                def gather(q, par, t):
                    if t == 0:
                        pool.wait_ge(idx_loaded[par], half_count(q, par, 16))
                        wait_used(pool, sumT_ready, q, 2)
                    hold(pool, pool_passed)
                    nc.gpsimd.indirect_dma_start(
                        out=xg[:, par, t, :], out_offset=None, in_=h1_dram,
                        in_offset=bass.IndirectOffsetOnAxis(ap=idx[:, par, 1, t:t + 1], axis=0)).then_inc(gathered[par], 16)

                def add(q, par, t):
                    if t == 0:
                        pool.wait_ge(comb_ready, q + 1)
                        pool.wait_ge(target_ready, q + 1)
                        pool.wait_ge(counted, q + 1)
                    k = t % CHAINS
                    n = 32 * q + 16 * (t // CHAINS)
                    if not (isinstance(n, int) and n == 0):
                        pool.wait_ge(added[k], n)
                    hold(pool, pool_passed)
                    nc.gpsimd.indirect_dma_start(
                        out=agg2[k], out_offset=bass.IndirectOffsetOnAxis(ap=target[:, par, t:t + 1], axis=0),
                        in_=comb[:, par, t, :], in_offset=None, compute_op=ALU.add).then_inc(added[k], 16)

                for t in range(QT):
                    gather(0, 0, t)
                for t in range(QT):
                    gather(1, 1, t)

                def step(q, par):
                    for t in range(QT):
                        add(q, par, t)
                        if exists(q + 2):
                            gather(q + 2, par, t)
                over_quads(pool, step)
                for k in range(CHAINS):
                    pool.wait_ge(added[k], 32 * QUADS)

            @block.vector
            def _(dve):
                def step(q, par):
                    dve.wait_ge(idx_loaded[par], half_count(q, par, 16))
                    nc.vector.tensor_copy(idxf[:, par, :], idx[:, par, 0, :]).then_inc(idxf_ready, 1)
                    dve.wait_ge(idxf_ready, q + 1)
                    dve.wait_ge(keys_loaded[par], half_count(q, par, 16))
                    wait_used(dve, sumT_ready, q, 2)
                    for t in range(QT):
                        last = nc.vector.tensor_scalar(same[:, par, t, :], key_rows[:, par, t * P:(t + 1) * P],
                                                       idxf[:, par, t:t + 1], None, ALU.is_equal)
                    last.then_inc(same_ready, 1)
                    dve.wait_ge(same_ready, q + 1)
                    for t in range(QT):
                        last = nc.vector.tensor_tensor_reduce(out=junk[:, t, :], in0=same[:, par, t, :], in1=lower[:], scale=1.0,
                                                              scalar=0.0, op0=ALU.mult, op1=ALU.add, accum_out=before[:, par, t:t + 1])
                    last.then_inc(before_ready, 1)
                    dve.wait_ge(before_ready, q + 1)
                    nc.vector.tensor_scalar(spare[:, par, :], before[:, par, :], 1.0, dump, ALU.min, ALU.mult).then_inc(spare_ready, 1)
                    dve.wait_ge(spare_ready, q + 1)
                    if not (isinstance(q, int) and q < 2):
                        for k in range(CHAINS):
                            dve.wait_ge(added[k], 32 * (q - 1))
                    else:
                        nc.vector.memset(comb[:, par, :, C:W2], 0.0)
                    nc.vector.tensor_tensor(target[:, par, :], spare[:, par, :], idxf[:, par, :], ALU.max).then_inc(target_ready, 1)
                    dve.wait_ge(target_ready, q + 1)
                    nc.vector.tensor_reduce(out=comb[:, par, :, C], in_=same[:, par, :, :], axis=AX.X, op=ALU.add).then_inc(counted, 1)
                over_quads(dve, step)

            @block.tensor
            def _(pe):
                def sums(q, par):
                    pe.wait_ge(gathered[par], half_count(q, par, 64))
                    pe.wait_ge(same_ready, q + 1)
                    wait_used(pe, sT_ready, q, 1)
                    for t in range(QT):
                        last = nc.tensor.matmul(sumT_ps[:, t * P:(t + 1) * P], xg[:, par, t, :], same[:, par, t, :], start=True, stop=True)
                    last.then_inc(sumT_ready, 1)
                    pe.wait_ge(sT_ready, q + 1)
                    wait_used(pe, comb_ready, q, 1)
                    for t in range(QT):
                        last = nc.tensor.matmul(neigh_ps[:, t * P:(t + 1) * P], hT[:, t * P:(t + 1) * P], wneigh[:], start=True, stop=True)
                    last.then_inc(neigh_ready, 1)
                over_quads(pe, sums)

            @block.scalar
            def _(act):
                def step(q, par):
                    act.wait_ge(sumT_ready, q + 1)
                    wait_used(act, neigh_ready, q, 1)
                    nc.scalar.activation(hT[:], sumT_ps[:], ACT.Copy).then_inc(sT_ready, 1)
                    act.wait_ge(neigh_ready, q + 1)
                    if not (isinstance(q, int) and q < 2):
                        for k in range(CHAINS):
                            act.wait_ge(added[k], 32 * (q - 1))
                    nc.scalar.activation(comb[:, par, :, 0:C], neigh_ps[:].rearrange("p (t c) -> p t c", t=QT), ACT.Copy).then_inc(comb_ready, 1)
                over_quads(act, step)

        with ExitStack() as sems:
            def s4(name):
                return sems.enter_context(nc.semaphore("n2_" + name))
            loaded = [s4(f"loaded{p}") for p in range(2)]
            stored = [s4(f"stored{p}") for p in range(2)]
            agg_ready, capped, rc_ready, cm_ready = s4("agg_ready"), s4("capped"), s4("rc_ready"), s4("cm_ready")
            yb_ready, out_ready = s4("yb_ready"), s4("out_ready")
            block = sems.enter_context(nc.Block())

            @block.sync
            def _(sp):
                def load(q, par):
                    wait_used(sp, agg_ready, q, 2)
                    hold(sp, sp_passed)
                    wait_used(sp, yb_ready, q, 2)
                    hold(sp, sp_passed)
                    for k in range(CHAINS):
                        sp.dma_start(flat(nagg[k], par), quad_rows(agg2[k], q, W2)).then_inc(loaded[par], 16)
                    sp.dma_start(flat(nx, par), quad_rows(y_dram, q, C)).then_inc(loaded[par], 16)
                over_quads(sp, load)

            @block.gpsimd
            def _(pool):
                def step(q, par):
                    pool.wait_ge(loaded[par], half_count(q, par, 48))
                    wait_used(pool, out_ready, q, 2)
                    nc.gpsimd.tensor_tensor(flat(comb, par), flat(nagg[0], par), flat(nagg[1], par), ALU.add).then_inc(agg_ready, 1)
                over_quads(pool, step)

            @block.vector
            def _(dve):
                def step(q, par):
                    dve.wait_ge(agg_ready, q + 1)
                    nc.vector.tensor_scalar(cm[:, par, :], comb[:, par, :, C], 1.0, None, ALU.min).then_inc(cm_ready, 1)
                    nc.vector.tensor_scalar(counts[:, par, :], comb[:, par, :, C], 1.0, None, ALU.max).then_inc(capped, 1)
                    dve.wait_ge(capped, q + 1)
                    nc.vector.reciprocal(rc[:, par, :], counts[:, par, :]).then_inc(rc_ready, 1)
                    dve.wait_ge(cm_ready, q + 1)
                    dve.wait_ge(rc_ready, q + 1)
                    wait_used(dve, out_ready, q, 2)
                    for t in range(QT):
                        last = nc.vector.scalar_tensor_tensor(out=x1[:, par, t, :], in0=bneigh[:], scalar=cm[:, par, t:t + 1],
                                                              in1=nx[:, par, t, :], op0=ALU.mult, op1=ALU.add)
                    last.then_inc(yb_ready, 1)
                    dve.wait_ge(yb_ready, q + 1)
                    if not (isinstance(q, int) and q < 2):
                        dve.wait_ge(stored[par], half_count(q, par, 16) - 16)
                    for t in range(QT):
                        last = nc.vector.scalar_tensor_tensor(out=ys[:, par, t, :], in0=comb[:, par, t, 0:C], scalar=rc[:, par, t:t + 1],
                                                              in1=x1[:, par, t, :], op0=ALU.mult, op1=ALU.add)
                    last.then_inc(out_ready, 1)
                over_quads(dve, step)

            @block.scalar
            def _(act):
                def step(q, par):
                    act.wait_ge(out_ready, q + 1)
                    act.dma_start(quad_rows(out_dram, q, C), flat(ys, par)).then_inc(stored[par], 16)
                over_quads(act, step)
                for par in range(2):
                    act.wait_ge(stored[par], 16 * (QUADS // 2))


CENTERS = (np.arange(BASIS, dtype=np.float32) / np.float32(BASIS - 1)) * np.float32(5.0)


def kernel(x, src, dst, edge_weight, L0_gnn_W_lin, L0_gnn_Wf1, L0_gnn_bf1, L0_gnn_Wf2, L0_gnn_bf2, L0_gnn_Wm1, L0_gnn_bm1,
           L0_gnn_Wm2, L0_gnn_bm2, L1_gnn_W_self, L1_gnn_b_self, L1_gnn_W_neigh, L1_gnn_b_neigh):
    import concourse.bacc as bacc
    from concourse.bass_utils import run_bass_kernel_spmd

    pad = ROWS - N_ROWS
    extra = np.arange(N_ROWS, ROWS, dtype=np.int32)
    src_pad = np.concatenate([np.asarray(src), extra])
    dst_pad = np.concatenate([np.asarray(dst), extra])
    ew_pad = np.concatenate([np.asarray(edge_weight), np.zeros(pad, np.float32)])
    x_pad = np.concatenate([np.asarray(x), np.zeros((pad, C), np.float32)])

    def by_column(a):
        return a.reshape(QUADS, QT, P).transpose(0, 2, 1)

    cols = np.zeros((P, 8), np.float32)
    for at in BASIS_AT:
        cols[at:at + BASIS, 0] = -CENTERS
    cols[:, 1] = ROWS + np.arange(P)
    cols[:, 2] = np.asarray(L0_gnn_bf1)
    cols[:, 3] = np.asarray(L0_gnn_bm1)
    cols[:, 4] = 0.5
    wf1 = np.zeros((P, C), np.float32)
    for at in BASIS_AT:
        wf1[at:at + BASIS] = np.asarray(L0_gnn_Wf1)
    arrays = {
        "x": x_pad,
        "edge_cols": np.concatenate([by_column(src_pad), by_column(dst_pad)], axis=2),
        "src_rows": src_pad.reshape(QUADS, QROWS),
        "dst_rows": dst_pad.reshape(QUADS, QROWS),
        "ew_rows": ew_pad.reshape(QUADS, QROWS),
        "ident": np.eye(P, dtype=np.float32),
        "lower": np.tri(P, k=-1, dtype=np.float32),
        "cols": cols,
        "wlin": np.asarray(L0_gnn_W_lin).T, "wf1": wf1, "wf2": np.asarray(L0_gnn_Wf2),
        "wm1": np.asarray(L0_gnn_Wm1), "wm2": np.asarray(L0_gnn_Wm2),
        "wself": np.asarray(L1_gnn_W_self).T, "wneigh": np.asarray(L1_gnn_W_neigh).T,
        "bf2": np.asarray(L0_gnn_bf2), "bm2": np.asarray(L0_gnn_bm2),
        "bself": np.asarray(L1_gnn_b_self), "bneigh": np.asarray(L1_gnn_b_neigh),
    }
    nc = bacc.Bacc("TRN2", target_bir_lowering=False, num_devices=1)
    given, ins = {}, {}
    for name, a in arrays.items():
        a = np.ascontiguousarray(a)
        given[f"in_{name}"] = a
        ins[name] = nc.dram_tensor(f"in_{name}", a.shape, mybir.dt.from_np(a.dtype), kind="ExternalInput").ap()
    out = nc.dram_tensor("out", (ROWS, C), mybir.dt.float32, kind="ExternalOutput").ap()
    gnn_kernel(nc, ins, out)
    r = run_bass_kernel_spmd(nc, [given], core_ids=[0])
    return r.results[0]["out"][:N_ROWS]
```

```python
from contextlib import ExitStack

import numpy as np

import concourse.bass as bass
from concourse import mybir

N_ROWS = 50000
C = 128
P = 128
QT = 4
QROWS = QT * P
QUADS = -(-N_ROWS // QROWS)
ROWS = QUADS * QROWS
TABLE_ROWS = ROWS + P
CHAINS = 2
W2 = 132
BASIS = 50
BASIS_AT = (0, 64)
TILES = QUADS * QT
SPAN = 2 * P
MW = C + 1
AHEAD = 2
LAG = 6
HI, LO = -(-ROWS // 4096), 32
ZEROS = 4096
TOP = 40.0
LOG2 = 0.6931471805599453
LN_EPS = 1e-5


def over_quads(eng, step):
    step(0, 0)
    step(1, 1)
    with eng.Fori(1, QUADS // 2 - 1) as i:
        step(2 * i, 0)
        step(2 * i + 1, 1)
    step(QUADS - 2, 0)
    step(QUADS - 1, 1)


def wait_used(eng, used, q, back):
    if isinstance(q, int) and q < back:
        return
    eng.wait_ge(used, q - back + 1)


def hold(eng, passed):
    eng.sem_inc(passed, 1)


def half_count(q, par, unit):
    return unit * ((q - par) // 2 + 1) if isinstance(q, int) else (unit // 2) * q + (unit - (unit // 2) * par)


def at_first(q, count):
    return isinstance(q, int) and q < count


def there(q):
    return not isinstance(q, int) or 0 <= q < QUADS


def over_steps(eng, step, pair_of=None):
    first = LAG + 4
    for s in range(-1, first):
        step(s, s % 2)
    loops = (QUADS - 3 - first) // 2
    with eng.Fori(0, loops) as i:
        if pair_of is not None:
            pair_of[0] = i + (first // 2 + 1)
        step(2 * i + first, 0)
        step(2 * i + (first + 1), 1)
    for s in range(first + 2 * loops, QUADS + LAG):
        step(s, s % 2)


def exists(q):
    return not isinstance(q, int) or q < QUADS


def gnn_kernel(nc, ins, out_dram):
    f32, i32, bf16 = mybir.dt.float32, mybir.dt.int32, mybir.dt.bfloat16
    ALU = mybir.AluOpType
    ACT = mybir.ActivationFunctionType
    AX = mybir.AxisListType

    with ExitStack() as ctx:
        def sb(name, shape, dt=f32):
            return ctx.enter_context(nc.sbuf_tensor(name, shape, dt))

        def sem(name):
            return ctx.enter_context(nc.semaphore(name))

        def dram(name, shape):
            return nc.dram_tensor(name, shape, f32, kind="Internal").ap()

        agg1 = [dram(f"agg1_{k}", [TABLE_ROWS, C]) for k in range(CHAINS)]
        agg2 = [dram(f"agg2_{k}", [TABLE_ROWS, W2]) for k in range(CHAINS)]
        h1_dram = dram("h1_table", [ROWS + SPAN, C])
        y_dram = dram("y_table", [ROWS, C])

        def quad_rows(table, q, width):
            return table[0:ROWS, :].rearrange("(q p t) c -> q p (t c)", p=P, t=QT)[q, :, :]

        def tiles_of(table, q, width):
            return table[0:ROWS, :].rearrange("(q t p) c -> q p t c", p=P, t=QT)[q, :, :, :]

        ident = sb("ident", [P, P])
        lower = sb("lower", [P, P])
        cols = sb("cols", [P, 16])
        negc, dump, bf1, bm1 = (cols[:, k:k + 1] for k in range(4))
        wlin = sb("wlin", [P, C])
        wf1 = sb("wf1", [P, C])
        wf2 = sb("wf2", [P, C])
        wm1 = sb("wm1", [P, C])
        wm2 = sb("wm2", [P, C])
        wself = sb("wself", [P, C])
        wneigh = sb("wneigh", [P, C])
        bf2 = sb("bf2", [P, C])
        bm2 = sb("bm2", [P, C])
        bself = sb("bself", [P, C])
        bneigh = sb("bneigh", [P, C])
        weights = [(ident, "ident"), (lower, "lower"), (cols, "cols"), (wlin, "wlin"), (wf1, "wf1"), (wf2, "wf2"),
                   (wm1, "wm1"), (wm2, "wm2"), (wself, "wself"), (wneigh, "wneigh")]
        rows = [(bf2, "bf2"), (bm2, "bm2"), (bself, "bself"), (bneigh, "bneigh")]
        weights_loaded = sem("weights_loaded")

        zeros = sb("zeros", [P, 4096])
        zeros_set = sem("zeros_set")
        tables_zeroed = sem("tables_zeroed")
        pool_passed, dve_passed, sp_passed = sem("pool_passed"), sem("dve_passed"), sem("sp_passed")

        ew = sb("ew", [P, 2, QROWS])
        basis = sb("basis", [P, 2, QROWS])
        idx = sb("idx", [P, 2, 2, QT], i32)
        idxf = sb("idxf", [P, 2, QT])
        key_rows = sb("key_rows", [P, 2, QROWS], i32)
        same = sb("same", [P, 2, QT, P])
        junk = sb("junk", [P, QT, P])
        before = sb("before", [P, 2, QT])
        spare = sb("spare", [P, 2, QT])
        target = sb("target", [P, 2, QT], i32)
        counts = sb("counts", [P, 2, QT])
        xg = sb("xg", [P, 2, QT, C])
        stats = sb("stats", [P, QT, 6])
        mv = sb("mv", [P, QT, 2])
        ve = sb("ve", [P, QT])
        lnv = sb("lnv", [P, QT])
        r0 = sb("r0", [P, QT])
        r1 = sb("r1", [P, QT])
        r2 = sb("r2", [P, QT])
        r3 = sb("r3", [P, QT])
        rstd = sb("rstd", [P, QT])
        xn = sb("xn", [P, QT, C])
        hT = sb("hT", [P, QROWS])
        aT = sb("aT", [P, QROWS])
        absu = sb("absu", [P, QROWS])
        posu = sb("posu", [P, QROWS])
        eu = sb("eu", [P, QROWS])
        lu = sb("lu", [P, QROWS])
        su = sb("su", [P, QROWS])
        efb = sb("efb", [P, QROWS])
        msg = sb("msg", [P, QROWS])
        comb = sb("comb", [P, 2, QT, W2])
        comb1 = sb("comb1", [P, 2, QT, C])
        nagg = [sb(f"nagg{k}", [P, 2, QT, W2]) for k in range(CHAINS)]
        nx = sb("nx", [P, 2, QT, C])
        x1 = sb("x1", [P, 2, QT, C])
        h1s = sb("h1s", [P, 2, QT, C])
        ys = sb("ys", [P, 2, QT, C])
        rc = sb("rc", [P, 2, QT])
        cm = sb("cm", [P, 2, QT])

        bank = [ctx.enter_context(nc.psum_tensor(f"bank{k}", [P, 512], f32)) for k in range(8)]

        phase = [sem(f"phase{k}_done") for k in range(5)]

        msg_dram = dram("msg_table", [ROWS + SPAN, MW])
        off_dram = nc.dram_tensor("block_starts", [HI * LO], i32, kind="Internal").ap()
        consts = sb("consts", [P, 4 * P])
        iota, ones, eye32, upper32 = consts[:, 0:P], consts[:, P:2 * P], consts[:, 2 * P:2 * P + 32], consts[:, 2 * P + 32:2 * P + 64]
        upper_hi = consts[:, 2 * P + 64:2 * P + 96]
        last_start = consts[:, 2 * P + 96:2 * P + 128]
        third, quarter = consts[:, 3 * P:3 * P + 3], consts[:, 3 * P + 3:3 * P + 7]
        qbase = sb("qbase", [P, QUADS])
        firsts = sb("firsts", [P, TILES])
        first_row = sb("first_row", [1, TILES], i32)
        start_row = sb("start_row", [1, HI * LO], i32)
        flag = sb("flag", [1, 1], i32)
        bias3 = sb("bias3", [P, 3, QROWS], bf16)
        ones3 = sb("ones3", [P, P], bf16)
        weights += [(consts, "consts"), (qbase, "qbase")]
        bf1_top, bf1_low, bm1_top, bm1_low = (cols[:, k:k + 1] for k in (5, 6, 7, 8))
        top = cols[:, 9:10]
        srcs = sb("srcs", [P, 2, QT], i32)
        dsts = sb("dsts", [P, 2, QT], i32)
        msgw = sb("msgw", [P, 2, QT, MW])
        win = sb("win", [P, 2, QT, 2, MW])
        rel = sb("rel", [P, QT, 2])
        hot = sb("hot", [P, QT, 2, P])
        efs = sb("efs", [P, QROWS])
        clampu = sb("clampu", [P, QROWS])
        ln_out = sb("ln_out", [P, QROWS])
        aggs = sb("aggs", [P, 2, QROWS])
        nclamp = sb("nclamp", [P, QROWS])
        neu = sb("neu", [P, QROWS])
        nlu = sb("nlu", [P, QROWS])
        nsu = sb("nsu", [P, QROWS])
        nstats = sb("nstats", [P, QT, 6])
        nmv = sb("nmv", [P, QT, 2])
        nsmall = sb("nsmall", [P, 7, QT])
        nxn = sb("nxn", [P, QT, C])
        nhT = sb("nhT", [P, QROWS])

        def flat(t, par, width=C):
            return t[:, par, :, :].rearrange("p t c -> p (t c)")

        def agg_in(k, par):
            return nagg[k][:, par, :, :].rearrange("p t c -> p (t c)")[:, 0:QT * C]

        def s4(name):
            return ctx.enter_context(nc.semaphore("n2_" + name))
        n2_loaded = [s4(f"loaded{p}") for p in range(2)]
        n2_stored = [s4(f"stored{p}") for p in range(2)]
        n2_agg, capped, rc_ready, cm_ready = s4("agg_ready"), s4("capped"), s4("rc_ready"), s4("cm_ready")
        n2_yb, n2_out = s4("yb_ready"), s4("out_ready")
        def zero_parts(table, width, n_rows):
            flat_table = table.rearrange("r c -> (r c)")
            per = n_rows * width // P
            view = flat_table.rearrange("(p n) -> p n", p=P)
            for at in range(0, per, ZEROS):
                yield view[:, at:at + min(ZEROS, per - at)], min(ZEROS, per - at)

        with ExitStack() as sems:
            def s0(name):
                return ctx.enter_context(nc.semaphore("s0_" + name))

            cur = sems.enter_context(nc.sbuf_tensor("cur", [P, TILES], i32))
            nxt = sems.enter_context(nc.sbuf_tensor("nxt", [P, TILES], i32))
            ends = sems.enter_context(nc.sbuf_tensor("ends", [P, 2, TILES], i32))
            curf = sems.enter_context(nc.sbuf_tensor("curf", [P, TILES], f32))
            nxtf = sems.enter_context(nc.sbuf_tensor("nxtf", [P, TILES], f32))
            lastf = sems.enter_context(nc.sbuf_tensor("lastf", [P, TILES], f32))
            bad = sems.enter_context(nc.sbuf_tensor("bad", [P, TILES], f32))
            hi_lo = sems.enter_context(nc.sbuf_tensor("hi_lo", [P, 2, TILES], i32))
            hi_lof = sems.enter_context(nc.sbuf_tensor("hi_lof", [P, 2, TILES], f32))
            hot_hi = sems.enter_context(nc.sbuf_tensor("hot_hi", [P, TILES, HI], bf16))
            hot_lo = sems.enter_context(nc.sbuf_tensor("hot_lo", [P, TILES, LO], bf16))
            by4 = sems.enter_context(nc.sbuf_tensor("by4", [P, 4 * HI], f32))
            count_cols = sems.enter_context(nc.sbuf_tensor("count_cols", [P, 4, HI], f32))
            per_hi = sems.enter_context(nc.sbuf_tensor("per_hi", [P, LO], f32))
            too_many = sems.enter_context(nc.sbuf_tensor("too_many", [HI, 2, LO], f32))
            starts = sems.enter_context(nc.sbuf_tensor("starts", [HI, LO], i32))
            violations = sems.enter_context(nc.sbuf_tensor("violations", [P, 4], f32))
            violated = sems.enter_context(nc.sbuf_tensor("violated", [P, 1], f32))
            part = sems.enter_context(nc.sbuf_tensor("part", [P, 9, C], f32))
            partb = sems.enter_context(nc.sbuf_tensor("partb", [P, 9, C], bf16))
            dst_loaded, hots_ready, counted4, by4_ready = s0("dst_loaded"), s0("hots_ready"), s0("counted4"), s0("by4_ready")
            sums_ready, per_hi_ready, starts_summed, starts_ready = s0("sums_ready"), s0("per_hi_ready"), s0("starts_summed"), s0("starts_ready")
            violated_ready, total_ready, flag_ready = s0("violated_ready"), s0("total_ready"), s0("flag_ready")
            starts_out, starts_in, pads_set, chain = s0("starts_out"), s0("starts_in"), s0("pads_set"), s0("chain")
            block = sems.enter_context(nc.Block())

            @block.sync
            def _(sp):
                for t, a in ((cur[:], ins["dst_flat"][0:ROWS].rearrange("(p t) -> p t", p=P)),
                             (nxt[:], ins["dst_flat"][1:ROWS + 1].rearrange("(p t) -> p t", p=P)),
                             (ends[:, 0, :], ins["tile_first"].partition_broadcast(P)),
                             (ends[:, 1, :], ins["tile_last"].partition_broadcast(P)),
                             (first_row[0:1, :], ins["tile_first"].unsqueeze(0))):
                    sp.dma_start(t, a).then_inc(dst_loaded, 16)
                for t, name in weights:
                    sp.dma_start(t[:], ins[name]).then_inc(weights_loaded, 16)
                for t, name in rows:
                    sp.dma_start(t[:], ins[name].partition_broadcast(P)).then_inc(weights_loaded, 16)
                sp.wait_ge(zeros_set, 1)
                sp.dma_start(msg_dram[ROWS:ROWS + SPAN, :].rearrange("(p w) c -> p (w c)", p=P), zeros[:, 0:2 * MW]).then_inc(pads_set, 16)
                sp.dma_start(h1_dram[ROWS:ROWS + SPAN, :].rearrange("(p w) c -> p (w c)", p=P), zeros[:, 0:2 * C]).then_inc(pads_set, 16)
                sp.wait_ge(starts_ready, 1)
                sp.dma_start(off_dram.rearrange("(h l) -> h l", h=HI), starts[:]).then_inc(starts_out, 16)
                sp.wait_ge(starts_out, 16)
                sp.dma_start(start_row[0:1, :], off_dram.unsqueeze(0)).then_inc(starts_in, 16)
                sp.wait_ge(starts_in, 16)
                sp.wait_ge(pads_set, 32)
                sp.wait_ge(weights_loaded, 16 * (len(weights) + len(rows)))

            @block.scalar
            def _(act):
                act.wait_ge(zeros_set, 1)
                for table in agg2:
                    for out, m in zero_parts(table, W2, TABLE_ROWS):
                        act.dma_start(out, zeros[:, 0:m]).then_inc(tables_zeroed, 16)

            @block.vector
            def _(dve):
                done = [0]

                def link(ins_):
                    done[0] += 1
                    ins_.then_inc(chain, 1)
                    dve.wait_ge(chain, done[0])

                nc.vector.memset(zeros[:], 0.0).then_inc(zeros_set, 1)
                nc.vector.memset(ones3[:], 1.0)
                nc.vector.memset(per_hi[:], 0.0)
                link(nc.vector.memset(violations[:], 0.0))
                dve.wait_ge(dst_loaded, 16 * 5)
                nc.vector.tensor_copy(curf[:], cur[:])
                nc.vector.tensor_copy(nxtf[:], nxt[:])
                nc.vector.tensor_copy(firsts[:], ends[:, 0, :])
                nc.vector.tensor_copy(lastf[:], ends[:, 1, :])
                nc.vector.tensor_scalar(hi_lo[:, 0, :], cur[:], 12, None, ALU.logical_shift_right)
                link(nc.vector.tensor_scalar(hi_lo[:, 1, :], cur[:], 7, LO - 1, ALU.logical_shift_right, ALU.bitwise_and))
                link(nc.vector.tensor_copy(hi_lof[:], hi_lo[:]))
                dve.wait_ge(weights_loaded, 16 * (len(weights) + len(rows)))
                nc.vector.tensor_tensor(hot_hi[:], iota[:, 0:HI].unsqueeze(1).broadcast_to([P, TILES, HI]),
                                        hi_lof[:, 0, :].unsqueeze(2).broadcast_to([P, TILES, HI]), ALU.is_equal)
                nc.vector.tensor_tensor(hot_lo[:], iota[:, 0:LO].unsqueeze(1).broadcast_to([P, TILES, LO]),
                                        hi_lof[:, 1, :].unsqueeze(2).broadcast_to([P, TILES, LO]), ALU.is_equal).then_inc(hots_ready, 1)
                link(nc.vector.tensor_tensor(bad[:], curf[:], nxtf[:], ALU.is_gt))
                link(nc.vector.tensor_reduce(out=violations[:, 0:1], in_=bad[:], axis=AX.X, op=ALU.add))
                link(nc.vector.tensor_tensor(bad[:], lastf[:], firsts[:], ALU.subtract))
                link(nc.vector.tensor_scalar(curf[:], bad[:], float(SPAN - 1), None, ALU.is_gt))
                link(nc.vector.tensor_reduce(out=violations[:, 1:2], in_=curf[:], axis=AX.X, op=ALU.add))
                for k, b in enumerate((bf2, bm2, bself)):
                    link(nc.vector.tensor_copy(partb[:, 3 * k, :], b[:]))
                    link(nc.vector.tensor_copy(part[:, 3 * k, :], partb[:, 3 * k, :]))
                    link(nc.vector.tensor_tensor(part[:, 3 * k + 1, :], b[:], part[:, 3 * k, :], ALU.subtract))
                    link(nc.vector.tensor_copy(partb[:, 3 * k + 1, :], part[:, 3 * k + 1, :]))
                    link(nc.vector.tensor_copy(part[:, 3 * k + 2, :], partb[:, 3 * k + 1, :]))
                    link(nc.vector.tensor_tensor(part[:, 3 * k + 2, :], part[:, 3 * k + 1, :], part[:, 3 * k + 2, :], ALU.subtract))
                    link(nc.vector.tensor_copy(part[:, 3 * k + 1, :], partb[:, 3 * k + 1, :]))
                    link(nc.vector.tensor_scalar(part[:, 3 * k, :], part[:, 3 * k, :], third[:, 0:1], None, ALU.mult))
                    link(nc.vector.scalar_tensor_tensor(out=part[:, 3 * k, :], in0=part[:, 3 * k + 1, :], scalar=third[:, 1:2],
                                                        in1=part[:, 3 * k, :], op0=ALU.mult, op1=ALU.add))
                    link(nc.vector.scalar_tensor_tensor(out=part[:, 3 * k, :], in0=part[:, 3 * k + 2, :], scalar=third[:, 2:3],
                                                        in1=part[:, 3 * k, :], op0=ALU.mult, op1=ALU.add))
                    nc.vector.tensor_copy(bias3[:, k, :].rearrange("p (t c) -> p t c", t=QT), part[:, 3 * k, :].unsqueeze(1).broadcast_to([P, QT, C]))
                for k, b in enumerate((bf1, bm1)):
                    nc.vector.tensor_scalar(cols[:, 5 + 2 * k:6 + 2 * k], b, -1.0, TOP, ALU.mult, ALU.add)
                    link(nc.vector.tensor_scalar(cols[:, 6 + 2 * k:7 + 2 * k], b, -LOG2, None, ALU.add))
                dve.wait_ge(counted4, 1)
                link(nc.vector.tensor_copy(by4[:], bank[0][:, 0:4 * HI]))
                link(nc.vector.tensor_scalar(count_cols[:, 0, :], by4[:, 0:HI], quarter[:, 0:1], None, ALU.mult))
                for a in range(1, 4):
                    last = nc.vector.scalar_tensor_tensor(out=count_cols[:, a, :], in0=by4[:, a * HI:(a + 1) * HI], scalar=quarter[:, a:a + 1],
                                                          in1=count_cols[:, a - 1, :], op0=ALU.mult, op1=ALU.add)
                    if a < 3:
                        link(last)
                last.then_inc(by4_ready, 1)
                dve.wait_ge(sums_ready, 1)
                nc.vector.tensor_copy(per_hi[0:HI, :], bank[1][0:HI, 0:LO]).then_inc(per_hi_ready, 1)
                link(nc.vector.tensor_scalar(too_many[:, 0, :], bank[2][0:HI, 0:LO], float(SPAN), None, ALU.is_gt))
                link(nc.vector.tensor_reduce(out=violations[0:HI, 2:3], in_=too_many[:, 0, :], axis=AX.X, op=ALU.add))
                dve.wait_ge(starts_summed, 1)
                nc.vector.tensor_copy(starts[:], bank[3][0:HI, 0:LO]).then_inc(starts_ready, 1)
                link(nc.vector.tensor_tensor(too_many[:, 1, :], bank[3][0:HI, 0:LO], last_start[0:HI, :], ALU.is_gt))
                link(nc.vector.tensor_reduce(out=violations[0:HI, 3:4], in_=too_many[:, 1, :], axis=AX.X, op=ALU.add))
                nc.vector.tensor_reduce(out=violated[:], in_=violations[:], axis=AX.X, op=ALU.add).then_inc(violated_ready, 1)
                dve.wait_ge(total_ready, 1)
                nc.vector.tensor_copy(flag[0:1, 0:1], bank[4][0:1, 0:1]).then_inc(flag_ready, 1)

            @block.tensor
            def _(pe):
                pe.wait_ge(hots_ready, 1)
                nc.tensor.matmul(bank[0][:, 0:4 * HI], hot_lo[:, 0:4, :].rearrange("p t l -> p (t l)"),
                                 hot_hi[:, 0:4, :].rearrange("p t h -> p (t h)"), start=True, stop=False)
                with pe.Fori(1, QUADS - 1) as i:
                    nc.tensor.matmul(bank[0][:, 0:4 * HI], hot_lo[:, bass.ds(4 * i, 4), :].rearrange("p t l -> p (t l)"),
                                     hot_hi[:, bass.ds(4 * i, 4), :].rearrange("p t h -> p (t h)"), start=False, stop=False)
                nc.tensor.matmul(bank[0][:, 0:4 * HI], hot_lo[:, TILES - 4:TILES, :].rearrange("p t l -> p (t l)"),
                                 hot_hi[:, TILES - 4:TILES, :].rearrange("p t h -> p (t h)"), start=False, stop=True).then_inc(counted4, 1)
                pe.wait_ge(by4_ready, 1)
                counts_by_block = count_cols[:, 3, :]
                nc.tensor.matmul(bank[1][0:HI, 0:LO], counts_by_block, ones[:, 0:LO], start=True, stop=True)
                nc.tensor.matmul(bank[2][0:HI, 0:LO], counts_by_block, eye32, start=True, stop=True).then_inc(sums_ready, 1)
                nc.tensor.matmul(bank[3][0:HI, 0:LO], counts_by_block, upper32, start=True, stop=False)
                pe.wait_ge(per_hi_ready, 1)
                nc.tensor.matmul(bank[3][0:HI, 0:LO], upper_hi[:, 0:HI], per_hi[:], start=False, stop=True).then_inc(starts_summed, 1)
                pe.wait_ge(violated_ready, 1)
                nc.tensor.matmul(bank[4][0:1, 0:1], violated[:], ones[:, 0:1], start=True, stop=True).then_inc(total_ready, 1)

        ZEROED = 16 * sum(1 for table in agg2 for _ in zero_parts(table, W2, TABLE_ROWS))

        unfit = nc.values_load(flag[0:1, 0:1], min_val=0, max_val=1 << 30, skip_runtime_bounds_check_because="a count of violations")
        with nc.If(unfit == 0):
            with ExitStack() as sems:
                def sa(name):
                    return sems.enter_context(nc.semaphore("a_" + name))

                src_loaded, dst_loaded = [sa(f"src_loaded{p}") for p in range(2)], [sa(f"dst_loaded{p}") for p in range(2)]
                gathered, ew_loaded = [sa(f"gathered{p}") for p in range(2)], sa("ew_loaded")
                win_loaded, x_loaded = [sa(f"win_loaded{p}") for p in range(2)], [sa(f"x_loaded{p}") for p in range(2)]
                msg_stored, node_stored = [sa(f"msg_stored{p}") for p in range(2)], [sa(f"node_stored{p}") for p in range(2)]
                squared, basis_ready = sa("squared"), sa("basis_ready")
                e_stats, e_aggr, e_cut, e_var, e_ln, e_r0 = sa("e_stats"), sa("e_aggr"), sa("e_cut"), sa("e_var"), sa("e_ln"), sa("e_r0")
                e_r1, e_r2, e_r3, e_rstd = sa("e_r1"), sa("e_r2"), sa("e_r3"), sa("e_rstd")
                e_turned, e_hT, e_proj = sa("e_turned"), sa("e_hT"), sa("e_proj")
                e_u, e_clamp, e_exp, e_softln, e_soft, e_filter, e_fsb = (sa("e_u"), sa("e_clamp"), sa("e_exp"), sa("e_softln"), sa("e_soft"),
                                                                         sa("e_filter"), sa("e_fsb"))
                e_dst, e_msg = sa("e_dst"), sa("e_msg")
                n_rel, n_hot, n_agg, n_aggsb = sa("n_rel"), sa("n_hot"), sa("n_agg"), sa("n_aggsb")
                n_u, n_clamp, n_exp, n_softln, n_soft, n_mlp, n_x1 = (sa("n_u"), sa("n_clamp"), sa("n_exp"), sa("n_softln"), sa("n_soft"),
                                                                      sa("n_mlp"), sa("n_x1"))
                n_stats, n_aggr, n_var, n_ln, n_r0 = sa("n_stats"), sa("n_aggr"), sa("n_var"), sa("n_ln"), sa("n_r0")
                n_r1, n_r2, n_r3, n_rstd, n_norm = sa("n_r1"), sa("n_r2"), sa("n_r3"), sa("n_rstd"), sa("n_norm")
                n_turned, n_hT, n_self, n_y, n_h1 = sa("n_turned"), sa("n_hT"), sa("n_self"), sa("n_y"), sa("n_h1")
                u_ps, turn_ps, proj_ps, filt_ps, agg_ps, nu_ps, mlp_ps, self_ps = bank
                nve, nlnv, nr0, nr1, nr2, nr3, nrstd = (nsmall[:, k, :] for k in range(7))
                xcut, x2 = xn, x1
                block = sems.enter_context(nc.Block())

                @block.sync
                def _(sp):
                    def load_src(q, par):
                        if not at_first(q, 2):
                            sp.wait_ge(gathered[par], half_count(q, par, 64) - 64)
                            hold(sp, sp_passed)
                        sp.dma_start(srcs[:, par, :], ins["src_cols"][q, :, :]).then_inc(src_loaded[par], 16)

                    def load_dst(q, par):
                        if not at_first(q, 2):
                            sp.wait_ge(e_dst, q - 1)
                            hold(sp, sp_passed)
                        sp.dma_start(dsts[:, par, :], ins["dst_cols"][q, :, :]).then_inc(dst_loaded[par], 16)

                    def load_ew(q):
                        if not at_first(q, 2):
                            sp.wait_ge(squared, q // 2 if isinstance(q, int) else pair_of[0])
                            hold(sp, sp_passed)
                        for half in range(2):
                            sp.dma_start(ew[64 * half:64 * half + 64, 0, :], ins["ew_rows"][q + half, :].partition_broadcast(64)).then_inc(ew_loaded, 16)

                    def load_windows(j, par):
                        for p in range(2):
                            up_to = j + AHEAD if p == par else j + AHEAD - 1
                            if isinstance(up_to, int):
                                up_to = min(up_to, QUADS - 2 + p)
                            sp.wait_ge(msg_stored[p], half_count(up_to, p, 16))
                            hold(sp, sp_passed)
                        if not at_first(j, 2):
                            sp.wait_ge(n_agg, j - 1)
                            hold(sp, sp_passed)
                        for k in range(QT):
                            start = sp.value_load(start_row[0:1, bass.ds(4 * j + k, 1)], min_val=0, max_val=ROWS)
                            sp.dma_start(win[:, par, k, :, :], msg_dram[bass.ds(start, SPAN), :].rearrange("(w p) c -> p w c", p=P)).then_inc(win_loaded[par], 16)

                    def load_x(j, par):
                        if not at_first(j, 2):
                            sp.wait_ge(n_x1, j - 1)
                            hold(sp, sp_passed)
                        sp.dma_start(nx[:, par, :, :], tiles_of(ins["x"], j, C)).then_inc(x_loaded[par], 16)

                    def store_msg(q, par):
                        sp.wait_ge(e_msg, q + 1)
                        hold(sp, sp_passed)
                        sp.dma_start(tiles_of(msg_dram, q, MW), msgw[:, par, :, :]).then_inc(msg_stored[par], 16)

                    def store_node(j, par):
                        sp.wait_ge(n_h1, j + 1)
                        hold(sp, sp_passed)
                        sp.dma_start(tiles_of(h1_dram, j, C), h1s[:, par, :, :]).then_inc(node_stored[par], 16)
                        sp.wait_ge(n_y, j + 1)
                        hold(sp, sp_passed)
                        sp.dma_start(tiles_of(y_dram, j, C), ys[:, par, :, :]).then_inc(node_stored[par], 16)

                    pair_of = [None]
                    load_src(0, 0)
                    load_src(1, 1)
                    load_ew(0)

                    def step(s, par):
                        if there(s + 3):
                            load_src(s + 3, 1 - par)
                        if there(s + 1):
                            load_dst(s + 1, 1 - par)
                        if par == 0 and there(s + 2):
                            load_ew(s + 2)
                        if there(s - 3):
                            load_windows(s - 3, 1 - par)
                        if there(s - 4):
                            load_x(s - 4, par)
                        if there(s):
                            store_msg(s, par)
                        if there(s - 6):
                            store_node(s - 6, par)
                    over_steps(sp, step, pair_of)
                    for p in range(2):
                        sp.wait_ge(node_stored[p], 32 * (QUADS // 2))

                @block.gpsimd
                def _(pool):
                    def gather(q, par):
                        pool.wait_ge(src_loaded[par], half_count(q, par, 16))
                        if not at_first(q, 2):
                            pool.wait_ge(e_cut, q - 1)
                            hold(pool, pool_passed)
                        for t in range(QT):
                            hold(pool, pool_passed)
                            nc.gpsimd.indirect_dma_start(
                                out=xg[:, par, t, :], out_offset=None, in_=ins["x"],
                                in_offset=bass.IndirectOffsetOnAxis(ap=srcs[:, par, t:t + 1], axis=0)).then_inc(gathered[par], 16)

                    gather(0, 0)

                    def step(s, par):
                        if there(s + 2):
                            gather(s + 2, par)
                        if there(s - 6):
                            j = s - 6
                            pool.wait_ge(n_norm, j + 1)
                            if not at_first(j, 2):
                                pool.wait_ge(node_stored[par], half_count(j, par, 32) - 32)
                            hold(pool, pool_passed)
                            nc.gpsimd.tensor_scalar(flat(h1s, par), nxn[:].rearrange("p t c -> p (t c)"), 0.0, None, ALU.max).then_inc(n_h1, 1)
                    over_steps(pool, step)

                @block.vector
                def _(dve):
                    def moments(source, stats_, mv_, s_sem, a_sem, q):
                        for t in range(QT):
                            last = nc.vector.bn_stats(out=stats_[:, t, :], in_=source[:, t, :])
                        last.then_inc(s_sem, 1)
                        dve.wait_ge(s_sem, q + 1)
                        hold(dve, dve_passed)
                        for t in range(QT):
                            last = nc.vector.bn_aggr(out=mv_[:, t, :], in_=stats_[:, t, :])
                        last.then_inc(a_sem, 1)
                        dve.wait_ge(a_sem, q + 1)

                    def edge_norm(q, par):
                        dve.wait_ge(gathered[par], half_count(q, par, 64))
                        moments(xg[:, par, :, :], stats, mv, e_stats, e_aggr, q)
                        nc.vector.tensor_scalar(ve[:], mv[:, :, 1], LN_EPS, None, ALU.add).then_inc(e_var, 1)
                        wait_used(dve, e_turned, q, 1)
                        for t in range(QT):
                            last = nc.vector.tensor_scalar(xcut[:, t, :], xg[:, par, t, :], mv[:, t, 0:1], 0.0, ALU.subtract, ALU.max)
                        last.then_inc(e_cut, 1)

                    def newton(q, v, y0, t1, t2, t3, out, has_y0, d1, d2, d3, d4):
                        dve.wait_ge(has_y0, q + 1)
                        nc.vector.tensor_tensor(t1, y0, y0, ALU.mult).then_inc(d1, 1)
                        dve.wait_ge(d1, q + 1)
                        nc.vector.tensor_tensor(t2, t1, v, ALU.mult).then_inc(d2, 1)
                        dve.wait_ge(d2, q + 1)
                        nc.vector.tensor_scalar(t3, t2, -0.5, 1.5, ALU.mult, ALU.add).then_inc(d3, 1)
                        dve.wait_ge(d3, q + 1)
                        nc.vector.tensor_tensor(out, t3, y0, ALU.mult).then_inc(d4, 1)

                    def message(q, par):
                        if not at_first(q, 2):
                            dve.wait_ge(msg_stored[par], half_count(q, par, 16) - 16)
                        dve.wait_ge(dst_loaded[par], half_count(q, par, 16))
                        nc.vector.tensor_copy(msgw[:, par, :, C], dsts[:, par, :]).then_inc(e_dst, 1)
                        dve.wait_ge(e_rstd, q + 1)
                        dve.wait_ge(e_proj, q + 1)
                        dve.wait_ge(e_fsb, q + 1)
                        for t in range(QT):
                            last = nc.vector.scalar_tensor_tensor(out=msgw[:, par, t, 0:C], in0=proj_ps[:, t * C:(t + 1) * C], scalar=rstd[:, t:t + 1],
                                                                  in1=efs[:, t * C:(t + 1) * C], op0=ALU.mult, op1=ALU.mult)
                        last.then_inc(e_msg, 1)

                    def soften(q, ups, low, l, out, has_l, used, done):
                        dve.wait_ge(has_l, q + 1)
                        wait_used(dve, used, q, 1)
                        nc.vector.scalar_tensor_tensor(out=out, in0=ups, scalar=low, in1=l, op0=ALU.add, op1=ALU.max).then_inc(done, 1)

                    def one_hots(j, par):
                        dve.wait_ge(win_loaded[par], half_count(j, par, 64))
                        nc.vector.tensor_scalar(rel[:], win[:, par, :, :, C], qbase[:, bass.ds(j, 1)], None, ALU.subtract).then_inc(n_rel, 1)
                        dve.wait_ge(n_rel, j + 1)
                        wait_used(dve, n_agg, j, 1)
                        for k in range(QT):
                            for w in range(2):
                                last = nc.vector.tensor_scalar(hot[:, k, w, :], iota, float(P * k), rel[:, k, w:w + 1], ALU.add, ALU.is_equal)
                        last.then_inc(n_hot, 1)

                    def residual(j, par):
                        dve.wait_ge(x_loaded[par], half_count(j, par, 16))
                        dve.wait_ge(n_mlp, j + 1)
                        wait_used(dve, n_y, j, 2)
                        nc.vector.tensor_tensor(flat(x2, par), mlp_ps[:], flat(nx, par), ALU.add).then_inc(n_x1, 1)

                    def node_moments(j, par):
                        dve.wait_ge(n_x1, j + 1)
                        moments(x2[:, par, :, :], nstats, nmv, n_stats, n_aggr, j)
                        nc.vector.tensor_scalar(nve, nmv[:, :, 1], LN_EPS, None, ALU.add).then_inc(n_var, 1)

                    def node_norm(j, par):
                        newton(j, nve, nr0, nr1, nr2, nr3, nrstd, n_r0, n_r1, n_r2, n_r3, n_rstd)
                        dve.wait_ge(n_rstd, j + 1)
                        wait_used(dve, n_turned, j, 1)
                        wait_used(dve, n_h1, j, 1)
                        for t in range(QT):
                            last = nc.vector.tensor_scalar(nxn[:, t, :], x2[:, par, t, :], nmv[:, t, 0:1], nrstd[:, t:t + 1], ALU.subtract, ALU.mult)
                        last.then_inc(n_norm, 1)

                    def node_out(j, par):
                        if not at_first(j, 2):
                            dve.wait_ge(node_stored[par], half_count(j, par, 32) - 32)
                        dve.wait_ge(n_self, j + 1)
                        nc.vector.tensor_tensor(flat(ys, par), self_ps[:], flat(x2, par), ALU.add).then_inc(n_y, 1)

                    def step(s, par):
                        if there(s):
                            message(s, par)
                        if there(s - 6):
                            node_moments(s - 6, par)
                        if there(s + 1):
                            edge_norm(s + 1, 1 - par)
                        if there(s - 6):
                            node_norm(s - 6, par)
                        if there(s + 1):
                            soften(s + 1, u_ps[:], bf1_low, ln_out[:], su[:], e_softln, e_filter, e_soft)
                        if there(s - 5):
                            soften(s - 5, nu_ps[:], bm1_low, nlu[:], nsu[:], n_softln, n_mlp, n_soft)
                        if there(s - 4):
                            one_hots(s - 4, par)
                        if there(s + 1):
                            newton(s + 1, ve[:], r0[:], r1[:], r2[:], r3[:], rstd[:], e_r0, e_r1, e_r2, e_r3, e_rstd)
                        if there(s - 6):
                            node_out(s - 6, par)
                        if there(s - 5):
                            residual(s - 5, 1 - par)
                    over_steps(dve, step)

                @block.scalar
                def _(act):
                    coef = 1.0 / (2.0 * float(CENTERS[1] - CENTERS[0]) ** 2)
                    half = cols[:, 4:5]

                    def make_basis(j):
                        act.wait_ge(ew_loaded, 32 * j + 32)
                        if not at_first(j, 1):
                            act.wait_ge(e_u, 2 * j)
                        nc.scalar.activation(basis[:, 1, :], ew[:, 0, :], ACT.Square, bias=negc).then_inc(squared, 1)
                        act.wait_ge(squared, j + 1)
                        nc.scalar.activation(basis[:, 0, :], basis[:, 1, :], ACT.Exp, scale=-coef).then_inc(basis_ready, 1)

                    def softplus(q, ups, high, c, e, l, has_u, soft, clamped, d_exp, d_ln):
                        act.wait_ge(has_u, q + 1)
                        nc.scalar.activation(c, ups, ACT.Relu, bias=high, scale=-1.0).then_inc(clamped, 1)
                        act.wait_ge(clamped, q + 1)
                        nc.scalar.activation(e, c, ACT.Exp, bias=top, scale=-1.0).then_inc(d_exp, 1)
                        act.wait_ge(d_exp, q + 1)
                        wait_used(act, soft, q, 1)
                        nc.scalar.activation(l, e, ACT.Ln, bias=half, scale=0.5).then_inc(d_ln, 1)

                    def inverse_root(q, v, l, y0, has_v, d_ln, used, done):
                        act.wait_ge(has_v, q + 1)
                        nc.scalar.activation(l, v, ACT.Ln).then_inc(d_ln, 1)
                        act.wait_ge(d_ln, q + 1)
                        wait_used(act, used, q, 1)
                        nc.scalar.activation(y0, l, ACT.Exp, scale=-0.5).then_inc(done, 1)

                    def evacuate(q, out, ps, func, ready, used, done):
                        act.wait_ge(ready, q + 1)
                        wait_used(act, used, q, 1)
                        nc.scalar.activation(out, ps, func).then_inc(done, 1)

                    nc.scalar.preload_act_table_set("natural_log_exp_and_others")
                    make_basis(0)
                    pair_of = [None]

                    def step(s, par):
                        if there(s + 1):
                            softplus(s + 1, u_ps[:], bf1_top, clampu[:], eu[:], ln_out[:], e_u, e_soft, e_clamp, e_exp, e_softln)
                        if there(s - 6):
                            inverse_root(s - 6, nve, nlnv, nr0, n_var, n_ln, n_rstd, n_r0)
                        if there(s - 5):
                            softplus(s - 5, nu_ps[:], bm1_top, nclamp[:], neu[:], nlu[:], n_u, n_soft, n_clamp, n_exp, n_softln)
                        if there(s + 1):
                            evacuate(s + 1, hT[:], turn_ps[:], ACT.Copy, e_turned, e_proj, e_hT)
                            inverse_root(s + 1, ve[:], lnv[:], r0[:], e_var, e_ln, e_rstd, e_r0)
                        if there(s - 6):
                            evacuate(s - 6, nhT[:], turn_ps[:], ACT.Relu, n_turned, n_self, n_hT)
                        if there(s + 1):
                            evacuate(s + 1, efs[:], filt_ps[:], ACT.Copy, e_filter, e_msg, e_fsb)
                        if there(s - 4):
                            evacuate(s - 4, aggs[:, 0, :], agg_ps[:], ACT.Copy, n_agg, n_u, n_aggsb)
                        if par == 0 and there(s + 2):
                            make_basis((s + 2) // 2 if isinstance(s, int) else pair_of[0])
                    over_steps(act, step, pair_of)

                @block.tensor
                def _(pe):
                    def filter_up(q, par):
                        pe.wait_ge(basis_ready, q // 2 + 1 if isinstance(q, int) else pair_of[0] + (1 - par))
                        wait_used(pe, e_soft, q, 1)
                        at = BASIS_AT[par]
                        nc.tensor.matmul(u_ps[:], wf1[at:at + BASIS, :], basis[at:at + BASIS, 0, :], start=True, stop=True).then_inc(e_u, 1)

                    def product(ps, left, weights_, b, done):
                        if b is not None:
                            nc.tensor.matmul(ps[:], ones3[0:3, :], bias3[0:3, b, :], start=True, stop=False)
                        for t in range(QT):
                            last = nc.tensor.matmul(ps[:, t * P:(t + 1) * P], left[:, t * P:(t + 1) * P], weights_[:],
                                                    start=(b is None), stop=(b is None or t == QT - 1))
                        last.then_inc(done, 1)

                    def turn(source, done):
                        for t in range(QT):
                            last = nc.tensor.transpose(turn_ps[:, t * P:(t + 1) * P], source[:, t, :], ident[:])
                        last.then_inc(done, 1)

                    def block_sums(j, par):
                        pe.wait_ge(n_hot, j + 1)
                        pe.wait_ge(win_loaded[par], half_count(j, par, 64))
                        wait_used(pe, n_aggsb, j, 1)
                        for k in range(QT):
                            for w in range(2):
                                last = nc.tensor.matmul(agg_ps[:, k * P:(k + 1) * P], win[:, par, k, w, 0:C], hot[:, k, w, :],
                                                        start=(w == 0), stop=(w == 1))
                        last.then_inc(n_agg, 1)

                    pair_of = [None]

                    def step(s, par):
                        if there(s - 5):
                            pe.wait_ge(n_aggsb, s - 5 + 1)
                            wait_used(pe, n_soft, s - 5, 1)
                            nc.tensor.matmul(nu_ps[:], wm1[:], aggs[:, 0, :], start=True, stop=True).then_inc(n_u, 1)
                        if there(s + 1):
                            filter_up(s + 1, 1 - par)
                            pe.wait_ge(e_cut, s + 2)
                            if there(s - 7):
                                pe.wait_ge(n_hT, s - 7 + 1)
                            wait_used(pe, e_hT, s + 1, 1)
                            turn(xcut, e_turned)
                            pe.wait_ge(e_hT, s + 2)
                            wait_used(pe, e_msg, s + 1, 1)
                            product(proj_ps, hT, wlin, None, e_proj)
                        if there(s - 6):
                            pe.wait_ge(n_norm, s - 6 + 1)
                            wait_used(pe, n_hT, s - 6, 1)
                            turn(nxn, n_turned)
                        if there(s + 1):
                            pe.wait_ge(e_soft, s + 2)
                            wait_used(pe, e_fsb, s + 1, 1)
                            product(filt_ps, su, wf2, 0, e_filter)
                        if there(s - 6):
                            pe.wait_ge(n_hT, s - 6 + 1)
                            wait_used(pe, n_y, s - 6, 1)
                            product(self_ps, nhT, wself, 2, n_self)
                        if there(s - 4):
                            block_sums(s - 4, par)
                        if there(s - 5):
                            pe.wait_ge(n_soft, s - 5 + 1)
                            wait_used(pe, n_x1, s - 5, 1)
                            product(mlp_ps, nsu, wm2, 1, n_mlp)
                    over_steps(pe, step, pair_of)

            with ExitStack() as sems:
                def sbm(name):
                    return sems.enter_context(nc.semaphore("b_" + name))

                idx_loaded, keys_loaded, win_loaded = ([sbm(f"{n}{p}") for p in range(2)] for n in ("idx_loaded", "keys_loaded", "win_loaded"))
                added = [sbm(f"added{k}") for k in range(CHAINS)]
                keyf, dstf, same_ready, counted = sbm("keyf"), sbm("dstf"), sbm("same_ready"), sbm("counted")
                before_ready, spare_ready, target_ready = sbm("before_ready"), sbm("spare_ready"), sbm("target_ready")
                rel0, rel1, hot_ready, pick_ready, picksb = sbm("rel0"), sbm("rel1"), sbm("hot_ready"), sbm("pick_ready"), sbm("picksb")
                sumT_ready, sT_ready, neigh_ready, comb_ready = sbm("sumT_ready"), sbm("sT_ready"), sbm("neigh_ready"), sbm("comb_ready")
                pick_ps, sumT_ps, neigh_ps = (bank[0], bank[1]), bank[2], bank[3]
                sameb = sems.enter_context(nc.sbuf_tensor("sameb", [P, QT, P], bf16))
                hotb = sems.enter_context(nc.sbuf_tensor("hotb", [P, QT, 2, P], bf16))
                pick = sems.enter_context(nc.sbuf_tensor("pick", [P, 2, QT, P], f32))
                hwin = win[:, :, :, :, 0:C]
                dst_f = sems.enter_context(nc.sbuf_tensor("dst_f", [P, QT], f32))
                block = sems.enter_context(nc.Block())

                @block.sync
                def _(sp):
                    def load(q, par):
                        if not at_first(q, 2):
                            sp.wait_ge(dstf, q - 1)
                            hold(sp, sp_passed)
                        sp.dma_start(idx[:, par, :, :].rearrange("p a t -> p (a t)"), ins["edge_cols"][q, :, :]).then_inc(idx_loaded[par], 16)
                        if not at_first(q, 2):
                            sp.wait_ge(same_ready, q - 1)
                            hold(sp, sp_passed)
                        sp.dma_start(key_rows[:, par, :], ins["src_rows"][q, :].partition_broadcast(P)).then_inc(keys_loaded[par], 16)
                        if not at_first(q, 2):
                            sp.wait_ge(sumT_ready, q - 1)
                            hold(sp, sp_passed)
                        for t in range(QT):
                            first = sp.value_load(first_row[0:1, bass.ds(4 * q + t, 1)], min_val=0, max_val=ROWS - 1)
                            sp.dma_start(hwin[:, par, t, :, :], h1_dram[bass.ds(first, SPAN), :].rearrange("(w p) c -> p w c", p=P)).then_inc(win_loaded[par], 16)
                    over_quads(sp, load)

                @block.gpsimd
                def _(pool):
                    pool.wait_ge(tables_zeroed, ZEROED)

                    def step(q, par):
                        pool.wait_ge(comb_ready, q + 1)
                        pool.wait_ge(target_ready, q + 1)
                        pool.wait_ge(counted, q + 1)
                        for t in range(QT):
                            k = t % CHAINS
                            n = 32 * q + 16 * (t // CHAINS)
                            if not (isinstance(n, int) and n == 0):
                                pool.wait_ge(added[k], n)
                            hold(pool, pool_passed)
                            nc.gpsimd.indirect_dma_start(
                                out=agg2[k], out_offset=bass.IndirectOffsetOnAxis(ap=target[:, par, t:t + 1], axis=0),
                                in_=comb[:, par, t, :], in_offset=None, compute_op=ALU.add).then_inc(added[k], 16)
                    over_quads(pool, step)
                    for k in range(CHAINS):
                        pool.wait_ge(added[k], 32 * QUADS)

                @block.vector
                def _(dve):
                    for par in range(2):
                        nc.vector.memset(comb[:, par, :, C:W2], 0.0)

                    def step(q, par):
                        dve.wait_ge(idx_loaded[par], half_count(q, par, 16))
                        nc.vector.tensor_copy(idxf[:, par, :], idx[:, par, 0, :]).then_inc(keyf, 1)
                        nc.vector.tensor_copy(dst_f[:], idx[:, par, 1, :]).then_inc(dstf, 1)
                        dve.wait_ge(dstf, q + 1)
                        nc.vector.tensor_tensor(rel[:, :, 0], dst_f[:], firsts[:, bass.ds(4 * q, QT)], ALU.subtract).then_inc(rel0, 1)
                        dve.wait_ge(rel0, q + 1)
                        nc.vector.tensor_scalar(rel[:, :, 1], rel[:, :, 0], -float(P), None, ALU.add).then_inc(rel1, 1)
                        dve.wait_ge(keys_loaded[par], half_count(q, par, 16))
                        wait_used(dve, pick_ready, q, 1)
                        for t in range(QT):
                            last = nc.vector.tensor_scalar(sameb[:, t, :], key_rows[:, par, t * P:(t + 1) * P], idxf[:, par, t:t + 1], None, ALU.is_equal)
                        last.then_inc(same_ready, 1)
                        dve.wait_ge(rel1, q + 1)
                        for t in range(QT):
                            for w in range(2):
                                last = nc.vector.tensor_scalar(hotb[:, t, w, :], iota, rel[:, t, w:w + 1], None, ALU.is_equal)
                        last.then_inc(hot_ready, 1)
                        dve.wait_ge(same_ready, q + 1)
                        for t in range(QT):
                            last = nc.vector.tensor_tensor_reduce(out=junk[:, t, :], in0=sameb[:, t, :], in1=lower[:], scale=1.0,
                                                                  scalar=0.0, op0=ALU.mult, op1=ALU.add, accum_out=before[:, par, t:t + 1])
                        last.then_inc(before_ready, 1)
                        if not at_first(q, 2):
                            for k in range(CHAINS):
                                dve.wait_ge(added[k], 32 * (q - 1))
                        nc.vector.tensor_reduce(out=comb[:, par, :, C], in_=sameb[:], axis=AX.X, op=ALU.add).then_inc(counted, 1)
                        dve.wait_ge(before_ready, q + 1)
                        nc.vector.tensor_scalar(spare[:, par, :], before[:, par, :], 1.0, dump, ALU.min, ALU.mult).then_inc(spare_ready, 1)
                        dve.wait_ge(spare_ready, q + 1)
                        nc.vector.tensor_tensor(target[:, par, :], spare[:, par, :], idxf[:, par, :], ALU.max).then_inc(target_ready, 1)
                    over_quads(dve, step)

                @block.tensor
                def _(pe):
                    def front(q):
                        pe.wait_ge(hot_ready, q + 1)
                        wait_used(pe, picksb, q, 1)
                        for w in range(2):
                            for t in range(QT):
                                last = nc.tensor.matmul(pick_ps[w][:, t * P:(t + 1) * P], hotb[:, t, w, :], sameb[:, t, :], start=True, stop=True)
                        last.then_inc(pick_ready, 1)

                    front(0)

                    def step(q, par):
                        pe.wait_ge(win_loaded[par], half_count(q, par, 64))
                        pe.wait_ge(picksb, q + 1)
                        wait_used(pe, sT_ready, q, 1)
                        for t in range(QT):
                            for w in range(2):
                                last = nc.tensor.matmul(sumT_ps[:, t * P:(t + 1) * P], hwin[:, par, t, w, :], pick[:, w, t, :], start=(w == 0), stop=(w == 1))
                        last.then_inc(sumT_ready, 1)
                        if exists(q + 1):
                            front(q + 1)
                        pe.wait_ge(sT_ready, q + 1)
                        wait_used(pe, comb_ready, q, 1)
                        for t in range(QT):
                            last = nc.tensor.matmul(neigh_ps[:, t * P:(t + 1) * P], hT[:, t * P:(t + 1) * P], wneigh[:], start=True, stop=True)
                        last.then_inc(neigh_ready, 1)
                    over_quads(pe, step)

                @block.scalar
                def _(act):
                    def take_pick(q):
                        act.wait_ge(pick_ready, q + 1)
                        wait_used(act, sumT_ready, q, 1)
                        for w in range(2):
                            last = nc.scalar.activation(pick[:, w, :, :].rearrange("p t e -> p (t e)"), pick_ps[w][:], ACT.Copy)
                        last.then_inc(picksb, 1)

                    take_pick(0)

                    def step(q, par):
                        act.wait_ge(sumT_ready, q + 1)
                        wait_used(act, neigh_ready, q, 1)
                        nc.scalar.activation(hT[:], sumT_ps[:], ACT.Copy).then_inc(sT_ready, 1)
                        if exists(q + 1):
                            take_pick(q + 1)
                        act.wait_ge(neigh_ready, q + 1)
                        if not at_first(q, 2):
                            for k in range(CHAINS):
                                act.wait_ge(added[k], 32 * (q - 1))
                        nc.scalar.activation(comb[:, par, :, 0:C], neigh_ps[:].rearrange("p (t c) -> p t c", t=QT), ACT.Copy).then_inc(comb_ready, 1)
                    over_quads(act, step)


        with nc.Else():
            zeroed1 = sem("zeroed1")
            with nc.Block() as block:
                @block.sync
                def _(sp):
                    n = 0
                    for table in agg1:
                        for out, m in zero_parts(table, C, TABLE_ROWS):
                            sp.dma_start(out, zeros[:, 0:m]).then_inc(zeroed1, 16)
                            n += 16
                    sp.wait_ge(zeroed1, n)
                    sp.wait_ge(tables_zeroed, ZEROED)

            with ExitStack() as sems:
                def s1(name):
                    return sems.enter_context(nc.semaphore("e1_" + name))
                idx_loaded = [s1(f"idx_loaded{p}") for p in range(2)]
                keys_loaded = [s1(f"keys_loaded{p}") for p in range(2)]
                ew_loaded = s1("ew_loaded")
                gathered = [s1(f"gathered{p}") for p in range(2)]
                added = [s1(f"added{k}") for k in range(CHAINS)]
                squared, basis_ready = s1("squared"), s1("basis_ready")
                stats_ready, aggr_ready, var_ready = s1("stats_ready"), s1("aggr_ready"), s1("var_ready")
                ln_ready, r0_ready = s1("ln_ready"), s1("r0_ready")
                r1_ready, r2_ready, r3_ready, rstd_ready = s1("r1_ready"), s1("r2_ready"), s1("r3_ready"), s1("rstd_ready")
                xn_ready, xnT_ready, hT_ready, hs_ready = s1("xn_ready"), s1("xnT_ready"), s1("hT_ready"), s1("hs_ready")
                u_ready, absu_ready, posu_ready = s1("u_ready"), s1("absu_ready"), s1("posu_ready")
                eu_ready, lu_ready, su_ready, ef_ready = s1("eu_ready"), s1("lu_ready"), s1("su_ready"), s1("ef_ready")
                efb_ready, msg_ready, sum_ready, comb_ready = s1("efb_ready"), s1("msg_ready"), s1("sum_ready"), s1("comb_ready")
                idxf_ready, same_ready = s1("idxf_ready"), s1("same_ready")
                before_ready, spare_ready, target_ready = s1("before_ready"), s1("spare_ready"), s1("target_ready")
                u_ps, xT_ps, hs_ps, ef_ps, sum_ps = bank[0], bank[1], bank[2], bank[3], bank[4]

                block = sems.enter_context(nc.Block())

                @block.sync
                def _(sp):
                    def load(q, par):
                        if not (isinstance(q, int) and q < 2):
                            sp.wait_ge(gathered[par], 64 * ((q - par) // 2) if isinstance(q, int) else 32 * q - 32 * par)
                        hold(sp, sp_passed)
                        wait_used(sp, idxf_ready, q, 2)
                        hold(sp, sp_passed)
                        sp.dma_start(idx[:, par, :, :].rearrange("p a t -> p (a t)"), ins["edge_cols"][q, :, :]).then_inc(idx_loaded[par], 16)
                        wait_used(sp, same_ready, q, 2)
                        hold(sp, sp_passed)
                        sp.dma_start(key_rows[:, par, :], ins["dst_rows"][q, :].partition_broadcast(P)).then_inc(keys_loaded[par], 16)

                    def pair(j, n):
                        if not isinstance(j, int) or j >= 2:
                            sp.wait_ge(squared, j - 1)
                        hold(sp, sp_passed)
                        for half in range(2):
                            sp.dma_start(ew[64 * half:64 * half + 64, n, :],
                                         ins["ew_rows"][2 * j + half, :].partition_broadcast(64)).then_inc(ew_loaded, 16)
                    pair(0, 0)
                    load(0, 0)
                    load(1, 1)
                    with sp.Fori(0, QUADS // 2 - 1) as i:
                        sp.wait_ge(squared, i + 1)
                        hold(sp, sp_passed)
                        for half in range(2):
                            sp.dma_start(ew[64 * half:64 * half + 64, 0, :],
                                         ins["ew_rows"][2 * i + (2 + half), :].partition_broadcast(64)).then_inc(ew_loaded, 16)
                        for par in range(2):
                            q = 2 * i + (2 + par)
                            sp.wait_ge(gathered[par], 64 * i + 64)
                            hold(sp, sp_passed)
                            sp.wait_ge(idxf_ready, 2 * i + (par + 1))
                            hold(sp, sp_passed)
                            sp.dma_start(idx[:, par, :, :].rearrange("p a t -> p (a t)"), ins["edge_cols"][q, :, :]).then_inc(idx_loaded[par], 16)
                            sp.wait_ge(same_ready, 2 * i + (par + 1))
                            hold(sp, sp_passed)
                            sp.dma_start(key_rows[:, par, :], ins["dst_rows"][q, :].partition_broadcast(P)).then_inc(keys_loaded[par], 16)

                @block.gpsimd
                def _(pool):
                    def gather(q, par, t):
                        if t == 0:
                            pool.wait_ge(idx_loaded[par], half_count(q, par, 16))
                            wait_used(pool, xn_ready, q, 2)
                        hold(pool, pool_passed)
                        nc.gpsimd.indirect_dma_start(
                            out=xg[:, par, t, :], out_offset=None, in_=ins["x"],
                            in_offset=bass.IndirectOffsetOnAxis(ap=idx[:, par, 0, t:t + 1], axis=0)).then_inc(gathered[par], 16)

                    def add(q, par, t):
                        if t == 0:
                            pool.wait_ge(comb_ready, q + 1)
                            pool.wait_ge(target_ready, q + 1)
                        k = t % CHAINS
                        n = 32 * q + 16 * (t // CHAINS)
                        if not (isinstance(n, int) and n == 0):
                            pool.wait_ge(added[k], n)
                        hold(pool, pool_passed)
                        nc.gpsimd.indirect_dma_start(
                            out=agg1[k], out_offset=bass.IndirectOffsetOnAxis(ap=target[:, par, t:t + 1], axis=0),
                            in_=comb1[:, par, t, :], in_offset=None, compute_op=ALU.add).then_inc(added[k], 16)

                    for t in range(QT):
                        gather(0, 0, t)
                    for t in range(QT):
                        gather(1, 1, t)

                    def step(q, par):
                        for t in range(QT):
                            add(q, par, t)
                            if exists(q + 2):
                                gather(q + 2, par, t)
                    over_quads(pool, step)
                    for k in range(CHAINS):
                        pool.wait_ge(added[k], 32 * QUADS)

                @block.vector
                def _(dve):
                    def norm_stats(q, par):
                        dve.wait_ge(gathered[par], half_count(q, par, 64))
                        for t in range(QT):
                            last = nc.vector.bn_stats(out=stats[:, t, :], in_=xg[:, par, t, :])
                        last.then_inc(stats_ready, 1)
                        dve.wait_ge(stats_ready, q + 1)
                        hold(dve, dve_passed)
                        for t in range(QT):
                            last = nc.vector.bn_aggr(out=mv[:, t, :], in_=stats[:, t, :])
                        last.then_inc(aggr_ready, 1)
                        dve.wait_ge(aggr_ready, q + 1)
                        wait_used(dve, ln_ready, q, 1)
                        nc.vector.tensor_scalar(ve[:], mv[:, :, 1], LN_EPS, None, ALU.add).then_inc(var_ready, 1)

                    def normalise(q, par):
                        dve.wait_ge(r0_ready, q + 1)
                        nc.vector.tensor_tensor(r1[:], r0[:], r0[:], ALU.mult).then_inc(r1_ready, 1)
                        dve.wait_ge(r1_ready, q + 1)
                        nc.vector.tensor_tensor(r2[:], r1[:], ve[:], ALU.mult).then_inc(r2_ready, 1)
                        dve.wait_ge(r2_ready, q + 1)
                        nc.vector.tensor_scalar(r3[:], r2[:], -0.5, 1.5, ALU.mult, ALU.add).then_inc(r3_ready, 1)
                        dve.wait_ge(r3_ready, q + 1)
                        nc.vector.tensor_tensor(rstd[:], r3[:], r0[:], ALU.mult).then_inc(rstd_ready, 1)
                        dve.wait_ge(rstd_ready, q + 1)
                        wait_used(dve, xnT_ready, q, 1)
                        for t in range(QT):
                            last = nc.vector.tensor_scalar(xn[:, t, :], xg[:, par, t, :], mv[:, t, 0:1], rstd[:, t:t + 1],
                                                           ALU.subtract, ALU.mult)
                        last.then_inc(xn_ready, 1)

                    def keys(q, par):
                        dve.wait_ge(idx_loaded[par], half_count(q, par, 16))
                        nc.vector.tensor_copy(idxf[:, par, :], idx[:, par, 1, :]).then_inc(idxf_ready, 1)
                        dve.wait_ge(idxf_ready, q + 1)
                        dve.wait_ge(keys_loaded[par], half_count(q, par, 16))
                        wait_used(dve, sum_ready, q, 2)
                        for t in range(QT):
                            last = nc.vector.tensor_scalar(same[:, par, t, :], key_rows[:, par, t * P:(t + 1) * P],
                                                           idxf[:, par, t:t + 1], None, ALU.is_equal)
                        last.then_inc(same_ready, 1)
                        dve.wait_ge(same_ready, q + 1)
                        for t in range(QT):
                            last = nc.vector.tensor_tensor_reduce(out=junk[:, t, :], in0=same[:, par, t, :], in1=lower[:], scale=1.0,
                                                                  scalar=0.0, op0=ALU.mult, op1=ALU.add, accum_out=before[:, par, t:t + 1])
                        last.then_inc(before_ready, 1)
                        dve.wait_ge(before_ready, q + 1)
                        nc.vector.tensor_scalar(spare[:, par, :], before[:, par, :], 1.0, dump, ALU.min, ALU.mult).then_inc(spare_ready, 1)
                        dve.wait_ge(spare_ready, q + 1)
                        if not (isinstance(q, int) and q < 2):
                            for k in range(CHAINS):
                                dve.wait_ge(added[k], 32 * (q - 1))
                        nc.vector.tensor_tensor(target[:, par, :], spare[:, par, :], idxf[:, par, :], ALU.max).then_inc(target_ready, 1)

                    def filter_in(q, par):
                        dve.wait_ge(u_ready, q + 1)
                        wait_used(dve, su_ready, q, 1)
                        nc.vector.tensor_scalar(posu[:], u_ps[:], bf1, 0.0, ALU.add, ALU.max).then_inc(posu_ready, 1)

                    def filter_out(q, par):
                        dve.wait_ge(posu_ready, q + 1)
                        dve.wait_ge(lu_ready, q + 1)
                        wait_used(dve, ef_ready, q, 1)
                        nc.vector.tensor_tensor(su[:], posu[:], lu[:], ALU.add).then_inc(su_ready, 1)

                    def message(q, par):
                        dve.wait_ge(ef_ready, q + 1)
                        wait_used(dve, msg_ready, q, 1)
                        nc.vector.tensor_tensor(efb[:].rearrange("p (t c) -> p t c", t=QT), ef_ps[:].rearrange("p (t c) -> p t c", t=QT),
                                                bf2[:].unsqueeze(1).broadcast_to([P, QT, C]), ALU.add).then_inc(efb_ready, 1)
                        dve.wait_ge(efb_ready, q + 1)
                        dve.wait_ge(hs_ready, q + 1)
                        wait_used(dve, sum_ready, q, 1)
                        nc.vector.tensor_tensor(msg[:], hs_ps[:], efb[:], ALU.mult).then_inc(msg_ready, 1)

                    def stage_a(q, par):
                        norm_stats(q, par)
                        filter_in(q, par)
                        normalise(q, par)
                        filter_out(q, par)
                        keys(q, par)
                    stage_a(0, 0)

                    def step(q, par):
                        if exists(q + 1):
                            norm_stats(q + 1, 1 - par)
                        message(q, par)
                        if exists(q + 1):
                            normalise(q + 1, 1 - par)
                            filter_in(q + 1, 1 - par)
                            keys(q + 1, 1 - par)
                            filter_out(q + 1, 1 - par)
                    over_quads(dve, step)

                @block.scalar
                def _(act):
                    coef = 1.0 / (2.0 * float(CENTERS[1] - CENTERS[0]) ** 2)

                    def make_basis(j):
                        act.wait_ge(ew_loaded, 32 * j + 32)
                        if not (isinstance(j, int) and j < 1):
                            act.wait_ge(u_ready, 2 * j)
                        nc.scalar.activation(basis[:, 1, :], ew[:, 0, :], ACT.Square, bias=negc).then_inc(squared, 1)
                        act.wait_ge(squared, j + 1)
                        nc.scalar.activation(basis[:, 0, :], basis[:, 1, :], ACT.Exp, scale=-coef).then_inc(basis_ready, 1)

                    def rstd_start(q):
                        act.wait_ge(var_ready, q + 1)
                        nc.scalar.activation(lnv[:], ve[:], ACT.Ln).then_inc(ln_ready, 1)
                        act.wait_ge(ln_ready, q + 1)
                        wait_used(act, rstd_ready, q, 1)
                        nc.scalar.activation(r0[:], lnv[:], ACT.Exp, scale=-0.5).then_inc(r0_ready, 1)

                    def softplus(q):
                        act.wait_ge(posu_ready, q + 1)
                        wait_used(act, eu_ready, q, 1)
                        nc.scalar.activation(absu[:], u_ps[:], ACT.Abs, bias=bf1).then_inc(absu_ready, 1)
                        act.wait_ge(absu_ready, q + 1)
                        nc.scalar.activation(eu[:], absu[:], ACT.Exp, scale=-1.0).then_inc(eu_ready, 1)
                        act.wait_ge(eu_ready, q + 1)
                        wait_used(act, su_ready, q, 1)
                        nc.scalar.activation(lu[:], eu[:], ACT.Ln, scale=0.5, bias=half).then_inc(lu_ready, 1)

                    def relu(q):
                        act.wait_ge(xnT_ready, q + 1)
                        wait_used(act, hs_ready, q, 1)
                        nc.scalar.activation(hT[:], xT_ps[:], ACT.Relu).then_inc(hT_ready, 1)

                    def sum_out(q, par):
                        act.wait_ge(sum_ready, q + 1)
                        if not (isinstance(q, int) and q < 2):
                            for k in range(CHAINS):
                                act.wait_ge(added[k], 32 * (q - 1))
                        nc.scalar.activation(comb1[:, par, :, :].rearrange("p t c -> p (t c)"), sum_ps[:], ACT.Copy).then_inc(comb_ready, 1)

                    half = cols[:, 4:5]
                    nc.scalar.preload_act_table_set("natural_log_exp_and_others")
                    make_basis(0)
                    rstd_start(0)
                    softplus(0)
                    relu(0)

                    def step(q, par):
                        if exists(q + 1):
                            rstd_start(q + 1)
                            if par == 1:
                                make_basis((q + 1) // 2 if isinstance(q, int) else pair_of[0])
                            relu(q + 1)
                        sum_out(q, par)
                        if exists(q + 1):
                            softplus(q + 1)
                    pair_of = [None]
                    step(0, 0)
                    step(1, 1)
                    with act.Fori(1, QUADS // 2 - 1) as i:
                        pair_of[0] = i + 1
                        step(2 * i, 0)
                        step(2 * i + 1, 1)
                    step(QUADS - 2, 0)
                    step(QUADS - 1, 1)

                @block.tensor
                def _(pe):
                    def filter_up(q, par):
                        pe.wait_ge(basis_ready, half_count(q, par, 2) // 2 if isinstance(q, int) else pair_of[0])
                        wait_used(pe, posu_ready, q, 1)
                        wait_used(pe, absu_ready, q, 1)
                        at = BASIS_AT[par]
                        nc.tensor.matmul(u_ps[:], wf1[at:at + BASIS, :], basis[at:at + BASIS, 0, :],
                                         start=True, stop=True).then_inc(u_ready, 1)

                    def filter_down(q):
                        pe.wait_ge(su_ready, q + 1)
                        wait_used(pe, efb_ready, q, 1)
                        for t in range(QT):
                            last = nc.tensor.matmul(ef_ps[:, t * P:(t + 1) * P], su[:, t * P:(t + 1) * P], wf2[:], start=True, stop=True)
                        last.then_inc(ef_ready, 1)

                    def turn(q):
                        pe.wait_ge(xn_ready, q + 1)
                        wait_used(pe, hT_ready, q, 1)
                        for t in range(QT):
                            last = nc.tensor.transpose(xT_ps[:, t * P:(t + 1) * P], xn[:, t, :], ident[:])
                        last.then_inc(xnT_ready, 1)

                    def project(q):
                        pe.wait_ge(hT_ready, q + 1)
                        wait_used(pe, msg_ready, q, 1)
                        for t in range(QT):
                            last = nc.tensor.matmul(hs_ps[:, t * P:(t + 1) * P], hT[:, t * P:(t + 1) * P], wlin[:], start=True, stop=True)
                        last.then_inc(hs_ready, 1)

                    def tile_sums(q, par):
                        pe.wait_ge(msg_ready, q + 1)
                        pe.wait_ge(same_ready, q + 1)
                        wait_used(pe, comb_ready, q, 1)
                        for t in range(QT):
                            last = nc.tensor.matmul(sum_ps[:, t * P:(t + 1) * P], same[:, par, t, :], msg[:, t * P:(t + 1) * P], start=True, stop=True)
                        last.then_inc(sum_ready, 1)

                    pair_of = [None]
                    filter_up(0, 0)
                    turn(0)
                    project(0)
                    filter_down(0)

                    def step(q, par):
                        tile_sums(q, par)
                        if exists(q + 1):
                            turn(q + 1)
                            filter_up(q + 1, 1 - par)
                            project(q + 1)
                            filter_down(q + 1)
                    step(0, 0)
                    step(1, 1)
                    with pe.Fori(1, QUADS // 2 - 1) as i:
                        pair_of[0] = i + 1
                        step(2 * i, 0)
                        pair_of[0] = i + 2
                        step(2 * i + 1, 1)
                    step(QUADS - 2, 0)
                    step(QUADS - 1, 1)

            with ExitStack() as sems:
                def s2(name):
                    return sems.enter_context(nc.semaphore("n1_" + name))
                loaded = [s2(f"loaded{p}") for p in range(2)]
                stored = [s2(f"stored{p}") for p in range(2)]
                agg_ready, xb_ready, aggT_ready, aT_ready = s2("agg_ready"), s2("xb_ready"), s2("aggT_ready"), s2("aT_ready")
                stats_ready, aggr_ready, var_ready = s2("stats_ready"), s2("aggr_ready"), s2("var_ready")
                ln_ready, r0_ready = s2("ln_ready"), s2("r0_ready")
                r1_ready, r2_ready, r3_ready, rstd_ready = s2("r1_ready"), s2("r2_ready"), s2("r3_ready"), s2("rstd_ready")
                xn_ready, xnT_ready, hT_ready, self_ready = s2("xn_ready"), s2("xnT_ready"), s2("hT_ready"), s2("self_ready")
                u_ready, absu_ready, posu_ready = s2("u_ready"), s2("absu_ready"), s2("posu_ready")
                eu_ready, lu_ready, su_ready, mlp_ready = s2("eu_ready"), s2("lu_ready"), s2("su_ready"), s2("mlp_ready")
                x1_ready, x1b_ready, h1_ready, y_ready = s2("x1_ready"), s2("x1b_ready"), s2("h1_ready"), s2("y_ready")
                aggT_ps, u_ps, mlp_ps, xT_ps, self_ps = bank[0], bank[1], bank[2], bank[3], bank[4]
                block = sems.enter_context(nc.Block())

                @block.sync
                def _(sp):
                    def load(q, par):
                        wait_used(sp, agg_ready, q, 2)
                        hold(sp, sp_passed)
                        wait_used(sp, xb_ready, q, 2)
                        hold(sp, sp_passed)
                        for k in range(CHAINS):
                            sp.dma_start(agg_in(k, par), quad_rows(agg1[k], q, C)).then_inc(loaded[par], 16)
                        sp.dma_start(flat(nx, par), quad_rows(ins["x"], q, C)).then_inc(loaded[par], 16)
                    over_quads(sp, load)

                @block.gpsimd
                def _(pool):
                    def enter(q, par):
                        pool.wait_ge(loaded[par], half_count(q, par, 48))
                        wait_used(pool, aggT_ready, q, 1)
                        nc.gpsimd.tensor_tensor(msg[:], agg_in(0, par), agg_in(1, par), ALU.add).then_inc(agg_ready, 1)
                        wait_used(pool, x1_ready, q, 2)
                        nc.gpsimd.tensor_tensor(xg[:, par, :, :], nx[:, par, :, :], bm2[:].unsqueeze(1).broadcast_to([P, QT, C]),
                                                ALU.add).then_inc(xb_ready, 1)
                    enter(0, 0)

                    def step(q, par):
                        if exists(q + 1):
                            enter(q + 1, 1 - par)
                        pool.wait_ge(x1_ready, q + 1)
                        wait_used(pool, y_ready, q, 1)
                        nc.gpsimd.tensor_tensor(efb[:].rearrange("p (t c) -> p t c", t=QT), x1[:, par, :, :],
                                                bself[:].unsqueeze(1).broadcast_to([P, QT, C]), ALU.add).then_inc(x1b_ready, 1)
                        pool.wait_ge(xn_ready, q + 1)
                        if not (isinstance(q, int) and q < 2):
                            pool.wait_ge(stored[par], half_count(q, par, 32) - 32)
                        hold(pool, pool_passed)
                        nc.gpsimd.tensor_scalar(h1s[:, par, :, :].rearrange("p t c -> p (t c)"), xn[:].rearrange("p t c -> p (t c)"), 0.0, None, ALU.max).then_inc(h1_ready, 1)
                    over_quads(pool, step)

                @block.vector
                def _(dve):
                    def mlp_in(q):
                        dve.wait_ge(u_ready, q + 1)
                        wait_used(dve, su_ready, q, 1)
                        nc.vector.tensor_scalar(posu[:], u_ps[:], bm1, 0.0, ALU.add, ALU.max).then_inc(posu_ready, 1)

                    def mlp_out(q):
                        dve.wait_ge(posu_ready, q + 1)
                        dve.wait_ge(lu_ready, q + 1)
                        wait_used(dve, mlp_ready, q, 1)
                        nc.vector.tensor_tensor(su[:], posu[:], lu[:], ALU.add).then_inc(su_ready, 1)

                    def residual(q, par):
                        dve.wait_ge(mlp_ready, q + 1)
                        dve.wait_ge(xb_ready, q + 1)
                        wait_used(dve, xn_ready, q, 2)
                        wait_used(dve, x1b_ready, q, 2)
                        nc.vector.tensor_tensor(flat(x1, par), mlp_ps[:], flat(xg, par), ALU.add).then_inc(x1_ready, 1)
                        dve.wait_ge(x1_ready, q + 1)
                        for t in range(QT):
                            last = nc.vector.bn_stats(out=stats[:, t, :], in_=x1[:, par, t, :])
                        last.then_inc(stats_ready, 1)
                        dve.wait_ge(stats_ready, q + 1)
                        hold(dve, dve_passed)
                        for t in range(QT):
                            last = nc.vector.bn_aggr(out=mv[:, t, :], in_=stats[:, t, :])
                        last.then_inc(aggr_ready, 1)
                        dve.wait_ge(aggr_ready, q + 1)
                        wait_used(dve, ln_ready, q, 1)
                        nc.vector.tensor_scalar(ve[:], mv[:, :, 1], LN_EPS, None, ALU.add).then_inc(var_ready, 1)

                    def normalise(q, par):
                        dve.wait_ge(r0_ready, q + 1)
                        nc.vector.tensor_tensor(r1[:], r0[:], r0[:], ALU.mult).then_inc(r1_ready, 1)
                        dve.wait_ge(r1_ready, q + 1)
                        nc.vector.tensor_tensor(r2[:], r1[:], ve[:], ALU.mult).then_inc(r2_ready, 1)
                        dve.wait_ge(r2_ready, q + 1)
                        nc.vector.tensor_scalar(r3[:], r2[:], -0.5, 1.5, ALU.mult, ALU.add).then_inc(r3_ready, 1)
                        dve.wait_ge(r3_ready, q + 1)
                        nc.vector.tensor_tensor(rstd[:], r3[:], r0[:], ALU.mult).then_inc(rstd_ready, 1)
                        dve.wait_ge(rstd_ready, q + 1)
                        wait_used(dve, xnT_ready, q, 1)
                        wait_used(dve, h1_ready, q, 1)
                        for t in range(QT):
                            last = nc.vector.tensor_scalar(xn[:, t, :], x1[:, par, t, :], mv[:, t, 0:1], rstd[:, t:t + 1],
                                                           ALU.subtract, ALU.mult)
                        last.then_inc(xn_ready, 1)

                    def leave(q, par):
                        dve.wait_ge(self_ready, q + 1)
                        dve.wait_ge(x1b_ready, q + 1)
                        if not (isinstance(q, int) and q < 2):
                            dve.wait_ge(stored[par], half_count(q, par, 32) - 32)
                        nc.vector.tensor_tensor(flat(ys, par), self_ps[:], efb[:], ALU.add).then_inc(y_ready, 1)

                    mlp_in(0)
                    mlp_out(0)

                    def step(q, par):
                        residual(q, par)
                        if exists(q + 1):
                            mlp_in(q + 1)
                        normalise(q, par)
                        if exists(q + 1):
                            mlp_out(q + 1)
                        leave(q, par)
                    over_quads(dve, step)

                @block.scalar
                def _(act):
                    half = cols[:, 4:5]

                    def agg_turned(q):
                        act.wait_ge(aggT_ready, q + 1)
                        wait_used(act, u_ready, q, 1)
                        nc.scalar.activation(aT[:], aggT_ps[:], ACT.Copy).then_inc(aT_ready, 1)

                    def softplus(q):
                        act.wait_ge(posu_ready, q + 1)
                        wait_used(act, eu_ready, q, 1)
                        nc.scalar.activation(absu[:], u_ps[:], ACT.Abs, bias=bm1).then_inc(absu_ready, 1)
                        act.wait_ge(absu_ready, q + 1)
                        nc.scalar.activation(eu[:], absu[:], ACT.Exp, scale=-1.0).then_inc(eu_ready, 1)
                        act.wait_ge(eu_ready, q + 1)
                        wait_used(act, su_ready, q, 1)
                        nc.scalar.activation(lu[:], eu[:], ACT.Ln, scale=0.5, bias=half).then_inc(lu_ready, 1)

                    nc.scalar.preload_act_table_set("natural_log_exp_and_others")
                    agg_turned(0)
                    softplus(0)

                    def step(q, par):
                        if exists(q + 1):
                            agg_turned(q + 1)
                        act.wait_ge(var_ready, q + 1)
                        nc.scalar.activation(lnv[:], ve[:], ACT.Ln).then_inc(ln_ready, 1)
                        act.wait_ge(ln_ready, q + 1)
                        wait_used(act, rstd_ready, q, 1)
                        nc.scalar.activation(r0[:], lnv[:], ACT.Exp, scale=-0.5).then_inc(r0_ready, 1)
                        if exists(q + 1):
                            softplus(q + 1)
                        act.wait_ge(xnT_ready, q + 1)
                        wait_used(act, self_ready, q, 1)
                        nc.scalar.activation(hT[:], xT_ps[:], ACT.Relu).then_inc(hT_ready, 1)
                        act.wait_ge(h1_ready, q + 1)
                        act.dma_start(quad_rows(h1_dram, q, C), flat(h1s, par)).then_inc(stored[par], 16)
                        act.wait_ge(y_ready, q + 1)
                        act.dma_start(quad_rows(y_dram, q, C), flat(ys, par)).then_inc(stored[par], 16)
                    over_quads(act, step)
                    for par in range(2):
                        act.wait_ge(stored[par], 32 * (QUADS // 2))

                @block.tensor
                def _(pe):
                    def agg_up(q):
                        pe.wait_ge(agg_ready, q + 1)
                        wait_used(pe, aT_ready, q, 1)
                        for t in range(QT):
                            last = nc.tensor.transpose(aggT_ps[:, t * P:(t + 1) * P], msg[:, t * P:(t + 1) * P], ident[:])
                        last.then_inc(aggT_ready, 1)
                        pe.wait_ge(aT_ready, q + 1)
                        wait_used(pe, posu_ready, q, 1)
                        wait_used(pe, absu_ready, q, 1)
                        nc.tensor.matmul(u_ps[:], wm1[:], aT[:], start=True, stop=True).then_inc(u_ready, 1)

                    def mlp_down(q):
                        pe.wait_ge(su_ready, q + 1)
                        wait_used(pe, x1_ready, q, 1)
                        for t in range(QT):
                            last = nc.tensor.matmul(mlp_ps[:, t * P:(t + 1) * P], su[:, t * P:(t + 1) * P], wm2[:], start=True, stop=True)
                        last.then_inc(mlp_ready, 1)
                    agg_up(0)
                    mlp_down(0)

                    def step(q, par):
                        if exists(q + 1):
                            agg_up(q + 1)
                        pe.wait_ge(xn_ready, q + 1)
                        wait_used(pe, hT_ready, q, 1)
                        for t in range(QT):
                            last = nc.tensor.transpose(xT_ps[:, t * P:(t + 1) * P], xn[:, t, :], ident[:])
                        last.then_inc(xnT_ready, 1)
                        if exists(q + 1):
                            mlp_down(q + 1)
                        pe.wait_ge(hT_ready, q + 1)
                        wait_used(pe, y_ready, q, 1)
                        for t in range(QT):
                            last = nc.tensor.matmul(self_ps[:, t * P:(t + 1) * P], hT[:, t * P:(t + 1) * P], wself[:], start=True, stop=True)
                        last.then_inc(self_ready, 1)
                    over_quads(pe, step)

            with ExitStack() as sems:
                def s3(name):
                    return sems.enter_context(nc.semaphore("e2_" + name))
                idx_loaded = [s3(f"idx_loaded{p}") for p in range(2)]
                keys_loaded = [s3(f"keys_loaded{p}") for p in range(2)]
                gathered = [s3(f"gathered{p}") for p in range(2)]
                added = [s3(f"added{k}") for k in range(CHAINS)]
                idxf_ready, same_ready, counted = s3("idxf_ready"), s3("same_ready"), s3("counted")
                before_ready, spare_ready, target_ready = s3("before_ready"), s3("spare_ready"), s3("target_ready")
                sumT_ready, sT_ready, neigh_ready, comb_ready = s3("sumT_ready"), s3("sT_ready"), s3("neigh_ready"), s3("comb_ready")
                sumT_ps, neigh_ps = bank[0], bank[1]
                block = sems.enter_context(nc.Block())

                @block.sync
                def _(sp):
                    def load(q, par):
                        if not (isinstance(q, int) and q < 2):
                            sp.wait_ge(gathered[par], half_count(q, par, 64) - 64)
                        hold(sp, sp_passed)
                        wait_used(sp, idxf_ready, q, 2)
                        hold(sp, sp_passed)
                        sp.dma_start(idx[:, par, :, :].rearrange("p a t -> p (a t)"), ins["edge_cols"][q, :, :]).then_inc(idx_loaded[par], 16)
                        wait_used(sp, same_ready, q, 2)
                        hold(sp, sp_passed)
                        sp.dma_start(key_rows[:, par, :], ins["src_rows"][q, :].partition_broadcast(P)).then_inc(keys_loaded[par], 16)
                    over_quads(sp, load)

                @block.gpsimd
                def _(pool):
                    def gather(q, par, t):
                        if t == 0:
                            pool.wait_ge(idx_loaded[par], half_count(q, par, 16))
                            wait_used(pool, sumT_ready, q, 2)
                        hold(pool, pool_passed)
                        nc.gpsimd.indirect_dma_start(
                            out=xg[:, par, t, :], out_offset=None, in_=h1_dram,
                            in_offset=bass.IndirectOffsetOnAxis(ap=idx[:, par, 1, t:t + 1], axis=0)).then_inc(gathered[par], 16)

                    def add(q, par, t):
                        if t == 0:
                            pool.wait_ge(comb_ready, q + 1)
                            pool.wait_ge(target_ready, q + 1)
                            pool.wait_ge(counted, q + 1)
                        k = t % CHAINS
                        n = 32 * q + 16 * (t // CHAINS)
                        if not (isinstance(n, int) and n == 0):
                            pool.wait_ge(added[k], n)
                        hold(pool, pool_passed)
                        nc.gpsimd.indirect_dma_start(
                            out=agg2[k], out_offset=bass.IndirectOffsetOnAxis(ap=target[:, par, t:t + 1], axis=0),
                            in_=comb[:, par, t, :], in_offset=None, compute_op=ALU.add).then_inc(added[k], 16)

                    for t in range(QT):
                        gather(0, 0, t)
                    for t in range(QT):
                        gather(1, 1, t)

                    def step(q, par):
                        for t in range(QT):
                            add(q, par, t)
                            if exists(q + 2):
                                gather(q + 2, par, t)
                    over_quads(pool, step)
                    for k in range(CHAINS):
                        pool.wait_ge(added[k], 32 * QUADS)

                @block.vector
                def _(dve):
                    def step(q, par):
                        dve.wait_ge(idx_loaded[par], half_count(q, par, 16))
                        nc.vector.tensor_copy(idxf[:, par, :], idx[:, par, 0, :]).then_inc(idxf_ready, 1)
                        dve.wait_ge(idxf_ready, q + 1)
                        dve.wait_ge(keys_loaded[par], half_count(q, par, 16))
                        wait_used(dve, sumT_ready, q, 2)
                        for t in range(QT):
                            last = nc.vector.tensor_scalar(same[:, par, t, :], key_rows[:, par, t * P:(t + 1) * P],
                                                           idxf[:, par, t:t + 1], None, ALU.is_equal)
                        last.then_inc(same_ready, 1)
                        dve.wait_ge(same_ready, q + 1)
                        for t in range(QT):
                            last = nc.vector.tensor_tensor_reduce(out=junk[:, t, :], in0=same[:, par, t, :], in1=lower[:], scale=1.0,
                                                                  scalar=0.0, op0=ALU.mult, op1=ALU.add, accum_out=before[:, par, t:t + 1])
                        last.then_inc(before_ready, 1)
                        dve.wait_ge(before_ready, q + 1)
                        nc.vector.tensor_scalar(spare[:, par, :], before[:, par, :], 1.0, dump, ALU.min, ALU.mult).then_inc(spare_ready, 1)
                        dve.wait_ge(spare_ready, q + 1)
                        if not (isinstance(q, int) and q < 2):
                            for k in range(CHAINS):
                                dve.wait_ge(added[k], 32 * (q - 1))
                        else:
                            nc.vector.memset(comb[:, par, :, C:W2], 0.0)
                        nc.vector.tensor_tensor(target[:, par, :], spare[:, par, :], idxf[:, par, :], ALU.max).then_inc(target_ready, 1)
                        dve.wait_ge(target_ready, q + 1)
                        nc.vector.tensor_reduce(out=comb[:, par, :, C], in_=same[:, par, :, :], axis=AX.X, op=ALU.add).then_inc(counted, 1)
                    over_quads(dve, step)

                @block.tensor
                def _(pe):
                    def sums(q, par):
                        pe.wait_ge(gathered[par], half_count(q, par, 64))
                        pe.wait_ge(same_ready, q + 1)
                        wait_used(pe, sT_ready, q, 1)
                        for t in range(QT):
                            last = nc.tensor.matmul(sumT_ps[:, t * P:(t + 1) * P], xg[:, par, t, :], same[:, par, t, :], start=True, stop=True)
                        last.then_inc(sumT_ready, 1)
                        pe.wait_ge(sT_ready, q + 1)
                        wait_used(pe, comb_ready, q, 1)
                        for t in range(QT):
                            last = nc.tensor.matmul(neigh_ps[:, t * P:(t + 1) * P], hT[:, t * P:(t + 1) * P], wneigh[:], start=True, stop=True)
                        last.then_inc(neigh_ready, 1)
                    over_quads(pe, sums)

                @block.scalar
                def _(act):
                    def step(q, par):
                        act.wait_ge(sumT_ready, q + 1)
                        wait_used(act, neigh_ready, q, 1)
                        nc.scalar.activation(hT[:], sumT_ps[:], ACT.Copy).then_inc(sT_ready, 1)
                        act.wait_ge(neigh_ready, q + 1)
                        if not (isinstance(q, int) and q < 2):
                            for k in range(CHAINS):
                                act.wait_ge(added[k], 32 * (q - 1))
                        nc.scalar.activation(comb[:, par, :, 0:C], neigh_ps[:].rearrange("p (t c) -> p t c", t=QT), ACT.Copy).then_inc(comb_ready, 1)
                    over_quads(act, step)

        with ExitStack() as sems:
            block = sems.enter_context(nc.Block())

            @block.sync
            def _(sp):
                def load(q, par):
                    wait_used(sp, n2_agg, q, 2)
                    hold(sp, sp_passed)
                    wait_used(sp, n2_yb, q, 2)
                    hold(sp, sp_passed)
                    for k in range(CHAINS):
                        sp.dma_start(flat(nagg[k], par), quad_rows(agg2[k], q, W2)).then_inc(n2_loaded[par], 16)
                    sp.dma_start(flat(nx, par), quad_rows(y_dram, q, C)).then_inc(n2_loaded[par], 16)
                over_quads(sp, load)

            @block.gpsimd
            def _(pool):
                def step(q, par):
                    pool.wait_ge(n2_loaded[par], half_count(q, par, 48))
                    wait_used(pool, n2_out, q, 2)
                    nc.gpsimd.tensor_tensor(flat(comb, par), flat(nagg[0], par), flat(nagg[1], par), ALU.add).then_inc(n2_agg, 1)
                over_quads(pool, step)

            @block.vector
            def _(dve):
                def step(q, par):
                    dve.wait_ge(n2_agg, q + 1)
                    nc.vector.tensor_scalar(cm[:, par, :], comb[:, par, :, C], 1.0, None, ALU.min).then_inc(cm_ready, 1)
                    nc.vector.tensor_scalar(counts[:, par, :], comb[:, par, :, C], 1.0, None, ALU.max).then_inc(capped, 1)
                    dve.wait_ge(capped, q + 1)
                    nc.vector.reciprocal(rc[:, par, :], counts[:, par, :]).then_inc(rc_ready, 1)
                    dve.wait_ge(cm_ready, q + 1)
                    dve.wait_ge(rc_ready, q + 1)
                    wait_used(dve, n2_out, q, 2)
                    for t in range(QT):
                        last = nc.vector.scalar_tensor_tensor(out=x1[:, par, t, :], in0=bneigh[:], scalar=cm[:, par, t:t + 1],
                                                              in1=nx[:, par, t, :], op0=ALU.mult, op1=ALU.add)
                    last.then_inc(n2_yb, 1)
                    dve.wait_ge(n2_yb, q + 1)
                    if not (isinstance(q, int) and q < 2):
                        dve.wait_ge(n2_stored[par], half_count(q, par, 16) - 16)
                    for t in range(QT):
                        last = nc.vector.scalar_tensor_tensor(out=ys[:, par, t, :], in0=comb[:, par, t, 0:C], scalar=rc[:, par, t:t + 1],
                                                              in1=x1[:, par, t, :], op0=ALU.mult, op1=ALU.add)
                    last.then_inc(n2_out, 1)
                over_quads(dve, step)

            @block.scalar
            def _(act):
                def step(q, par):
                    act.wait_ge(n2_out, q + 1)
                    act.dma_start(quad_rows(out_dram, q, C), flat(ys, par)).then_inc(n2_stored[par], 16)
                over_quads(act, step)
                for par in range(2):
                    act.wait_ge(n2_stored[par], 16 * (QUADS // 2))


CENTERS = (np.arange(BASIS, dtype=np.float32) / np.float32(BASIS - 1)) * np.float32(5.0)


def kernel(x, src, dst, edge_weight, L0_gnn_W_lin, L0_gnn_Wf1, L0_gnn_bf1, L0_gnn_Wf2, L0_gnn_bf2, L0_gnn_Wm1, L0_gnn_bm1,
           L0_gnn_Wm2, L0_gnn_bm2, L1_gnn_W_self, L1_gnn_b_self, L1_gnn_W_neigh, L1_gnn_b_neigh):
    import concourse.bacc as bacc
    from concourse.bass_utils import run_bass_kernel_spmd

    pad = ROWS - N_ROWS
    extra = np.arange(N_ROWS, ROWS, dtype=np.int32)
    src_pad = np.concatenate([np.asarray(src), extra])
    dst_pad = np.concatenate([np.asarray(dst), extra])
    ew_pad = np.concatenate([np.asarray(edge_weight), np.zeros(pad, np.float32)])
    x_pad = np.concatenate([np.asarray(x), np.zeros((pad, C), np.float32)])

    def by_column(a):
        return a.reshape(QUADS, QT, P).transpose(0, 2, 1)

    cols = np.zeros((P, 16), np.float32)
    for at in BASIS_AT:
        cols[at:at + BASIS, 0] = -CENTERS
    cols[:, 1] = ROWS + np.arange(P)
    cols[:, 2] = np.asarray(L0_gnn_bf1)
    cols[:, 3] = np.asarray(L0_gnn_bm1)
    cols[:, 4] = 0.5
    cols[:, 9] = TOP
    wf1 = np.zeros((P, C), np.float32)
    for at in BASIS_AT:
        wf1[at:at + BASIS] = np.asarray(L0_gnn_Wf1)
    consts = np.zeros((P, 4 * P), np.float32)
    p32, c32, b = np.arange(P)[:, None] % 32, np.arange(32)[None], 32 * np.arange(HI)[:, None] + np.arange(LO)[None]
    consts[:, 0:P] = np.arange(P)
    consts[:, P:2 * P] = 1.0
    consts[:, 2 * P:2 * P + 32] = p32 == c32
    consts[:, 2 * P + 32:2 * P + 64] = p32 < c32
    consts[:, 2 * P + 64:2 * P + 96] = np.arange(P)[:, None] < c32
    consts[0:HI, 2 * P + 96:3 * P] = np.where(b // QT + AHEAD >= QUADS - 1, ROWS, QROWS * (b // QT + AHEAD + 1) - SPAN)
    consts[:, 3 * P:3 * P + 3] = np.arange(P)[:, None] == np.arange(3)
    consts[:, 3 * P + 3:3 * P + 7] = np.arange(P)[:, None] // 32 == np.arange(4)
    arrays = {
        "consts": consts,
        "qbase": np.broadcast_to((QROWS * np.arange(QUADS)).astype(np.float32), (P, QUADS)),
        "dst_flat": np.concatenate([dst_pad, np.array([ROWS], np.int32)]),
        "tile_first": dst_pad[::P], "tile_last": dst_pad[P - 1::P],
        "src_cols": by_column(src_pad), "dst_cols": by_column(dst_pad),
        "x": x_pad,
        "edge_cols": np.concatenate([by_column(src_pad), by_column(dst_pad)], axis=2),
        "src_rows": src_pad.reshape(QUADS, QROWS),
        "dst_rows": dst_pad.reshape(QUADS, QROWS),
        "ew_rows": ew_pad.reshape(QUADS, QROWS),
        "ident": np.eye(P, dtype=np.float32),
        "lower": np.tri(P, k=-1, dtype=np.float32),
        "cols": cols,
        "wlin": np.asarray(L0_gnn_W_lin).T, "wf1": wf1, "wf2": np.asarray(L0_gnn_Wf2),
        "wm1": np.asarray(L0_gnn_Wm1), "wm2": np.asarray(L0_gnn_Wm2),
        "wself": np.asarray(L1_gnn_W_self).T, "wneigh": np.asarray(L1_gnn_W_neigh).T,
        "bf2": np.asarray(L0_gnn_bf2), "bm2": np.asarray(L0_gnn_bm2),
        "bself": np.asarray(L1_gnn_b_self), "bneigh": np.asarray(L1_gnn_b_neigh),
    }
    nc = bacc.Bacc("TRN2", target_bir_lowering=False, num_devices=1)
    given, ins = {}, {}
    for name, a in arrays.items():
        a = np.ascontiguousarray(a)
        given[f"in_{name}"] = a
        ins[name] = nc.dram_tensor(f"in_{name}", a.shape, mybir.dt.from_np(a.dtype), kind="ExternalInput").ap()
    out = nc.dram_tensor("out", (ROWS, C), mybir.dt.float32, kind="ExternalOutput").ap()
    gnn_kernel(nc, ins, out)
    r = run_bass_kernel_spmd(nc, [given], core_ids=[0])
    return r.results[0]["out"][:N_ROWS]
```

```python
from contextlib import ExitStack

import numpy as np

import concourse.bass as bass
from concourse import mybir

N_ROWS = 50000
C = 128
P = 128
QT = 4
QROWS = QT * P
QUADS = -(-N_ROWS // QROWS)
ROWS = QUADS * QROWS
TABLE_ROWS = ROWS + P
CHAINS = 2
W2 = 132
BASIS = 50
BASIS_AT = (0, 64)
TILES = QUADS * QT
SPAN = 2 * P
MW = C + 1
UT = 2 * QT
UNITS = ROWS // (UT * P)
AHEAD = 2
LAG = 12
HI, LO = -(-ROWS // 4096), 32
ZEROS = 2 * CHAINS * UT * W2
TOP = 40.0
LOG2 = 0.6931471805599453
LN_EPS = 1e-5


def over_quads(eng, step):
    step(0, 0)
    step(1, 1)
    with eng.Fori(1, QUADS // 2 - 1) as i:
        step(2 * i, 0)
        step(2 * i + 1, 1)
    step(QUADS - 2, 0)
    step(QUADS - 1, 1)


def over_units(eng, step):
    step(0, 0)
    step(1, 1)
    with eng.Fori(1, (UNITS - 1) // 2) as i:
        step(2 * i, 0)
        step(2 * i + 1, 1)
    step(UNITS - 1, 0)


def wait_used(eng, used, q, back):
    if isinstance(q, int) and q < back:
        return
    eng.wait_ge(used, q - back + 1)


def hold(eng, passed):
    eng.sem_inc(passed, 1)


def half_count(q, par, unit):
    return unit * ((q - par) // 2 + 1) if isinstance(q, int) else (unit // 2) * q + (unit - (unit // 2) * par)


def at_first(q, count):
    return isinstance(q, int) and q < count


def there(q):
    return not isinstance(q, int) or 0 <= q < QUADS


def over_steps(eng, step):
    first = -(-(LAG + 2) // 4) * 4
    loops = (QUADS - 2 - first) // 4

    def peeled(s):
        step(s, s % 2, 1 - s % 2, s // 2, s // 2 % 2)
    for s in range(first):
        peeled(s)
    with eng.Fori(0, loops) as i:
        for n in range(4):
            step(4 * i + (first + n), n % 2, 1 - n % 2, 2 * i + (first // 2 + n // 2), n // 2)
    for s in range(first + 4 * loops, QUADS + LAG):
        peeled(s)


def exists(q):
    return not isinstance(q, int) or q < QUADS


def gnn_kernel(nc, ins, out_dram):
    f32, i32, bf16 = mybir.dt.float32, mybir.dt.int32, mybir.dt.bfloat16
    ALU = mybir.AluOpType
    ACT = mybir.ActivationFunctionType
    AX = mybir.AxisListType

    with ExitStack() as ctx:
        def sb(name, shape, dt=f32):
            return ctx.enter_context(nc.sbuf_tensor(name, shape, dt))

        def sem(name):
            return ctx.enter_context(nc.semaphore(name))

        def dram(name, shape):
            return nc.dram_tensor(name, shape, f32, kind="Internal").ap()

        agg1 = [dram(f"agg1_{k}", [TABLE_ROWS, C]) for k in range(CHAINS)]
        agg2 = [dram(f"agg2_{k}", [TABLE_ROWS, W2]) for k in range(CHAINS)]
        h1_dram = dram("h1_table", [ROWS + SPAN, C])
        y_dram = dram("y_table", [ROWS, C])

        def quad_rows(table, q, width):
            return table[0:ROWS, :].rearrange("(q p t) c -> q p (t c)", p=P, t=QT)[q, :, :]

        def tiles_of(table, q, width):
            return table[0:ROWS, :].rearrange("(q t p) c -> q p t c", p=P, t=QT)[q, :, :, :]

        ident = sb("ident", [P, P])
        lower = sb("lower", [P, P])
        cols = sb("cols", [P, 16])
        negc, dump, bf1, bm1 = (cols[:, k:k + 1] for k in range(4))
        wlin = sb("wlin", [P, C])
        wf1 = sb("wf1", [P, C])
        wf2 = sb("wf2", [P, C])
        wm1 = sb("wm1", [P, C])
        wm2 = sb("wm2", [P, C])
        wself = sb("wself", [P, C])
        wneigh = sb("wneigh", [P, C])
        bf2 = sb("bf2", [P, C])
        bm2 = sb("bm2", [P, C])
        bself = sb("bself", [P, C])
        bneigh = sb("bneigh", [P, C])
        weights = [(ident, "ident"), (lower, "lower"), (cols, "cols"), (wlin, "wlin"), (wf1, "wf1"), (wf2, "wf2"),
                   (wm1, "wm1"), (wm2, "wm2"), (wself, "wself"), (wneigh, "wneigh")]
        rows = [(bf2, "bf2"), (bm2, "bm2"), (bself, "bself"), (bneigh, "bneigh")]
        weights_loaded = sem("weights_loaded")

        zeros = sb("zeros", [P, ZEROS])
        zeros_set = sem("zeros_set")
        tables_zeroed = sem("tables_zeroed")
        pool_passed, dve_passed, sp_passed = sem("pool_passed"), sem("dve_passed"), sem("sp_passed")

        ew = sb("ew", [P, 2, QROWS])
        basis = sb("basis", [P, 2, QROWS])
        idx = sb("idx", [P, 2, 2, QT], i32)
        idxf = sb("idxf", [P, 2, QT])
        key_rows = sb("key_rows", [P, 2, QROWS], i32)
        same = sb("same", [P, 2, QT, P])
        junk = sb("junk", [P, QT, P])
        before = sb("before", [P, 2, QT])
        spare = sb("spare", [P, 2, QT])
        target = sb("target", [P, 2, QT], i32)
        counts = sb("counts", [P, 2, QT])
        xg = sb("xg", [P, 2, QT, C])
        stats = sb("stats", [P, QT, 6])
        mv = sb("mv", [P, QT, 2])
        ve = sb("ve", [P, QT])
        lnv = sb("lnv", [P, QT])
        r0 = sb("r0", [P, QT])
        r1 = sb("r1", [P, QT])
        r2 = sb("r2", [P, QT])
        r3 = sb("r3", [P, QT])
        rstd = sb("rstd", [P, QT])
        xn = sb("xn", [P, QT, C])
        hT = sb("hT", [P, QROWS])
        aT = sb("aT", [P, QROWS])
        absu = sb("absu", [P, QROWS])
        posu = sb("posu", [P, QROWS])
        eu = sb("eu", [P, QROWS])
        lu = sb("lu", [P, QROWS])
        su = sb("su", [P, QROWS])
        efb = sb("efb", [P, QROWS])
        msg = sb("msg", [P, QROWS])
        comb = sb("comb", [P, 2, QT, W2])
        comb1 = sb("comb1", [P, 2, QT, C])
        agg_rows = sb("agg_rows", [P, 2 * UT * W2])
        nx = sb("nx", [P, 2, QT, C])
        x1 = sb("x1", [P, 2, QT, C])
        h1s = sb("h1s", [P, 2, QT, C])
        ys = sb("ys", [P, 2, QT, C])
        rc = sb("rc", [P, 2, UT])
        cm = sb("cm", [P, 2, UT])
        capped_counts = sb("capped_counts", [P, 2, UT])

        bank = [ctx.enter_context(nc.psum_tensor(f"bank{k}", [P, 512], f32)) for k in range(8)]

        msg_dram = dram("msg_table", [ROWS + SPAN, MW])
        off_dram = nc.dram_tensor("block_starts", [HI * LO], i32, kind="Internal").ap()
        consts = sb("consts", [P, 4 * P])
        iota, ones, eye32, upper32 = consts[:, 0:P], consts[:, P:2 * P], consts[:, 2 * P:2 * P + 32], consts[:, 2 * P + 32:2 * P + 64]
        upper_hi = consts[:, 2 * P + 64:2 * P + 96]
        last_start = consts[:, 2 * P + 96:2 * P + 128]
        third, quarter = consts[:, 3 * P:3 * P + 3], consts[:, 3 * P + 3:3 * P + 7]
        qbase = sb("qbase", [P, QUADS])
        firsts = sb("firsts", [P, TILES])
        first_row = sb("first_row", [1, TILES], i32)
        start_row = sb("start_row", [1, HI * LO], i32)
        flag = sb("flag", [1, 1], i32)
        bias3 = sb("bias3", [P, 3, QROWS], bf16)
        ones3 = sb("ones3", [P, P], bf16)
        efs, clampu, ln_out, neu, nlu, distance = efb, absu, lu, posu, msg, junk[:].rearrange("p t c -> p (t c)")
        nxn = comb1[:, 0, :, :]
        iota4 = sb("iota4", [P, QROWS])
        weights += [(qbase, "qbase"), (iota4, "iota4")]
        bf1_top, bf1_low, bm1_top, bm1_low = (cols[:, k:k + 1] for k in (5, 6, 7, 8))
        top, eps, minus_one = (cols[:, k:k + 1] for k in (9, 10, 11))
        srcs = sb("srcs", [P, 2, QT], i32)
        src_cols = sb("src_cols", [P, TILES], i32)
        dst_cols = sb("dst_cols", [P, TILES], i32)
        src_f = sb("src_f", [P, TILES])
        dst_f = sb("dst_f", [P, TILES])
        weights += [(src_cols, "src_cols"), (dst_cols, "dst_cols")]
        msgw = sb("msgw", [P, 2, QT, MW])
        win = sb("win", [P, 2, QT, 2, MW])
        rel = sb("rel", [P, QT, 2])
        hot = sb("hot", [P, QT, 2, P])
        aggs = sb("aggs", [P, QROWS])
        nclamp = sb("nclamp", [P, QROWS])
        nsu = sb("nsu", [P, QROWS])
        nstats = sb("nstats", [P, QT, 6])
        nmv = sb("nmv", [P, QT, 2])
        emv = sb("emv", [P, 2, QT, 2])
        root, square, ratio, factor, shift = (sb(name, [P, QT]) for name in ("root", "square", "ratio", "factor", "shift"))
        nsmall = sb("nsmall", [P, 6, QT])
        nhT = sb("nhT", [P, QROWS])

        def flat(t, par):
            return t[:, par, :, :].rearrange("p t c -> p (t c)")

        def agg_in(k, par):
            return agg_rows[:, (2 * k + par) * QT * C:(2 * k + par + 1) * QT * C]

        def whole(t):
            return t[:].rearrange("p b t c -> p (b t c)")

        def s4(name):
            return ctx.enter_context(nc.semaphore("n2_" + name))
        n2_loaded = [s4(f"loaded{p}") for p in range(2)]
        n2_stored = [s4(f"stored{p}") for p in range(2)]
        n2_agg, capped, rc_ready, cm_ready = s4("agg_ready"), s4("capped"), s4("rc_ready"), s4("cm_ready")
        n2_yb, n2_out = s4("yb_ready"), s4("out_ready")

        def zero_parts(table, width, n_rows):
            flat_table = table.rearrange("r c -> (r c)")
            per = n_rows * width // P
            view = flat_table.rearrange("(p n) -> p n", p=P)
            for at in range(0, per, ZEROS):
                yield view[:, at:at + min(ZEROS, per - at)], min(ZEROS, per - at)

        with ExitStack() as sems:
            def s0(name):
                return ctx.enter_context(nc.semaphore("s0_" + name))

            cur = sems.enter_context(nc.sbuf_tensor("cur", [P, TILES], i32))
            nxt = sems.enter_context(nc.sbuf_tensor("nxt", [P, TILES], i32))
            ends = sems.enter_context(nc.sbuf_tensor("ends", [P, 2, TILES], i32))
            curf = sems.enter_context(nc.sbuf_tensor("curf", [P, TILES], f32))
            nxtf = sems.enter_context(nc.sbuf_tensor("nxtf", [P, TILES], f32))
            lastf = sems.enter_context(nc.sbuf_tensor("lastf", [P, TILES], f32))
            bad = sems.enter_context(nc.sbuf_tensor("bad", [P, TILES], f32))
            hi_lo = sems.enter_context(nc.sbuf_tensor("hi_lo", [P, 2, TILES], i32))
            hi_lof = sems.enter_context(nc.sbuf_tensor("hi_lof", [P, 2, TILES], f32))
            hot_hi = sems.enter_context(nc.sbuf_tensor("hot_hi", [P, TILES, HI], bf16))
            hot_lo = sems.enter_context(nc.sbuf_tensor("hot_lo", [P, TILES, LO], bf16))
            by4 = sems.enter_context(nc.sbuf_tensor("by4", [P, 4 * HI], f32))
            count_cols = sems.enter_context(nc.sbuf_tensor("count_cols", [P, 4, HI], f32))
            per_hi = sems.enter_context(nc.sbuf_tensor("per_hi", [P, LO], f32))
            too_many = sems.enter_context(nc.sbuf_tensor("too_many", [HI, 2, LO], f32))
            starts = sems.enter_context(nc.sbuf_tensor("starts", [HI, LO], i32))
            violations = sems.enter_context(nc.sbuf_tensor("violations", [P, 4], f32))
            violated = sems.enter_context(nc.sbuf_tensor("violated", [P, 1], f32))
            part = sems.enter_context(nc.sbuf_tensor("part", [P, 9, C], f32))
            partb = sems.enter_context(nc.sbuf_tensor("partb", [P, 9, C], bf16))
            dst_loaded, hots_ready, counted4, by4_ready = s0("dst_loaded"), s0("hots_ready"), s0("counted4"), s0("by4_ready")
            sums_ready, per_hi_ready, starts_summed, starts_ready = s0("sums_ready"), s0("per_hi_ready"), s0("starts_summed"), s0("starts_ready")
            violated_ready, total_ready, flag_ready = s0("violated_ready"), s0("total_ready"), s0("flag_ready")
            consts_loaded = s0("consts_loaded")
            starts_out, starts_in, pads_set, chain = s0("starts_out"), s0("starts_in"), s0("pads_set"), s0("chain")
            block = sems.enter_context(nc.Block())

            @block.sync
            def _(sp):
                for t, a in ((cur[:], ins["dst_flat"][0:ROWS].rearrange("(p t) -> p t", p=P)),
                             (nxt[:], ins["dst_flat"][1:ROWS + 1].rearrange("(p t) -> p t", p=P)),
                             (ends[:, 0, :], ins["tile_first"].partition_broadcast(P)),
                             (ends[:, 1, :], ins["tile_last"].partition_broadcast(P)),
                             (first_row[0:1, :], ins["tile_first"].unsqueeze(0))):
                    sp.dma_start(t, a).then_inc(dst_loaded, 16)
                sp.dma_start(consts[:], ins["consts"]).then_inc(consts_loaded, 16)
                for t, name in weights:
                    sp.dma_start(t[:], ins[name]).then_inc(weights_loaded, 16)
                for t, name in rows:
                    sp.dma_start(t[:], ins[name].partition_broadcast(P)).then_inc(weights_loaded, 16)
                sp.wait_ge(zeros_set, 1)
                for table in agg2:
                    sp.dma_start(table[ROWS:TABLE_ROWS, :], zeros[:, 0:W2]).then_inc(pads_set, 16)
                sp.dma_start(msg_dram[ROWS:ROWS + SPAN, :].rearrange("(p w) c -> p (w c)", p=P), zeros[:, 0:2 * MW]).then_inc(pads_set, 16)
                sp.dma_start(h1_dram[ROWS:ROWS + SPAN, :].rearrange("(p w) c -> p (w c)", p=P), zeros[:, 0:2 * C]).then_inc(pads_set, 16)
                sp.wait_ge(starts_ready, 1)
                sp.dma_start(off_dram.rearrange("(h l) -> h l", h=HI), starts[:]).then_inc(starts_out, 16)
                sp.wait_ge(starts_out, 16)
                sp.dma_start(start_row[0:1, :], off_dram.unsqueeze(0)).then_inc(starts_in, 16)
                sp.wait_ge(starts_in, 16)
                sp.wait_ge(pads_set, 16 * (2 + CHAINS))
                sp.wait_ge(weights_loaded, 16 * (len(weights) + len(rows)))

            @block.vector
            def _(dve):
                done = [0]

                def link(ins_):
                    done[0] += 1
                    ins_.then_inc(chain, 1)
                    dve.wait_ge(chain, done[0])

                nc.vector.memset(zeros[:], 0.0).then_inc(zeros_set, 1)
                nc.vector.memset(ones3[:], 1.0)
                nc.vector.memset(per_hi[:], 0.0)
                link(nc.vector.memset(violations[:], 0.0))
                dve.wait_ge(dst_loaded, 16 * 5)
                nc.vector.tensor_copy(curf[:], cur[:])
                nc.vector.tensor_copy(nxtf[:], nxt[:])
                nc.vector.tensor_copy(firsts[:], ends[:, 0, :])
                nc.vector.tensor_copy(lastf[:], ends[:, 1, :])
                nc.vector.tensor_scalar(hi_lo[:, 0, :], cur[:], 12, None, ALU.logical_shift_right)
                link(nc.vector.tensor_scalar(hi_lo[:, 1, :], cur[:], 7, LO - 1, ALU.logical_shift_right, ALU.bitwise_and))
                link(nc.vector.tensor_copy(hi_lof[:], hi_lo[:]))
                dve.wait_ge(consts_loaded, 16)
                nc.vector.tensor_tensor(hot_hi[:], iota[:, 0:HI].unsqueeze(1).broadcast_to([P, TILES, HI]),
                                        hi_lof[:, 0, :].unsqueeze(2).broadcast_to([P, TILES, HI]), ALU.is_equal)
                nc.vector.tensor_tensor(hot_lo[:], iota[:, 0:LO].unsqueeze(1).broadcast_to([P, TILES, LO]),
                                        hi_lof[:, 1, :].unsqueeze(2).broadcast_to([P, TILES, LO]), ALU.is_equal).then_inc(hots_ready, 1)
                dve.wait_ge(weights_loaded, 16 * (len(weights) + len(rows)))
                link(nc.vector.tensor_tensor(bad[:], curf[:], nxtf[:], ALU.is_gt))
                link(nc.vector.tensor_reduce(out=violations[:, 0:1], in_=bad[:], axis=AX.X, op=ALU.add))
                link(nc.vector.tensor_tensor(bad[:], lastf[:], firsts[:], ALU.subtract))
                link(nc.vector.tensor_scalar(curf[:], bad[:], float(SPAN - 1), None, ALU.is_gt))
                link(nc.vector.tensor_reduce(out=violations[:, 1:2], in_=curf[:], axis=AX.X, op=ALU.add))
                nc.vector.tensor_copy(src_f[:], src_cols[:])
                nc.vector.tensor_copy(dst_f[:], dst_cols[:])
                for k, b in enumerate((bf2, bm2, bself)):
                    link(nc.vector.tensor_copy(partb[:, 3 * k, :], b[:]))
                    link(nc.vector.tensor_copy(part[:, 3 * k, :], partb[:, 3 * k, :]))
                    link(nc.vector.tensor_tensor(part[:, 3 * k + 1, :], b[:], part[:, 3 * k, :], ALU.subtract))
                    link(nc.vector.tensor_copy(partb[:, 3 * k + 1, :], part[:, 3 * k + 1, :]))
                    link(nc.vector.tensor_copy(part[:, 3 * k + 2, :], partb[:, 3 * k + 1, :]))
                    link(nc.vector.tensor_tensor(part[:, 3 * k + 2, :], part[:, 3 * k + 1, :], part[:, 3 * k + 2, :], ALU.subtract))
                    link(nc.vector.tensor_copy(part[:, 3 * k + 1, :], partb[:, 3 * k + 1, :]))
                    link(nc.vector.tensor_scalar(part[:, 3 * k, :], part[:, 3 * k, :], third[:, 0:1], None, ALU.mult))
                    link(nc.vector.scalar_tensor_tensor(out=part[:, 3 * k, :], in0=part[:, 3 * k + 1, :], scalar=third[:, 1:2],
                                                        in1=part[:, 3 * k, :], op0=ALU.mult, op1=ALU.add))
                    link(nc.vector.scalar_tensor_tensor(out=part[:, 3 * k, :], in0=part[:, 3 * k + 2, :], scalar=third[:, 2:3],
                                                        in1=part[:, 3 * k, :], op0=ALU.mult, op1=ALU.add))
                    nc.vector.tensor_copy(bias3[:, k, :].rearrange("p (t c) -> p t c", t=QT), part[:, 3 * k, :].unsqueeze(1).broadcast_to([P, QT, C]))
                for k, b in enumerate((bf1, bm1)):
                    nc.vector.tensor_scalar(cols[:, 5 + 2 * k:6 + 2 * k], b, -1.0, TOP, ALU.mult, ALU.add)
                    link(nc.vector.tensor_scalar(cols[:, 6 + 2 * k:7 + 2 * k], b, -LOG2, None, ALU.add))
                dve.wait_ge(counted4, 1)
                link(nc.vector.tensor_copy(by4[:], bank[0][:, 0:4 * HI]))
                link(nc.vector.tensor_scalar(count_cols[:, 0, :], by4[:, 0:HI], quarter[:, 0:1], None, ALU.mult))
                for a in range(1, 4):
                    last = nc.vector.scalar_tensor_tensor(out=count_cols[:, a, :], in0=by4[:, a * HI:(a + 1) * HI], scalar=quarter[:, a:a + 1],
                                                          in1=count_cols[:, a - 1, :], op0=ALU.mult, op1=ALU.add)
                    if a < 3:
                        link(last)
                last.then_inc(by4_ready, 1)
                dve.wait_ge(sums_ready, 1)
                nc.vector.tensor_copy(per_hi[0:HI, :], bank[1][0:HI, 0:LO]).then_inc(per_hi_ready, 1)
                link(nc.vector.tensor_scalar(too_many[:, 0, :], bank[2][0:HI, 0:LO], float(SPAN), None, ALU.is_gt))
                link(nc.vector.tensor_reduce(out=violations[0:HI, 2:3], in_=too_many[:, 0, :], axis=AX.X, op=ALU.add))
                dve.wait_ge(starts_summed, 1)
                nc.vector.tensor_copy(starts[:], bank[3][0:HI, 0:LO]).then_inc(starts_ready, 1)
                link(nc.vector.tensor_tensor(too_many[:, 1, :], bank[3][0:HI, 0:LO], last_start[0:HI, :], ALU.is_gt))
                link(nc.vector.tensor_reduce(out=violations[0:HI, 3:4], in_=too_many[:, 1, :], axis=AX.X, op=ALU.add))
                nc.vector.tensor_reduce(out=violated[:], in_=violations[:], axis=AX.X, op=ALU.add).then_inc(violated_ready, 1)
                dve.wait_ge(total_ready, 1)
                nc.vector.tensor_copy(flag[0:1, 0:1], bank[4][0:1, 0:1]).then_inc(flag_ready, 1)

            @block.tensor
            def _(pe):
                pe.wait_ge(hots_ready, 1)
                for q in range(QUADS):
                    last = nc.tensor.matmul(bank[0][:, 0:4 * HI], hot_lo[:, QT * q:QT * q + QT, :].rearrange("p t l -> p (t l)"),
                                            hot_hi[:, QT * q:QT * q + QT, :].rearrange("p t h -> p (t h)"), start=(q == 0), stop=(q == QUADS - 1))
                last.then_inc(counted4, 1)
                pe.wait_ge(by4_ready, 1)
                counts_by_block = count_cols[:, 3, :]
                nc.tensor.matmul(bank[1][0:HI, 0:LO], counts_by_block, ones[:, 0:LO], start=True, stop=True)
                nc.tensor.matmul(bank[2][0:HI, 0:LO], counts_by_block, eye32, start=True, stop=True).then_inc(sums_ready, 1)
                nc.tensor.matmul(bank[3][0:HI, 0:LO], counts_by_block, upper32, start=True, stop=False)
                pe.wait_ge(per_hi_ready, 1)
                nc.tensor.matmul(bank[3][0:HI, 0:LO], upper_hi[:, 0:HI], per_hi[:], start=False, stop=True).then_inc(starts_summed, 1)
                pe.wait_ge(violated_ready, 1)
                nc.tensor.matmul(bank[4][0:1, 0:1], violated[:], ones[:, 0:1], start=True, stop=True).then_inc(total_ready, 1)

        ZEROED = 16 * (CHAINS * QUADS // 2)

        unfit = nc.values_load(flag[0:1, 0:1], min_val=0, max_val=1 << 30, skip_runtime_bounds_check_because="a count of violations")
        with nc.If(unfit == 0):
            with ExitStack() as sems:
                def sa(name):
                    return sems.enter_context(nc.semaphore("a_" + name))

                def sa2(name):
                    return [sa(f"{name}{p}") for p in range(2)]

                src_ready, gathered, ew_loaded = sa("src_ready"), sa2("gathered"), sa("ew_loaded")
                win_loaded, x_loaded, msg_stored = sa2("win_loaded"), sa2("x_loaded"), sa2("msg_stored")
                h1_stored, y_stored = sa2("h1_stored"), sa2("y_stored")
                squared, basis_ready = sa("squared"), sa("basis_ready")
                e_stats, e_aggr, e_ln, e_root = sa("e_stats"), sa("e_aggr"), sa("e_ln"), sa("e_root")
                e_square, e_ratio, e_factor, e_rstd, e_shift = sa("e_square"), sa("e_ratio"), sa("e_factor"), sa("e_rstd"), sa("e_shift")
                e_norm, e_turned, e_hT, e_proj = sa("e_norm"), sa("e_turned"), sa("e_hT"), sa("e_proj")
                e_u, e_clamp, e_exp, e_softln, e_soft = sa("e_u"), sa("e_clamp"), sa("e_exp"), sa("e_softln"), sa("e_soft")
                e_filter, e_filter_sb, e_dst, e_msg = sa("e_filter"), sa("e_filter_sb"), sa("e_dst"), sa("e_msg")
                n_rel, n_hot, n_agg, n_aggT = sa("n_rel"), sa("n_hot"), sa("n_agg"), sa("n_aggT")
                n_u, n_clamp, n_exp, n_softln, n_soft, n_mlp, n_x1 = (sa("n_u"), sa("n_clamp"), sa("n_exp"), sa("n_softln"), sa("n_soft"),
                                                                      sa("n_mlp"), sa("n_x1"))
                n_stats, n_aggr, n_ln, n_root = sa("n_stats"), sa("n_aggr"), sa("n_ln"), sa("n_root")
                n_square, n_ratio, n_factor, n_rstd = sa("n_square"), sa("n_ratio"), sa("n_factor"), sa("n_rstd")
                n_norm, n_h1, n_turned, n_hT, n_self, n_y = sa("n_norm"), sa("n_h1"), sa("n_turned"), sa("n_hT"), sa("n_self"), sa("n_y")
                u_ps, turn_ps, proj_ps, filt_ps, agg_ps, nu_ps, mlp_ps, self_ps = bank
                nlnv, nroot, nsquare, nratio, nfactor, nrstd = (nsmall[:, k, :] for k in range(6))
                block = sems.enter_context(nc.Block())

                @block.sync
                def _(sp):
                    def load_ew(j):
                        if not at_first(j, 1):
                            sp.wait_ge(squared, j)
                            hold(sp, sp_passed)
                        for half in range(2):
                            sp.dma_start(ew[64 * half:64 * half + 64, 0, :], ins["ew_rows"][2 * j + half, :].partition_broadcast(64)).then_inc(ew_loaded, 16)

                    def load_x(j, par):
                        if not at_first(j, 2):
                            sp.wait_ge(n_x1, j - 1)
                            hold(sp, sp_passed)
                        sp.dma_start(nx[:, par, :, :], tiles_of(ins["x"], j, C)).then_inc(x_loaded[par], 16)

                    def store_h1(j, par):
                        sp.wait_ge(n_h1, j + 1)
                        hold(sp, sp_passed)
                        sp.dma_start(tiles_of(h1_dram, j, C), h1s[:, par, :, :]).then_inc(h1_stored[par], 16)

                    def store_msg(q, par):
                        sp.wait_ge(e_msg, q + 1)
                        hold(sp, sp_passed)
                        sp.dma_start(tiles_of(msg_dram, q, MW), msgw[:, par, :, :]).then_inc(msg_stored[par], 16)

                    def store_y(j, par):
                        sp.wait_ge(n_y, j + 1)
                        hold(sp, sp_passed)
                        sp.dma_start(tiles_of(y_dram, j, C), ys[:, par, :, :]).then_inc(y_stored[par], 16)

                    def load_windows(j, par):
                        for p in range(2):
                            up_to = j + AHEAD if p == par else j + AHEAD - 1
                            if isinstance(up_to, int):
                                up_to = min(up_to, QUADS - 2 + p)
                            sp.wait_ge(msg_stored[p], half_count(up_to, p, 16))
                            hold(sp, sp_passed)
                        if not at_first(j, 2):
                            sp.wait_ge(n_agg, j - 1)
                            hold(sp, sp_passed)
                        starts_of = [sp.value_load(start_row[0:1, bass.ds(4 * j + k, 1)], min_val=0, max_val=ROWS) for k in range(QT)]
                        for k, start in enumerate(starts_of):
                            sp.dma_start(win[:, par, k, :, :], msg_dram[bass.ds(start, SPAN), :].rearrange("(w p) c -> p w c", p=P)).then_inc(win_loaded[par], 16)

                    def step(s, even, odd, pair, slot):
                        if there(s - 10):
                            load_x(s - 10, even)
                        if there(s - 12):
                            store_y(s - 12, even)
                        if even == 0 and there(s):
                            load_ew(pair)
                        if there(s - 7):
                            load_windows(s - 7, odd)
                        if there(s - 11):
                            store_h1(s - 11, odd)
                        if there(s - 3):
                            store_msg(s - 3, odd)
                    over_steps(sp, step)
                    for p in range(2):
                        sp.wait_ge(h1_stored[p], 16 * (QUADS // 2))
                        sp.wait_ge(y_stored[p], 16 * (QUADS // 2))

                @block.gpsimd
                def _(pool):
                    def gather(q, par, t):
                        if t == 0:
                            pool.wait_ge(src_ready, q + 1)
                            wait_used(pool, e_norm, q, 2)
                        hold(pool, pool_passed)
                        nc.gpsimd.indirect_dma_start(
                            out=xg[:, par, t, :], out_offset=None, in_=ins["x"],
                            in_offset=bass.IndirectOffsetOnAxis(ap=srcs[:, par, t:t + 1], axis=0)).then_inc(gathered[par], 16)

                    def node_relu(j, par):
                        pool.wait_ge(n_norm, j + 1)
                        wait_used(pool, n_turned, j, 2)
                        if not at_first(j, 2):
                            pool.wait_ge(h1_stored[par], half_count(j, par, 16) - 16)
                        hold(pool, pool_passed)
                        nc.gpsimd.tensor_scalar(flat(h1s, par), nxn.rearrange("p t c -> p (t c)"), 0.0, None, ALU.max).then_inc(n_h1, 1)

                    def zero_rows(table, pair):
                        pool.dma_start(table[0:ROWS, :].rearrange("(j p t) c -> j p (t c)", p=P, t=2 * QT)[pair, :, :],
                                       zeros[:, 0:2 * QT * W2]).then_inc(tables_zeroed, 16)

                    def step(s, even, odd, pair, slot):
                        if there(s - 1):
                            gather(s - 1, odd, 3)
                        if there(s - 11):
                            node_relu(s - 11, odd)
                        if there(s):
                            zero_rows(agg2[even], pair)
                            for t in range(3):
                                gather(s, even, t)
                    over_steps(pool, step)

                @block.vector
                def _(dve):
                    def take_src(q, par):
                        nc.vector.tensor_copy(srcs[:, par, :], src_cols[:, bass.ds(QT * q, QT)]).then_inc(src_ready, 1)

                    def row_stats(source, stats_, done):
                        for t in range(QT):
                            last = nc.vector.bn_stats(out=stats_[:, t, :], in_=source[:, t, :])
                        last.then_inc(done, 1)

                    def row_aggr(q, stats_, mv_, has_stats, done):
                        dve.wait_ge(has_stats, q + 1)
                        hold(dve, dve_passed)
                        for t in range(QT):
                            last = nc.vector.bn_aggr(out=mv_[:, t, :], in_=stats_[:, t, :])
                        last.then_inc(done, 1)

                    def square_root(q, root, out, has_root, done):
                        dve.wait_ge(has_root, q + 1)
                        nc.vector.tensor_tensor(out, root, root, ALU.mult).then_inc(done, 1)

                    def times_var(q, mv_, squared_root, out, has_square, done):
                        dve.wait_ge(has_square, q + 1)
                        nc.vector.scalar_tensor_tensor(out=out, in0=mv_[:, :, 1], scalar=eps, in1=squared_root,
                                                       op0=ALU.add, op1=ALU.mult).then_inc(done, 1)

                    def correction(q, ratio, out, has_ratio, done):
                        dve.wait_ge(has_ratio, q + 1)
                        nc.vector.tensor_scalar(out, ratio, -0.5, 1.5, ALU.mult, ALU.add).then_inc(done, 1)

                    def inverse_root(q, factor, root, out, has_factor, used, done):
                        dve.wait_ge(has_factor, q + 1)
                        if used is not None:
                            wait_used(dve, used, q, 1)
                        nc.vector.tensor_tensor(out, factor, root, ALU.mult).then_inc(done, 1)

                    def mean_shift(q, mv_, rstd_, out, has_rstd, done):
                        dve.wait_ge(has_rstd, q + 1)
                        nc.vector.scalar_tensor_tensor(out=out, in0=mv_[:, :, 0], scalar=minus_one, in1=rstd_,
                                                       op0=ALU.mult, op1=ALU.mult).then_inc(done, 1)

                    def soften(q, ups, low, l, out, has_l, used, done):
                        dve.wait_ge(has_l, q + 1)
                        wait_used(dve, used, q, 1)
                        nc.vector.scalar_tensor_tensor(out=out, in0=ups, scalar=low, in1=l, op0=ALU.add, op1=ALU.max).then_inc(done, 1)

                    def dst_column(q, par):
                        if not at_first(q, 2):
                            dve.wait_ge(msg_stored[par], half_count(q, par, 16) - 16)
                        nc.vector.tensor_copy(msgw[:, par, :, C], dst_f[:, bass.ds(QT * q, QT)]).then_inc(e_dst, 1)

                    def message(q, par):
                        dve.wait_ge(e_proj, q + 1)
                        dve.wait_ge(e_filter_sb, q + 1)
                        nc.vector.tensor_tensor(msgw[:, par, :, 0:C], proj_ps[:].rearrange("p (t c) -> p t c", t=QT),
                                                efs[:].rearrange("p (t c) -> p t c", t=QT), ALU.mult).then_inc(e_msg, 1)

                    def window_dst(j, par):
                        dve.wait_ge(win_loaded[par], half_count(j, par, 64))
                        nc.vector.tensor_scalar(rel[:], win[:, par, :, :, C], qbase[:, bass.ds(j, 1)], None, ALU.subtract).then_inc(n_rel, 1)

                    def one_hots(j):
                        dve.wait_ge(n_rel, j + 1)
                        wait_used(dve, n_agg, j, 1)
                        nc.vector.tensor_tensor(hot[:], iota4[:].rearrange("p (t c) -> p t c", t=QT).unsqueeze(2).broadcast_to([P, QT, 2, P]),
                                                rel[:].unsqueeze(3).broadcast_to([P, QT, 2, P]), ALU.is_equal).then_inc(n_hot, 1)

                    def node_norm(j, par):
                        dve.wait_ge(n_rstd, j + 1)
                        wait_used(dve, n_h1, j, 1)
                        for t in range(QT):
                            last = nc.vector.tensor_scalar(nxn[:, t, :], x1[:, par, t, :], nmv[:, t, 0:1], nrstd[:, t:t + 1], ALU.subtract, ALU.mult)
                        last.then_inc(n_norm, 1)

                    def residual(j, par):
                        dve.wait_ge(x_loaded[par], half_count(j, par, 16))
                        dve.wait_ge(n_mlp, j + 1)
                        wait_used(dve, n_y, j, 2)
                        nc.vector.tensor_tensor(flat(x1, par), mlp_ps[:], flat(nx, par), ALU.add).then_inc(n_x1, 1)

                    def node_out(j, par):
                        if not at_first(j, 2):
                            dve.wait_ge(y_stored[par], half_count(j, par, 16) - 16)
                        dve.wait_ge(n_self, j + 1)
                        nc.vector.tensor_tensor(flat(ys, par), self_ps[:], flat(x1, par), ALU.add).then_inc(n_y, 1)

                    def step(s, even, odd, pair, slot):
                        if there(s - 8):
                            one_hots(s - 8)
                        if there(s - 3):
                            message(s - 3, odd)
                        if there(s - 10):
                            square_root(s - 10, nroot, nsquare, n_root, n_square)
                        if there(s - 1):
                            square_root(s - 1, root[:], square[:], e_root, e_square)
                        if there(s - 10):
                            times_var(s - 10, nmv, nsquare, nratio, n_square, n_ratio)
                        if there(s - 2):
                            dst_column(s - 2, even)
                        if there(s - 1):
                            times_var(s - 1, emv[:, odd, :, :], square[:], ratio[:], e_square, e_ratio)
                        if there(s - 9):
                            soften(s - 9, nu_ps[:], bm1_low, nlu[:], nsu[:], n_softln, n_mlp, n_soft)
                        if there(s - 10):
                            correction(s - 10, nratio, nfactor, n_ratio, n_factor)
                        if there(s - 1):
                            correction(s - 1, ratio[:], factor[:], e_ratio, e_factor)
                        if there(s - 11):
                            node_out(s - 11, odd)
                        if there(s - 1):
                            inverse_root(s - 1, factor[:], root[:], rstd[:], e_factor, e_norm, e_rstd)
                        if there(s - 10):
                            inverse_root(s - 10, nfactor, nroot, nrstd, n_factor, None, n_rstd)
                        if there(s - 7):
                            window_dst(s - 7, odd)
                        if there(s - 10):
                            node_norm(s - 10, even)
                        if there(s - 1):
                            mean_shift(s - 1, emv[:, odd, :, :], rstd[:], shift[:], e_rstd, e_shift)
                            soften(s - 1, u_ps[:], bf1_low, ln_out[:], su[:], e_softln, e_filter, e_soft)
                        if there(s - 9):
                            residual(s - 9, odd)
                        if there(s):
                            dve.wait_ge(gathered[even], half_count(s, even, 64))
                            row_stats(xg[:, even, :, :], stats, e_stats)
                            if there(s + 2):
                                take_src(s + 2, even)
                        if there(s - 9):
                            dve.wait_ge(n_x1, s - 9 + 1)
                            row_stats(x1[:, odd, :, :], nstats, n_stats)
                        if there(s):
                            wait_used(dve, e_ln, s, 2)
                            row_aggr(s, stats, emv[:, even, :, :], e_stats, e_aggr)
                        if there(s - 9):
                            wait_used(dve, n_ln, s - 9, 1)
                            row_aggr(s - 9, nstats, nmv, n_stats, n_aggr)
                    take_src(0, 0)
                    take_src(1, 1)
                    over_steps(dve, step)

                @block.scalar
                def _(act):
                    coef = 1.0 / (2.0 * float(CENTERS[1] - CENTERS[0]) ** 2)
                    half = cols[:, 4:5]

                    def make_basis(j, slot):
                        act.wait_ge(ew_loaded, 32 * j + 32)
                        nc.scalar.activation(distance, ew[:, 0, :], ACT.Square, bias=negc).then_inc(squared, 1)
                        act.wait_ge(squared, j + 1)
                        if not at_first(j, 2):
                            act.wait_ge(e_u, 2 * j - 2)
                        nc.scalar.activation(basis[:, slot, :], distance, ACT.Exp, scale=-coef).then_inc(basis_ready, 1)

                    def clamp(q, ups, high, c, has_u, done):
                        act.wait_ge(has_u, q + 1)
                        nc.scalar.activation(c, ups, ACT.Relu, bias=high, scale=-1.0).then_inc(done, 1)

                    def exponential(q, c, e, has_c, done):
                        act.wait_ge(has_c, q + 1)
                        nc.scalar.activation(e, c, ACT.Exp, bias=top, scale=-1.0).then_inc(done, 1)

                    def logarithm(q, e, l, has_e, soft, done):
                        act.wait_ge(has_e, q + 1)
                        wait_used(act, soft, q, 1)
                        nc.scalar.activation(l, e, ACT.Ln, bias=half, scale=0.5).then_inc(done, 1)

                    def log_var(q, mv_, l, has_var, done):
                        act.wait_ge(has_var, q + 1)
                        nc.scalar.activation(l, mv_[:, :, 1], ACT.Ln, bias=eps).then_inc(done, 1)

                    def first_root(q, l, out, has_ln, used, done):
                        act.wait_ge(has_ln, q + 1)
                        wait_used(act, used, q, 1)
                        nc.scalar.activation(out, l, ACT.Exp, scale=-0.5).then_inc(done, 1)

                    def norm_relu(source, rstd_, shift_, out, done):
                        for t in range(QT):
                            last = nc.scalar.activation(out[:, t, :], source[:, t, :], ACT.Relu, bias=shift_[:, t:t + 1], scale=rstd_[:, t:t + 1])
                        last.then_inc(done, 1)

                    def evacuate(q, out, ps, ready, used, done):
                        act.wait_ge(ready, q + 1)
                        wait_used(act, used, q, 1)
                        nc.scalar.activation(out, ps, ACT.Copy).then_inc(done, 1)

                    nc.scalar.preload_act_table_set("natural_log_exp_and_others")
                    def step(s, even, odd, pair, slot):
                        if there(s - 9):
                            evacuate(s - 9, aggs[:], agg_ps[:], n_agg, n_u, n_aggT)
                        if there(s - 3):
                            evacuate(s - 3, hT[:], turn_ps[:], e_turned, e_proj, e_hT)
                            evacuate(s - 3, efs[:], filt_ps[:], e_filter, e_msg, e_filter_sb)
                        if there(s - 2):
                            act.wait_ge(e_shift, s - 2 + 1)
                            wait_used(act, e_turned, s - 2, 1)
                            norm_relu(xg[:, even, :, :], rstd, shift, xn, e_norm)
                        if there(s - 9):
                            clamp(s - 9, nu_ps[:], bm1_top, nclamp[:], n_u, n_clamp)
                        if there(s - 11):
                            evacuate(s - 11, nhT[:], turn_ps[:], n_turned, n_self, n_hT)
                        if there(s - 1):
                            log_var(s - 1, emv[:, odd, :, :], lnv[:], e_aggr, e_ln)
                        if there(s - 10):
                            log_var(s - 10, nmv, nlnv, n_aggr, n_ln)
                        if there(s - 9):
                            exponential(s - 9, nclamp[:], neu[:], n_clamp, n_exp)
                        if there(s - 10):
                            first_root(s - 10, nlnv, nroot, n_ln, n_rstd, n_root)
                        if there(s - 1):
                            first_root(s - 1, lnv[:], root[:], e_ln, e_rstd, e_root)
                        if there(s - 9):
                            logarithm(s - 9, neu[:], nlu[:], n_exp, n_soft, n_softln)
                        if there(s - 1):
                            clamp(s - 1, u_ps[:], bf1_top, clampu[:], e_u, e_clamp)
                            exponential(s - 1, clampu[:], eu[:], e_clamp, e_exp)
                        if even == 0 and there(s):
                            make_basis(pair, slot)
                        if there(s - 1):
                            logarithm(s - 1, eu[:], ln_out[:], e_exp, e_soft, e_softln)
                    over_steps(act, step)

                @block.tensor
                def _(pe):
                    def product(q, ps, left, weights_, b, has_left, used, done):
                        pe.wait_ge(has_left, q + 1)
                        wait_used(pe, used, q, 1)
                        if b is not None:
                            nc.tensor.matmul(ps[:], ones3[0:3, :], bias3[0:3, b, :], start=True, stop=False)
                        for t in range(QT):
                            last = nc.tensor.matmul(ps[:, t * P:(t + 1) * P], left[:, t * P:(t + 1) * P], weights_[:],
                                                    start=(b is None), stop=(b is None or t == QT - 1))
                        last.then_inc(done, 1)

                    def turn(source, done):
                        for t in range(QT):
                            last = nc.tensor.transpose(turn_ps[:, t * P:(t + 1) * P], source[:, t, :], ident[:])
                        last.then_inc(done, 1)

                    def filter_up(q, par, pair, slot):
                        pe.wait_ge(basis_ready, pair + 1)
                        wait_used(pe, e_soft, q, 1)
                        at = BASIS_AT[par]
                        nc.tensor.matmul(u_ps[:], wf1[at:at + BASIS, :], basis[at:at + BASIS, slot, :], start=True, stop=True).then_inc(e_u, 1)

                    def block_sums(j, par):
                        pe.wait_ge(n_hot, j + 1)
                        pe.wait_ge(win_loaded[par], half_count(j, par, 64))
                        wait_used(pe, n_aggT, j, 1)
                        for k in range(QT):
                            for w in range(2):
                                last = nc.tensor.matmul(agg_ps[:, k * P:(k + 1) * P], win[:, par, k, w, 0:C], hot[:, k, w, :],
                                                        start=(w == 0), stop=(w == 1))
                        last.then_inc(n_agg, 1)

                    def step(s, even, odd, pair, slot):
                        if there(s - 11):
                            product(s - 11, self_ps, nhT, wself, 2, n_hT, n_y, n_self)
                        if there(s - 8):
                            block_sums(s - 8, even)
                        if there(s - 9):
                            product(s - 9, mlp_ps, nsu, wm2, 1, n_soft, n_x1, n_mlp)
                        if there(s - 8):
                            pe.wait_ge(n_aggT, s - 8 + 1)
                            wait_used(pe, n_soft, s - 8, 1)
                            nc.tensor.matmul(nu_ps[:], wm1[:], aggs[:], start=True, stop=True).then_inc(n_u, 1)
                        if there(s):
                            filter_up(s, even, pair, slot)
                        if there(s - 10):
                            pe.wait_ge(n_h1, s - 10 + 1)
                            if there(s - 2):
                                pe.wait_ge(e_hT, s - 2 + 1)
                            wait_used(pe, n_hT, s - 10, 1)
                            turn(h1s[:, even, :, :], n_turned)
                        if there(s - 2):
                            product(s - 2, proj_ps, hT, wlin, None, e_hT, e_msg, e_proj)
                        if there(s - 1):
                            product(s - 1, filt_ps, su, wf2, 0, e_soft, e_filter_sb, e_filter)
                            pe.wait_ge(e_norm, s - 1 + 1)
                            if there(s - 10):
                                pe.wait_ge(n_hT, s - 10 + 1)
                            wait_used(pe, e_hT, s - 1, 1)
                            turn(xn, e_turned)
                    over_steps(pe, step)

            with ExitStack() as sems:
                def sbm(name):
                    return sems.enter_context(nc.semaphore("b_" + name))

                keys_loaded, win_loaded = ([sbm(f"{n}{p}") for p in range(2)] for n in ("keys_loaded", "win_loaded"))
                added = [sbm(f"added{k}") for k in range(CHAINS)]
                keyf, same_ready, counted = sbm("keyf"), sbm("same_ready"), sbm("counted")
                before_ready, spare_ready, target_ready = sbm("before_ready"), sbm("spare_ready"), sbm("target_ready")
                rel0, rel1, hot_ready, pick_ready, picksb = sbm("rel0"), sbm("rel1"), sbm("hot_ready"), sbm("pick_ready"), sbm("picksb")
                sumT_ready, sT_ready, neigh_ready, comb_ready = sbm("sumT_ready"), sbm("sT_ready"), sbm("neigh_ready"), sbm("comb_ready")
                pick_ps, sumT_ps, neigh_ps = (bank[0], bank[1]), bank[2], bank[3]
                sameb = sems.enter_context(nc.sbuf_tensor("sameb", [P, QT, P], bf16))
                hotb = sems.enter_context(nc.sbuf_tensor("hotb", [P, QT, 2, P], bf16))
                pick = sems.enter_context(nc.sbuf_tensor("pick", [P, 2, QT, P], f32))
                hwin = win[:, :, :, :, 0:C]
                block = sems.enter_context(nc.Block())

                @block.sync
                def _(sp):
                    def load(q, par):
                        if not at_first(q, 2):
                            sp.wait_ge(same_ready, q - 1)
                            hold(sp, sp_passed)
                        sp.dma_start(key_rows[:, par, :], ins["src_rows"][q, :].partition_broadcast(P)).then_inc(keys_loaded[par], 16)
                        if not at_first(q, 2):
                            sp.wait_ge(sumT_ready, q - 1)
                            hold(sp, sp_passed)
                        for t in range(QT):
                            first = sp.value_load(first_row[0:1, bass.ds(4 * q + t, 1)], min_val=0, max_val=ROWS - 1)
                            sp.dma_start(hwin[:, par, t, :, :], h1_dram[bass.ds(first, SPAN), :].rearrange("(w p) c -> p w c", p=P)).then_inc(win_loaded[par], 16)
                    over_quads(sp, load)

                @block.gpsimd
                def _(pool):
                    pool.wait_ge(tables_zeroed, ZEROED)

                    def step(q, par):
                        pool.wait_ge(comb_ready, q + 1)
                        pool.wait_ge(target_ready, q + 1)
                        for t in range(QT):
                            k = t % CHAINS
                            n = 32 * q + 16 * (t // CHAINS)
                            if not (isinstance(n, int) and n == 0):
                                pool.wait_ge(added[k], n)
                            hold(pool, pool_passed)
                            nc.gpsimd.indirect_dma_start(
                                out=agg2[k], out_offset=bass.IndirectOffsetOnAxis(ap=target[:, par, t:t + 1], axis=0),
                                in_=comb[:, par, t, :], in_offset=None, compute_op=ALU.add).then_inc(added[k], 16)
                    over_quads(pool, step)
                    for k in range(CHAINS):
                        pool.wait_ge(added[k], 32 * QUADS)

                @block.vector
                def _(dve):
                    for par in range(2):
                        nc.vector.memset(comb[:, par, :, C:W2], 0.0)

                    def front(q, par):
                        wait_used(dve, target_ready, q, 2)
                        nc.vector.tensor_copy(idxf[:, par, :], src_f[:, bass.ds(QT * q, QT)]).then_inc(keyf, 1)
                        nc.vector.tensor_tensor(rel[:, :, 0], dst_f[:, bass.ds(QT * q, QT)], firsts[:, bass.ds(QT * q, QT)], ALU.subtract).then_inc(rel0, 1)
                        dve.wait_ge(rel0, q + 1)
                        nc.vector.tensor_scalar(rel[:, :, 1], rel[:, :, 0], -float(P), None, ALU.add).then_inc(rel1, 1)
                        dve.wait_ge(keyf, q + 1)
                        dve.wait_ge(keys_loaded[par], half_count(q, par, 16))
                        wait_used(dve, pick_ready, q, 1)
                        for t in range(QT):
                            last = nc.vector.tensor_scalar(sameb[:, t, :], key_rows[:, par, t * P:(t + 1) * P], idxf[:, par, t:t + 1], None, ALU.is_equal)
                        last.then_inc(same_ready, 1)
                        dve.wait_ge(rel1, q + 1)
                        nc.vector.tensor_tensor(hotb[:], iota.unsqueeze(1).unsqueeze(1).broadcast_to([P, QT, 2, P]),
                                                rel[:].unsqueeze(3).broadcast_to([P, QT, 2, P]), ALU.is_equal).then_inc(hot_ready, 1)
                        dve.wait_ge(same_ready, q + 1)
                        for t in range(QT):
                            last = nc.vector.tensor_tensor_reduce(out=junk[:, t, :], in0=sameb[:, t, :], in1=lower[:], scale=1.0,
                                                                  scalar=0.0, op0=ALU.mult, op1=ALU.add, accum_out=before[:, par, t:t + 1])
                        last.then_inc(before_ready, 1)
                        nc.vector.tensor_reduce(out=counts[:, par, :], in_=sameb[:], axis=AX.X, op=ALU.add).then_inc(counted, 1)
                        dve.wait_ge(before_ready, q + 1)
                        nc.vector.tensor_scalar(spare[:, par, :], before[:, par, :], 1.0, dump, ALU.min, ALU.mult).then_inc(spare_ready, 1)

                    def back(q, par):
                        dve.wait_ge(spare_ready, q + 1)
                        if not at_first(q, 2):
                            for k in range(CHAINS):
                                dve.wait_ge(added[k], 32 * (q - 1))
                        nc.vector.tensor_copy(comb[:, par, :, C], counts[:, par, :])
                        nc.vector.tensor_tensor(target[:, par, :], spare[:, par, :], idxf[:, par, :], ALU.max).then_inc(target_ready, 1)

                    front(0, 0)

                    def step(q, par):
                        if exists(q + 1):
                            front(q + 1, 1 - par)
                        back(q, par)
                    over_quads(dve, step)

                @block.tensor
                def _(pe):
                    def front(q):
                        pe.wait_ge(hot_ready, q + 1)
                        wait_used(pe, picksb, q, 1)
                        for w in range(2):
                            for t in range(QT):
                                last = nc.tensor.matmul(pick_ps[w][:, t * P:(t + 1) * P], hotb[:, t, w, :], sameb[:, t, :], start=True, stop=True)
                        last.then_inc(pick_ready, 1)

                    front(0)

                    def step(q, par):
                        pe.wait_ge(win_loaded[par], half_count(q, par, 64))
                        pe.wait_ge(picksb, q + 1)
                        wait_used(pe, sT_ready, q, 1)
                        for t in range(QT):
                            for w in range(2):
                                last = nc.tensor.matmul(sumT_ps[:, t * P:(t + 1) * P], hwin[:, par, t, w, :], pick[:, w, t, :], start=(w == 0), stop=(w == 1))
                        last.then_inc(sumT_ready, 1)
                        if exists(q + 1):
                            front(q + 1)
                        pe.wait_ge(sT_ready, q + 1)
                        wait_used(pe, comb_ready, q, 1)
                        for t in range(QT):
                            last = nc.tensor.matmul(neigh_ps[:, t * P:(t + 1) * P], hT[:, t * P:(t + 1) * P], wneigh[:], start=True, stop=True)
                        last.then_inc(neigh_ready, 1)
                    over_quads(pe, step)

                @block.scalar
                def _(act):
                    def take_pick(q):
                        act.wait_ge(pick_ready, q + 1)
                        wait_used(act, sumT_ready, q, 1)
                        for w in range(2):
                            last = nc.scalar.activation(pick[:, w, :, :].rearrange("p t e -> p (t e)"), pick_ps[w][:], ACT.Copy)
                        last.then_inc(picksb, 1)

                    take_pick(0)

                    def step(q, par):
                        act.wait_ge(sumT_ready, q + 1)
                        wait_used(act, neigh_ready, q, 1)
                        nc.scalar.activation(hT[:], sumT_ps[:], ACT.Copy).then_inc(sT_ready, 1)
                        if exists(q + 1):
                            take_pick(q + 1)
                        act.wait_ge(neigh_ready, q + 1)
                        if not at_first(q, 2):
                            for k in range(CHAINS):
                                act.wait_ge(added[k], 32 * (q - 1))
                        nc.scalar.activation(comb[:, par, :, 0:C], neigh_ps[:].rearrange("p (t c) -> p t c", t=QT), ACT.Copy).then_inc(comb_ready, 1)
                    over_quads(act, step)


        with nc.Else():
            zeroed1 = sem("zeroed1")
            with nc.Block() as block:
                @block.sync
                def _(sp):
                    n = 0
                    for table in agg1:
                        for out, m in zero_parts(table, C, TABLE_ROWS):
                            sp.dma_start(out, zeros[:, 0:m]).then_inc(zeroed1, 16)
                            n += 16
                    for table in agg2:
                        for out, m in zero_parts(table, W2, TABLE_ROWS):
                            sp.dma_start(out, zeros[:, 0:m]).then_inc(zeroed1, 16)
                            n += 16
                    sp.wait_ge(zeroed1, n)

            with ExitStack() as sems:
                def s1(name):
                    return sems.enter_context(nc.semaphore("e1_" + name))
                idx_loaded = [s1(f"idx_loaded{p}") for p in range(2)]
                keys_loaded = [s1(f"keys_loaded{p}") for p in range(2)]
                ew_loaded = s1("ew_loaded")
                gathered = [s1(f"gathered{p}") for p in range(2)]
                added = [s1(f"added{k}") for k in range(CHAINS)]
                squared, basis_ready = s1("squared"), s1("basis_ready")
                stats_ready, aggr_ready, var_ready = s1("stats_ready"), s1("aggr_ready"), s1("var_ready")
                ln_ready, r0_ready = s1("ln_ready"), s1("r0_ready")
                r1_ready, r2_ready, r3_ready, rstd_ready = s1("r1_ready"), s1("r2_ready"), s1("r3_ready"), s1("rstd_ready")
                xn_ready, xnT_ready, hT_ready, hs_ready = s1("xn_ready"), s1("xnT_ready"), s1("hT_ready"), s1("hs_ready")
                u_ready, absu_ready, posu_ready = s1("u_ready"), s1("absu_ready"), s1("posu_ready")
                eu_ready, lu_ready, su_ready, ef_ready = s1("eu_ready"), s1("lu_ready"), s1("su_ready"), s1("ef_ready")
                efb_ready, msg_ready, sum_ready, comb_ready = s1("efb_ready"), s1("msg_ready"), s1("sum_ready"), s1("comb_ready")
                idxf_ready, same_ready = s1("idxf_ready"), s1("same_ready")
                before_ready, spare_ready, target_ready = s1("before_ready"), s1("spare_ready"), s1("target_ready")
                u_ps, xT_ps, hs_ps, ef_ps, sum_ps = bank[0], bank[1], bank[2], bank[3], bank[4]

                block = sems.enter_context(nc.Block())

                @block.sync
                def _(sp):
                    def load(q, par):
                        if not (isinstance(q, int) and q < 2):
                            sp.wait_ge(gathered[par], 64 * ((q - par) // 2) if isinstance(q, int) else 32 * q - 32 * par)
                        hold(sp, sp_passed)
                        wait_used(sp, idxf_ready, q, 2)
                        hold(sp, sp_passed)
                        sp.dma_start(idx[:, par, :, :].rearrange("p a t -> p (a t)"), ins["edge_cols"][q, :, :]).then_inc(idx_loaded[par], 16)
                        wait_used(sp, same_ready, q, 2)
                        hold(sp, sp_passed)
                        sp.dma_start(key_rows[:, par, :], ins["dst_rows"][q, :].partition_broadcast(P)).then_inc(keys_loaded[par], 16)

                    def pair(j, n):
                        if not isinstance(j, int) or j >= 2:
                            sp.wait_ge(squared, j - 1)
                        hold(sp, sp_passed)
                        for half in range(2):
                            sp.dma_start(ew[64 * half:64 * half + 64, n, :],
                                         ins["ew_rows"][2 * j + half, :].partition_broadcast(64)).then_inc(ew_loaded, 16)
                    pair(0, 0)
                    load(0, 0)
                    load(1, 1)
                    with sp.Fori(0, QUADS // 2 - 1) as i:
                        sp.wait_ge(squared, i + 1)
                        hold(sp, sp_passed)
                        for half in range(2):
                            sp.dma_start(ew[64 * half:64 * half + 64, 0, :],
                                         ins["ew_rows"][2 * i + (2 + half), :].partition_broadcast(64)).then_inc(ew_loaded, 16)
                        for par in range(2):
                            q = 2 * i + (2 + par)
                            sp.wait_ge(gathered[par], 64 * i + 64)
                            hold(sp, sp_passed)
                            sp.wait_ge(idxf_ready, 2 * i + (par + 1))
                            hold(sp, sp_passed)
                            sp.dma_start(idx[:, par, :, :].rearrange("p a t -> p (a t)"), ins["edge_cols"][q, :, :]).then_inc(idx_loaded[par], 16)
                            sp.wait_ge(same_ready, 2 * i + (par + 1))
                            hold(sp, sp_passed)
                            sp.dma_start(key_rows[:, par, :], ins["dst_rows"][q, :].partition_broadcast(P)).then_inc(keys_loaded[par], 16)

                @block.gpsimd
                def _(pool):
                    def gather(q, par, t):
                        if t == 0:
                            pool.wait_ge(idx_loaded[par], half_count(q, par, 16))
                            wait_used(pool, xn_ready, q, 2)
                        hold(pool, pool_passed)
                        nc.gpsimd.indirect_dma_start(
                            out=xg[:, par, t, :], out_offset=None, in_=ins["x"],
                            in_offset=bass.IndirectOffsetOnAxis(ap=idx[:, par, 0, t:t + 1], axis=0)).then_inc(gathered[par], 16)

                    def add(q, par, t):
                        if t == 0:
                            pool.wait_ge(comb_ready, q + 1)
                            pool.wait_ge(target_ready, q + 1)
                        k = t % CHAINS
                        n = 32 * q + 16 * (t // CHAINS)
                        if not (isinstance(n, int) and n == 0):
                            pool.wait_ge(added[k], n)
                        hold(pool, pool_passed)
                        nc.gpsimd.indirect_dma_start(
                            out=agg1[k], out_offset=bass.IndirectOffsetOnAxis(ap=target[:, par, t:t + 1], axis=0),
                            in_=comb1[:, par, t, :], in_offset=None, compute_op=ALU.add).then_inc(added[k], 16)

                    for t in range(QT):
                        gather(0, 0, t)
                    for t in range(QT):
                        gather(1, 1, t)

                    def step(q, par):
                        for t in range(QT):
                            add(q, par, t)
                            if exists(q + 2):
                                gather(q + 2, par, t)
                    over_quads(pool, step)
                    for k in range(CHAINS):
                        pool.wait_ge(added[k], 32 * QUADS)

                @block.vector
                def _(dve):
                    def norm_stats(q, par):
                        dve.wait_ge(gathered[par], half_count(q, par, 64))
                        for t in range(QT):
                            last = nc.vector.bn_stats(out=stats[:, t, :], in_=xg[:, par, t, :])
                        last.then_inc(stats_ready, 1)
                        dve.wait_ge(stats_ready, q + 1)
                        hold(dve, dve_passed)
                        for t in range(QT):
                            last = nc.vector.bn_aggr(out=mv[:, t, :], in_=stats[:, t, :])
                        last.then_inc(aggr_ready, 1)
                        dve.wait_ge(aggr_ready, q + 1)
                        wait_used(dve, ln_ready, q, 1)
                        nc.vector.tensor_scalar(ve[:], mv[:, :, 1], LN_EPS, None, ALU.add).then_inc(var_ready, 1)

                    def normalise(q, par):
                        dve.wait_ge(r0_ready, q + 1)
                        nc.vector.tensor_tensor(r1[:], r0[:], r0[:], ALU.mult).then_inc(r1_ready, 1)
                        dve.wait_ge(r1_ready, q + 1)
                        nc.vector.tensor_tensor(r2[:], r1[:], ve[:], ALU.mult).then_inc(r2_ready, 1)
                        dve.wait_ge(r2_ready, q + 1)
                        nc.vector.tensor_scalar(r3[:], r2[:], -0.5, 1.5, ALU.mult, ALU.add).then_inc(r3_ready, 1)
                        dve.wait_ge(r3_ready, q + 1)
                        nc.vector.tensor_tensor(rstd[:], r3[:], r0[:], ALU.mult).then_inc(rstd_ready, 1)
                        dve.wait_ge(rstd_ready, q + 1)
                        wait_used(dve, xnT_ready, q, 1)
                        for t in range(QT):
                            last = nc.vector.tensor_scalar(xn[:, t, :], xg[:, par, t, :], mv[:, t, 0:1], rstd[:, t:t + 1],
                                                           ALU.subtract, ALU.mult)
                        last.then_inc(xn_ready, 1)

                    def keys(q, par):
                        dve.wait_ge(idx_loaded[par], half_count(q, par, 16))
                        nc.vector.tensor_copy(idxf[:, par, :], idx[:, par, 1, :]).then_inc(idxf_ready, 1)
                        dve.wait_ge(idxf_ready, q + 1)
                        dve.wait_ge(keys_loaded[par], half_count(q, par, 16))
                        wait_used(dve, sum_ready, q, 2)
                        for t in range(QT):
                            last = nc.vector.tensor_scalar(same[:, par, t, :], key_rows[:, par, t * P:(t + 1) * P],
                                                           idxf[:, par, t:t + 1], None, ALU.is_equal)
                        last.then_inc(same_ready, 1)
                        dve.wait_ge(same_ready, q + 1)
                        for t in range(QT):
                            last = nc.vector.tensor_tensor_reduce(out=junk[:, t, :], in0=same[:, par, t, :], in1=lower[:], scale=1.0,
                                                                  scalar=0.0, op0=ALU.mult, op1=ALU.add, accum_out=before[:, par, t:t + 1])
                        last.then_inc(before_ready, 1)
                        dve.wait_ge(before_ready, q + 1)
                        nc.vector.tensor_scalar(spare[:, par, :], before[:, par, :], 1.0, dump, ALU.min, ALU.mult).then_inc(spare_ready, 1)
                        dve.wait_ge(spare_ready, q + 1)
                        if not (isinstance(q, int) and q < 2):
                            for k in range(CHAINS):
                                dve.wait_ge(added[k], 32 * (q - 1))
                        nc.vector.tensor_tensor(target[:, par, :], spare[:, par, :], idxf[:, par, :], ALU.max).then_inc(target_ready, 1)

                    def filter_in(q, par):
                        dve.wait_ge(u_ready, q + 1)
                        wait_used(dve, su_ready, q, 1)
                        nc.vector.tensor_scalar(posu[:], u_ps[:], bf1, 0.0, ALU.add, ALU.max).then_inc(posu_ready, 1)

                    def filter_out(q, par):
                        dve.wait_ge(posu_ready, q + 1)
                        dve.wait_ge(lu_ready, q + 1)
                        wait_used(dve, ef_ready, q, 1)
                        nc.vector.tensor_tensor(su[:], posu[:], lu[:], ALU.add).then_inc(su_ready, 1)

                    def message(q, par):
                        dve.wait_ge(ef_ready, q + 1)
                        wait_used(dve, msg_ready, q, 1)
                        nc.vector.tensor_tensor(efb[:].rearrange("p (t c) -> p t c", t=QT), ef_ps[:].rearrange("p (t c) -> p t c", t=QT),
                                                bf2[:].unsqueeze(1).broadcast_to([P, QT, C]), ALU.add).then_inc(efb_ready, 1)
                        dve.wait_ge(efb_ready, q + 1)
                        dve.wait_ge(hs_ready, q + 1)
                        wait_used(dve, sum_ready, q, 1)
                        nc.vector.tensor_tensor(msg[:], hs_ps[:], efb[:], ALU.mult).then_inc(msg_ready, 1)

                    def stage_a(q, par):
                        norm_stats(q, par)
                        filter_in(q, par)
                        normalise(q, par)
                        filter_out(q, par)
                        keys(q, par)
                    stage_a(0, 0)

                    def step(q, par):
                        if exists(q + 1):
                            norm_stats(q + 1, 1 - par)
                        message(q, par)
                        if exists(q + 1):
                            normalise(q + 1, 1 - par)
                            filter_in(q + 1, 1 - par)
                            keys(q + 1, 1 - par)
                            filter_out(q + 1, 1 - par)
                    over_quads(dve, step)

                @block.scalar
                def _(act):
                    coef = 1.0 / (2.0 * float(CENTERS[1] - CENTERS[0]) ** 2)

                    def make_basis(j):
                        act.wait_ge(ew_loaded, 32 * j + 32)
                        if not (isinstance(j, int) and j < 1):
                            act.wait_ge(u_ready, 2 * j)
                        nc.scalar.activation(basis[:, 1, :], ew[:, 0, :], ACT.Square, bias=negc).then_inc(squared, 1)
                        act.wait_ge(squared, j + 1)
                        nc.scalar.activation(basis[:, 0, :], basis[:, 1, :], ACT.Exp, scale=-coef).then_inc(basis_ready, 1)

                    def rstd_start(q):
                        act.wait_ge(var_ready, q + 1)
                        nc.scalar.activation(lnv[:], ve[:], ACT.Ln).then_inc(ln_ready, 1)
                        act.wait_ge(ln_ready, q + 1)
                        wait_used(act, rstd_ready, q, 1)
                        nc.scalar.activation(r0[:], lnv[:], ACT.Exp, scale=-0.5).then_inc(r0_ready, 1)

                    def softplus(q):
                        act.wait_ge(posu_ready, q + 1)
                        wait_used(act, eu_ready, q, 1)
                        nc.scalar.activation(absu[:], u_ps[:], ACT.Abs, bias=bf1).then_inc(absu_ready, 1)
                        act.wait_ge(absu_ready, q + 1)
                        nc.scalar.activation(eu[:], absu[:], ACT.Exp, scale=-1.0).then_inc(eu_ready, 1)
                        act.wait_ge(eu_ready, q + 1)
                        wait_used(act, su_ready, q, 1)
                        nc.scalar.activation(lu[:], eu[:], ACT.Ln, scale=0.5, bias=half).then_inc(lu_ready, 1)

                    def relu(q):
                        act.wait_ge(xnT_ready, q + 1)
                        wait_used(act, hs_ready, q, 1)
                        nc.scalar.activation(hT[:], xT_ps[:], ACT.Relu).then_inc(hT_ready, 1)

                    def sum_out(q, par):
                        act.wait_ge(sum_ready, q + 1)
                        if not (isinstance(q, int) and q < 2):
                            for k in range(CHAINS):
                                act.wait_ge(added[k], 32 * (q - 1))
                        nc.scalar.activation(comb1[:, par, :, :].rearrange("p t c -> p (t c)"), sum_ps[:], ACT.Copy).then_inc(comb_ready, 1)

                    half = cols[:, 4:5]
                    nc.scalar.preload_act_table_set("natural_log_exp_and_others")
                    make_basis(0)
                    rstd_start(0)
                    softplus(0)
                    relu(0)

                    def step(q, par):
                        if exists(q + 1):
                            rstd_start(q + 1)
                            if par == 1:
                                make_basis((q + 1) // 2 if isinstance(q, int) else pair_of[0])
                            relu(q + 1)
                        sum_out(q, par)
                        if exists(q + 1):
                            softplus(q + 1)
                    pair_of = [None]
                    step(0, 0)
                    step(1, 1)
                    with act.Fori(1, QUADS // 2 - 1) as i:
                        pair_of[0] = i + 1
                        step(2 * i, 0)
                        step(2 * i + 1, 1)
                    step(QUADS - 2, 0)
                    step(QUADS - 1, 1)

                @block.tensor
                def _(pe):
                    def filter_up(q, par):
                        pe.wait_ge(basis_ready, half_count(q, par, 2) // 2 if isinstance(q, int) else pair_of[0])
                        wait_used(pe, posu_ready, q, 1)
                        wait_used(pe, absu_ready, q, 1)
                        at = BASIS_AT[par]
                        nc.tensor.matmul(u_ps[:], wf1[at:at + BASIS, :], basis[at:at + BASIS, 0, :],
                                         start=True, stop=True).then_inc(u_ready, 1)

                    def filter_down(q):
                        pe.wait_ge(su_ready, q + 1)
                        wait_used(pe, efb_ready, q, 1)
                        for t in range(QT):
                            last = nc.tensor.matmul(ef_ps[:, t * P:(t + 1) * P], su[:, t * P:(t + 1) * P], wf2[:], start=True, stop=True)
                        last.then_inc(ef_ready, 1)

                    def turn(q):
                        pe.wait_ge(xn_ready, q + 1)
                        wait_used(pe, hT_ready, q, 1)
                        for t in range(QT):
                            last = nc.tensor.transpose(xT_ps[:, t * P:(t + 1) * P], xn[:, t, :], ident[:])
                        last.then_inc(xnT_ready, 1)

                    def project(q):
                        pe.wait_ge(hT_ready, q + 1)
                        wait_used(pe, msg_ready, q, 1)
                        for t in range(QT):
                            last = nc.tensor.matmul(hs_ps[:, t * P:(t + 1) * P], hT[:, t * P:(t + 1) * P], wlin[:], start=True, stop=True)
                        last.then_inc(hs_ready, 1)

                    def tile_sums(q, par):
                        pe.wait_ge(msg_ready, q + 1)
                        pe.wait_ge(same_ready, q + 1)
                        wait_used(pe, comb_ready, q, 1)
                        for t in range(QT):
                            last = nc.tensor.matmul(sum_ps[:, t * P:(t + 1) * P], same[:, par, t, :], msg[:, t * P:(t + 1) * P], start=True, stop=True)
                        last.then_inc(sum_ready, 1)

                    pair_of = [None]
                    filter_up(0, 0)
                    turn(0)
                    project(0)
                    filter_down(0)

                    def step(q, par):
                        tile_sums(q, par)
                        if exists(q + 1):
                            turn(q + 1)
                            filter_up(q + 1, 1 - par)
                            project(q + 1)
                            filter_down(q + 1)
                    step(0, 0)
                    step(1, 1)
                    with pe.Fori(1, QUADS // 2 - 1) as i:
                        pair_of[0] = i + 1
                        step(2 * i, 0)
                        pair_of[0] = i + 2
                        step(2 * i + 1, 1)
                    step(QUADS - 2, 0)
                    step(QUADS - 1, 1)

            with ExitStack() as sems:
                def s2(name):
                    return sems.enter_context(nc.semaphore("n1_" + name))
                loaded = [s2(f"loaded{p}") for p in range(2)]
                stored = [s2(f"stored{p}") for p in range(2)]
                agg_ready, xb_ready, aggT_ready, aT_ready = s2("agg_ready"), s2("xb_ready"), s2("aggT_ready"), s2("aT_ready")
                stats_ready, aggr_ready, var_ready = s2("stats_ready"), s2("aggr_ready"), s2("var_ready")
                ln_ready, r0_ready = s2("ln_ready"), s2("r0_ready")
                r1_ready, r2_ready, r3_ready, rstd_ready = s2("r1_ready"), s2("r2_ready"), s2("r3_ready"), s2("rstd_ready")
                xn_ready, xnT_ready, hT_ready, self_ready = s2("xn_ready"), s2("xnT_ready"), s2("hT_ready"), s2("self_ready")
                u_ready, absu_ready, posu_ready = s2("u_ready"), s2("absu_ready"), s2("posu_ready")
                eu_ready, lu_ready, su_ready, mlp_ready = s2("eu_ready"), s2("lu_ready"), s2("su_ready"), s2("mlp_ready")
                x1_ready, x1b_ready, h1_ready, y_ready = s2("x1_ready"), s2("x1b_ready"), s2("h1_ready"), s2("y_ready")
                aggT_ps, u_ps, mlp_ps, xT_ps, self_ps = bank[0], bank[1], bank[2], bank[3], bank[4]
                block = sems.enter_context(nc.Block())

                @block.sync
                def _(sp):
                    def load(q, par):
                        wait_used(sp, agg_ready, q, 2)
                        hold(sp, sp_passed)
                        wait_used(sp, xb_ready, q, 2)
                        hold(sp, sp_passed)
                        for k in range(CHAINS):
                            sp.dma_start(agg_in(k, par), quad_rows(agg1[k], q, C)).then_inc(loaded[par], 16)
                        sp.dma_start(flat(nx, par), quad_rows(ins["x"], q, C)).then_inc(loaded[par], 16)
                    over_quads(sp, load)

                @block.gpsimd
                def _(pool):
                    def enter(q, par):
                        pool.wait_ge(loaded[par], half_count(q, par, 48))
                        wait_used(pool, aggT_ready, q, 1)
                        nc.gpsimd.tensor_tensor(msg[:], agg_in(0, par), agg_in(1, par), ALU.add).then_inc(agg_ready, 1)
                        wait_used(pool, x1_ready, q, 2)
                        nc.gpsimd.tensor_tensor(xg[:, par, :, :], nx[:, par, :, :], bm2[:].unsqueeze(1).broadcast_to([P, QT, C]),
                                                ALU.add).then_inc(xb_ready, 1)
                    enter(0, 0)

                    def step(q, par):
                        if exists(q + 1):
                            enter(q + 1, 1 - par)
                        pool.wait_ge(x1_ready, q + 1)
                        wait_used(pool, y_ready, q, 1)
                        nc.gpsimd.tensor_tensor(efb[:].rearrange("p (t c) -> p t c", t=QT), x1[:, par, :, :],
                                                bself[:].unsqueeze(1).broadcast_to([P, QT, C]), ALU.add).then_inc(x1b_ready, 1)
                        pool.wait_ge(xn_ready, q + 1)
                        if not (isinstance(q, int) and q < 2):
                            pool.wait_ge(stored[par], half_count(q, par, 32) - 32)
                        hold(pool, pool_passed)
                        nc.gpsimd.tensor_scalar(h1s[:, par, :, :].rearrange("p t c -> p (t c)"), xn[:].rearrange("p t c -> p (t c)"), 0.0, None, ALU.max).then_inc(h1_ready, 1)
                    over_quads(pool, step)

                @block.vector
                def _(dve):
                    def mlp_in(q):
                        dve.wait_ge(u_ready, q + 1)
                        wait_used(dve, su_ready, q, 1)
                        nc.vector.tensor_scalar(posu[:], u_ps[:], bm1, 0.0, ALU.add, ALU.max).then_inc(posu_ready, 1)

                    def mlp_out(q):
                        dve.wait_ge(posu_ready, q + 1)
                        dve.wait_ge(lu_ready, q + 1)
                        wait_used(dve, mlp_ready, q, 1)
                        nc.vector.tensor_tensor(su[:], posu[:], lu[:], ALU.add).then_inc(su_ready, 1)

                    def residual(q, par):
                        dve.wait_ge(mlp_ready, q + 1)
                        dve.wait_ge(xb_ready, q + 1)
                        wait_used(dve, xn_ready, q, 2)
                        wait_used(dve, x1b_ready, q, 2)
                        nc.vector.tensor_tensor(flat(x1, par), mlp_ps[:], flat(xg, par), ALU.add).then_inc(x1_ready, 1)
                        dve.wait_ge(x1_ready, q + 1)
                        for t in range(QT):
                            last = nc.vector.bn_stats(out=stats[:, t, :], in_=x1[:, par, t, :])
                        last.then_inc(stats_ready, 1)
                        dve.wait_ge(stats_ready, q + 1)
                        hold(dve, dve_passed)
                        for t in range(QT):
                            last = nc.vector.bn_aggr(out=mv[:, t, :], in_=stats[:, t, :])
                        last.then_inc(aggr_ready, 1)
                        dve.wait_ge(aggr_ready, q + 1)
                        wait_used(dve, ln_ready, q, 1)
                        nc.vector.tensor_scalar(ve[:], mv[:, :, 1], LN_EPS, None, ALU.add).then_inc(var_ready, 1)

                    def normalise(q, par):
                        dve.wait_ge(r0_ready, q + 1)
                        nc.vector.tensor_tensor(r1[:], r0[:], r0[:], ALU.mult).then_inc(r1_ready, 1)
                        dve.wait_ge(r1_ready, q + 1)
                        nc.vector.tensor_tensor(r2[:], r1[:], ve[:], ALU.mult).then_inc(r2_ready, 1)
                        dve.wait_ge(r2_ready, q + 1)
                        nc.vector.tensor_scalar(r3[:], r2[:], -0.5, 1.5, ALU.mult, ALU.add).then_inc(r3_ready, 1)
                        dve.wait_ge(r3_ready, q + 1)
                        nc.vector.tensor_tensor(rstd[:], r3[:], r0[:], ALU.mult).then_inc(rstd_ready, 1)
                        dve.wait_ge(rstd_ready, q + 1)
                        wait_used(dve, xnT_ready, q, 1)
                        wait_used(dve, h1_ready, q, 1)
                        for t in range(QT):
                            last = nc.vector.tensor_scalar(xn[:, t, :], x1[:, par, t, :], mv[:, t, 0:1], rstd[:, t:t + 1],
                                                           ALU.subtract, ALU.mult)
                        last.then_inc(xn_ready, 1)

                    def leave(q, par):
                        dve.wait_ge(self_ready, q + 1)
                        dve.wait_ge(x1b_ready, q + 1)
                        if not (isinstance(q, int) and q < 2):
                            dve.wait_ge(stored[par], half_count(q, par, 32) - 32)
                        nc.vector.tensor_tensor(flat(ys, par), self_ps[:], efb[:], ALU.add).then_inc(y_ready, 1)

                    mlp_in(0)
                    mlp_out(0)

                    def step(q, par):
                        residual(q, par)
                        if exists(q + 1):
                            mlp_in(q + 1)
                        normalise(q, par)
                        if exists(q + 1):
                            mlp_out(q + 1)
                        leave(q, par)
                    over_quads(dve, step)

                @block.scalar
                def _(act):
                    half = cols[:, 4:5]

                    def agg_turned(q):
                        act.wait_ge(aggT_ready, q + 1)
                        wait_used(act, u_ready, q, 1)
                        nc.scalar.activation(aT[:], aggT_ps[:], ACT.Copy).then_inc(aT_ready, 1)

                    def softplus(q):
                        act.wait_ge(posu_ready, q + 1)
                        wait_used(act, eu_ready, q, 1)
                        nc.scalar.activation(absu[:], u_ps[:], ACT.Abs, bias=bm1).then_inc(absu_ready, 1)
                        act.wait_ge(absu_ready, q + 1)
                        nc.scalar.activation(eu[:], absu[:], ACT.Exp, scale=-1.0).then_inc(eu_ready, 1)
                        act.wait_ge(eu_ready, q + 1)
                        wait_used(act, su_ready, q, 1)
                        nc.scalar.activation(lu[:], eu[:], ACT.Ln, scale=0.5, bias=half).then_inc(lu_ready, 1)

                    nc.scalar.preload_act_table_set("natural_log_exp_and_others")
                    agg_turned(0)
                    softplus(0)

                    def step(q, par):
                        if exists(q + 1):
                            agg_turned(q + 1)
                        act.wait_ge(var_ready, q + 1)
                        nc.scalar.activation(lnv[:], ve[:], ACT.Ln).then_inc(ln_ready, 1)
                        act.wait_ge(ln_ready, q + 1)
                        wait_used(act, rstd_ready, q, 1)
                        nc.scalar.activation(r0[:], lnv[:], ACT.Exp, scale=-0.5).then_inc(r0_ready, 1)
                        if exists(q + 1):
                            softplus(q + 1)
                        act.wait_ge(xnT_ready, q + 1)
                        wait_used(act, self_ready, q, 1)
                        nc.scalar.activation(hT[:], xT_ps[:], ACT.Relu).then_inc(hT_ready, 1)
                        act.wait_ge(h1_ready, q + 1)
                        act.dma_start(quad_rows(h1_dram, q, C), flat(h1s, par)).then_inc(stored[par], 16)
                        act.wait_ge(y_ready, q + 1)
                        act.dma_start(quad_rows(y_dram, q, C), flat(ys, par)).then_inc(stored[par], 16)
                    over_quads(act, step)
                    for par in range(2):
                        act.wait_ge(stored[par], 32 * (QUADS // 2))

                @block.tensor
                def _(pe):
                    def agg_up(q):
                        pe.wait_ge(agg_ready, q + 1)
                        wait_used(pe, aT_ready, q, 1)
                        for t in range(QT):
                            last = nc.tensor.transpose(aggT_ps[:, t * P:(t + 1) * P], msg[:, t * P:(t + 1) * P], ident[:])
                        last.then_inc(aggT_ready, 1)
                        pe.wait_ge(aT_ready, q + 1)
                        wait_used(pe, posu_ready, q, 1)
                        wait_used(pe, absu_ready, q, 1)
                        nc.tensor.matmul(u_ps[:], wm1[:], aT[:], start=True, stop=True).then_inc(u_ready, 1)

                    def mlp_down(q):
                        pe.wait_ge(su_ready, q + 1)
                        wait_used(pe, x1_ready, q, 1)
                        for t in range(QT):
                            last = nc.tensor.matmul(mlp_ps[:, t * P:(t + 1) * P], su[:, t * P:(t + 1) * P], wm2[:], start=True, stop=True)
                        last.then_inc(mlp_ready, 1)
                    agg_up(0)
                    mlp_down(0)

                    def step(q, par):
                        if exists(q + 1):
                            agg_up(q + 1)
                        pe.wait_ge(xn_ready, q + 1)
                        wait_used(pe, hT_ready, q, 1)
                        for t in range(QT):
                            last = nc.tensor.transpose(xT_ps[:, t * P:(t + 1) * P], xn[:, t, :], ident[:])
                        last.then_inc(xnT_ready, 1)
                        if exists(q + 1):
                            mlp_down(q + 1)
                        pe.wait_ge(hT_ready, q + 1)
                        wait_used(pe, y_ready, q, 1)
                        for t in range(QT):
                            last = nc.tensor.matmul(self_ps[:, t * P:(t + 1) * P], hT[:, t * P:(t + 1) * P], wself[:], start=True, stop=True)
                        last.then_inc(self_ready, 1)
                    over_quads(pe, step)

            with ExitStack() as sems:
                def s3(name):
                    return sems.enter_context(nc.semaphore("e2_" + name))
                idx_loaded = [s3(f"idx_loaded{p}") for p in range(2)]
                keys_loaded = [s3(f"keys_loaded{p}") for p in range(2)]
                gathered = [s3(f"gathered{p}") for p in range(2)]
                added = [s3(f"added{k}") for k in range(CHAINS)]
                idxf_ready, same_ready, counted = s3("idxf_ready"), s3("same_ready"), s3("counted")
                before_ready, spare_ready, target_ready = s3("before_ready"), s3("spare_ready"), s3("target_ready")
                sumT_ready, sT_ready, neigh_ready, comb_ready = s3("sumT_ready"), s3("sT_ready"), s3("neigh_ready"), s3("comb_ready")
                sumT_ps, neigh_ps = bank[0], bank[1]
                block = sems.enter_context(nc.Block())

                @block.sync
                def _(sp):
                    def load(q, par):
                        if not (isinstance(q, int) and q < 2):
                            sp.wait_ge(gathered[par], half_count(q, par, 64) - 64)
                        hold(sp, sp_passed)
                        wait_used(sp, idxf_ready, q, 2)
                        hold(sp, sp_passed)
                        sp.dma_start(idx[:, par, :, :].rearrange("p a t -> p (a t)"), ins["edge_cols"][q, :, :]).then_inc(idx_loaded[par], 16)
                        wait_used(sp, same_ready, q, 2)
                        hold(sp, sp_passed)
                        sp.dma_start(key_rows[:, par, :], ins["src_rows"][q, :].partition_broadcast(P)).then_inc(keys_loaded[par], 16)
                    over_quads(sp, load)

                @block.gpsimd
                def _(pool):
                    def gather(q, par, t):
                        if t == 0:
                            pool.wait_ge(idx_loaded[par], half_count(q, par, 16))
                            wait_used(pool, sumT_ready, q, 2)
                        hold(pool, pool_passed)
                        nc.gpsimd.indirect_dma_start(
                            out=xg[:, par, t, :], out_offset=None, in_=h1_dram,
                            in_offset=bass.IndirectOffsetOnAxis(ap=idx[:, par, 1, t:t + 1], axis=0)).then_inc(gathered[par], 16)

                    def add(q, par, t):
                        if t == 0:
                            pool.wait_ge(comb_ready, q + 1)
                            pool.wait_ge(target_ready, q + 1)
                            pool.wait_ge(counted, q + 1)
                        k = t % CHAINS
                        n = 32 * q + 16 * (t // CHAINS)
                        if not (isinstance(n, int) and n == 0):
                            pool.wait_ge(added[k], n)
                        hold(pool, pool_passed)
                        nc.gpsimd.indirect_dma_start(
                            out=agg2[k], out_offset=bass.IndirectOffsetOnAxis(ap=target[:, par, t:t + 1], axis=0),
                            in_=comb[:, par, t, :], in_offset=None, compute_op=ALU.add).then_inc(added[k], 16)

                    for t in range(QT):
                        gather(0, 0, t)
                    for t in range(QT):
                        gather(1, 1, t)

                    def step(q, par):
                        for t in range(QT):
                            add(q, par, t)
                            if exists(q + 2):
                                gather(q + 2, par, t)
                    over_quads(pool, step)
                    for k in range(CHAINS):
                        pool.wait_ge(added[k], 32 * QUADS)

                @block.vector
                def _(dve):
                    def step(q, par):
                        dve.wait_ge(idx_loaded[par], half_count(q, par, 16))
                        nc.vector.tensor_copy(idxf[:, par, :], idx[:, par, 0, :]).then_inc(idxf_ready, 1)
                        dve.wait_ge(idxf_ready, q + 1)
                        dve.wait_ge(keys_loaded[par], half_count(q, par, 16))
                        wait_used(dve, sumT_ready, q, 2)
                        for t in range(QT):
                            last = nc.vector.tensor_scalar(same[:, par, t, :], key_rows[:, par, t * P:(t + 1) * P],
                                                           idxf[:, par, t:t + 1], None, ALU.is_equal)
                        last.then_inc(same_ready, 1)
                        dve.wait_ge(same_ready, q + 1)
                        for t in range(QT):
                            last = nc.vector.tensor_tensor_reduce(out=junk[:, t, :], in0=same[:, par, t, :], in1=lower[:], scale=1.0,
                                                                  scalar=0.0, op0=ALU.mult, op1=ALU.add, accum_out=before[:, par, t:t + 1])
                        last.then_inc(before_ready, 1)
                        dve.wait_ge(before_ready, q + 1)
                        nc.vector.tensor_scalar(spare[:, par, :], before[:, par, :], 1.0, dump, ALU.min, ALU.mult).then_inc(spare_ready, 1)
                        dve.wait_ge(spare_ready, q + 1)
                        if not (isinstance(q, int) and q < 2):
                            for k in range(CHAINS):
                                dve.wait_ge(added[k], 32 * (q - 1))
                        else:
                            nc.vector.memset(comb[:, par, :, C:W2], 0.0)
                        nc.vector.tensor_tensor(target[:, par, :], spare[:, par, :], idxf[:, par, :], ALU.max).then_inc(target_ready, 1)
                        dve.wait_ge(target_ready, q + 1)
                        nc.vector.tensor_reduce(out=comb[:, par, :, C], in_=same[:, par, :, :], axis=AX.X, op=ALU.add).then_inc(counted, 1)
                    over_quads(dve, step)

                @block.tensor
                def _(pe):
                    def sums(q, par):
                        pe.wait_ge(gathered[par], half_count(q, par, 64))
                        pe.wait_ge(same_ready, q + 1)
                        wait_used(pe, sT_ready, q, 1)
                        for t in range(QT):
                            last = nc.tensor.matmul(sumT_ps[:, t * P:(t + 1) * P], xg[:, par, t, :], same[:, par, t, :], start=True, stop=True)
                        last.then_inc(sumT_ready, 1)
                        pe.wait_ge(sT_ready, q + 1)
                        wait_used(pe, comb_ready, q, 1)
                        for t in range(QT):
                            last = nc.tensor.matmul(neigh_ps[:, t * P:(t + 1) * P], hT[:, t * P:(t + 1) * P], wneigh[:], start=True, stop=True)
                        last.then_inc(neigh_ready, 1)
                    over_quads(pe, sums)

                @block.scalar
                def _(act):
                    def step(q, par):
                        act.wait_ge(sumT_ready, q + 1)
                        wait_used(act, neigh_ready, q, 1)
                        nc.scalar.activation(hT[:], sumT_ps[:], ACT.Copy).then_inc(sT_ready, 1)
                        act.wait_ge(neigh_ready, q + 1)
                        if not (isinstance(q, int) and q < 2):
                            for k in range(CHAINS):
                                act.wait_ge(added[k], 32 * (q - 1))
                        nc.scalar.activation(comb[:, par, :, 0:C], neigh_ps[:].rearrange("p (t c) -> p t c", t=QT), ACT.Copy).then_inc(comb_ready, 1)
                    over_quads(act, step)

        with ExitStack() as sems:
            block = sems.enter_context(nc.Block())
            tables_in = zeros[:].rearrange("p (b k n) -> p b k n", b=2, k=CHAINS)
            sums = agg_rows[:].rearrange("p (b n) -> p b n", b=2)
            y_in, rows_out = [whole(nx), whole(h1s)], [whole(ys), whole(x1)]

            def unit_rows(table, u):
                return table[0:ROWS, :].rearrange("(u p t) c -> u p (t c)", p=P, t=UT)[u, :, :]

            @block.sync
            def _(sp):
                def load(u, par):
                    wait_used(sp, n2_agg, u, 2)
                    hold(sp, sp_passed)
                    for k in range(CHAINS):
                        sp.dma_start(tables_in[:, par, k, :], unit_rows(agg2[k], u)).then_inc(n2_loaded[par], 16)
                    wait_used(sp, n2_yb, u, 2)
                    hold(sp, sp_passed)
                    sp.dma_start(y_in[par], unit_rows(y_dram, u)).then_inc(n2_loaded[par], 16)
                over_units(sp, load)

            @block.gpsimd
            def _(pool):
                def step(u, par):
                    pool.wait_ge(n2_loaded[par], half_count(u, par, 48))
                    wait_used(pool, n2_out, u, 2)
                    nc.gpsimd.tensor_tensor(sums[:, par, :], tables_in[:, par, 0, :], tables_in[:, par, 1, :], ALU.add).then_inc(n2_agg, 1)
                over_units(pool, step)

            @block.vector
            def _(dve):
                def step(u, par):
                    rows = sums[:, par, :].rearrange("p (t c) -> p t c", t=UT)
                    dve.wait_ge(n2_agg, u + 1)
                    nc.vector.tensor_scalar(cm[:, par, :], rows[:, :, C], 1.0, None, ALU.min).then_inc(cm_ready, 1)
                    nc.vector.tensor_scalar(capped_counts[:, par, :], rows[:, :, C], 1.0, None, ALU.max).then_inc(capped, 1)
                    dve.wait_ge(capped, u + 1)
                    nc.vector.reciprocal(rc[:, par, :], capped_counts[:, par, :]).then_inc(rc_ready, 1)
                    if not at_first(u, 2):
                        dve.wait_ge(n2_stored[par], half_count(u, par, 16) - 16)
                    dve.wait_ge(cm_ready, u + 1)
                    dve.wait_ge(rc_ready, u + 1)
                    for t in range(UT):
                        at = slice(t * C, (t + 1) * C)
                        last = nc.vector.scalar_tensor_tensor(out=rows_out[par][:, at], in0=bneigh[:], scalar=cm[:, par, t:t + 1],
                                                              in1=y_in[par][:, at], op0=ALU.mult, op1=ALU.add)
                    last.then_inc(n2_yb, 1)
                    dve.wait_ge(n2_yb, u + 1)
                    for t in range(UT):
                        at = slice(t * C, (t + 1) * C)
                        last = nc.vector.scalar_tensor_tensor(out=rows_out[par][:, at], in0=rows[:, t, 0:C], scalar=rc[:, par, t:t + 1],
                                                              in1=rows_out[par][:, at], op0=ALU.mult, op1=ALU.add)
                    last.then_inc(n2_out, 1)
                over_units(dve, step)

            @block.scalar
            def _(act):
                def step(u, par):
                    act.wait_ge(n2_out, u + 1)
                    act.dma_start(unit_rows(out_dram, u), rows_out[par]).then_inc(n2_stored[par], 16)
                over_units(act, step)
                act.wait_ge(n2_stored[0], 16 * (UNITS // 2 + 1))
                act.wait_ge(n2_stored[1], 16 * (UNITS // 2))


CENTERS = (np.arange(BASIS, dtype=np.float32) / np.float32(BASIS - 1)) * np.float32(5.0)


def kernel(x, src, dst, edge_weight, L0_gnn_W_lin, L0_gnn_Wf1, L0_gnn_bf1, L0_gnn_Wf2, L0_gnn_bf2, L0_gnn_Wm1, L0_gnn_bm1,
           L0_gnn_Wm2, L0_gnn_bm2, L1_gnn_W_self, L1_gnn_b_self, L1_gnn_W_neigh, L1_gnn_b_neigh):
    import concourse.bacc as bacc
    from concourse.bass_utils import run_bass_kernel_spmd

    pad = ROWS - N_ROWS
    extra = np.arange(N_ROWS, ROWS, dtype=np.int32)
    src_pad = np.concatenate([np.asarray(src), extra])
    dst_pad = np.concatenate([np.asarray(dst), extra])
    ew_pad = np.concatenate([np.asarray(edge_weight), np.zeros(pad, np.float32)])
    x_pad = np.concatenate([np.asarray(x), np.zeros((pad, C), np.float32)])

    def by_column(a):
        return a.reshape(QUADS, QT, P).transpose(0, 2, 1)

    cols = np.zeros((P, 16), np.float32)
    for at in BASIS_AT:
        cols[at:at + BASIS, 0] = -CENTERS
    cols[:, 1] = ROWS + np.arange(P)
    cols[:, 2] = np.asarray(L0_gnn_bf1)
    cols[:, 3] = np.asarray(L0_gnn_bm1)
    cols[:, 4] = 0.5
    cols[:, 9] = TOP
    cols[:, 10] = LN_EPS
    cols[:, 11] = -1.0
    wf1 = np.zeros((P, C), np.float32)
    for at in BASIS_AT:
        wf1[at:at + BASIS] = np.asarray(L0_gnn_Wf1)
    consts = np.zeros((P, 4 * P), np.float32)
    p32, c32, b = np.arange(P)[:, None] % 32, np.arange(32)[None], 32 * np.arange(HI)[:, None] + np.arange(LO)[None]
    consts[:, 0:P] = np.arange(P)
    consts[:, P:2 * P] = 1.0
    consts[:, 2 * P:2 * P + 32] = p32 == c32
    consts[:, 2 * P + 32:2 * P + 64] = p32 < c32
    consts[:, 2 * P + 64:2 * P + 96] = np.arange(P)[:, None] < c32
    consts[0:HI, 2 * P + 96:3 * P] = np.where(b // QT + AHEAD >= QUADS - 1, ROWS, QROWS * (b // QT + AHEAD + 1) - SPAN)
    consts[:, 3 * P:3 * P + 3] = np.arange(P)[:, None] == np.arange(3)
    consts[:, 3 * P + 3:3 * P + 7] = np.arange(P)[:, None] // 32 == np.arange(4)
    arrays = {
        "consts": consts,
        "qbase": np.broadcast_to((QROWS * np.arange(QUADS)).astype(np.float32), (P, QUADS)),
        "iota4": np.broadcast_to(np.arange(QROWS, dtype=np.float32), (P, QROWS)),
        "dst_flat": np.concatenate([dst_pad, np.array([ROWS], np.int32)]),
        "tile_first": dst_pad[::P], "tile_last": dst_pad[P - 1::P],
        "src_cols": src_pad.reshape(TILES, P).T, "dst_cols": dst_pad.reshape(TILES, P).T,
        "x": x_pad,
        "edge_cols": np.concatenate([by_column(src_pad), by_column(dst_pad)], axis=2),
        "src_rows": src_pad.reshape(QUADS, QROWS),
        "dst_rows": dst_pad.reshape(QUADS, QROWS),
        "ew_rows": ew_pad.reshape(QUADS, QROWS),
        "ident": np.eye(P, dtype=np.float32),
        "lower": np.tri(P, k=-1, dtype=np.float32),
        "cols": cols,
        "wlin": np.asarray(L0_gnn_W_lin).T, "wf1": wf1, "wf2": np.asarray(L0_gnn_Wf2),
        "wm1": np.asarray(L0_gnn_Wm1), "wm2": np.asarray(L0_gnn_Wm2),
        "wself": np.asarray(L1_gnn_W_self).T, "wneigh": np.asarray(L1_gnn_W_neigh).T,
        "bf2": np.asarray(L0_gnn_bf2), "bm2": np.asarray(L0_gnn_bm2),
        "bself": np.asarray(L1_gnn_b_self), "bneigh": np.asarray(L1_gnn_b_neigh),
    }
    nc = bacc.Bacc("TRN2", target_bir_lowering=False, num_devices=1)
    given, ins = {}, {}
    for name, a in arrays.items():
        a = np.ascontiguousarray(a)
        given[f"in_{name}"] = a
        ins[name] = nc.dram_tensor(f"in_{name}", a.shape, mybir.dt.from_np(a.dtype), kind="ExternalInput").ap()
    out = nc.dram_tensor("out", (ROWS, C), mybir.dt.float32, kind="ExternalOutput").ap()
    gnn_kernel(nc, ins, out)
    r = run_bass_kernel_spmd(nc, [given], core_ids=[0])
    return r.results[0]["out"][:N_ROWS]
```
